# Optimizing a Trainium2 kernel written in Bass

```python
import numpy as np
import jax
import jax.numpy as jnp

def _softmax(x, axis=-1):
    return jax.nn.softmax(x, axis=axis)

def _gelu(x):
    return jax.nn.gelu(x, approximate=True)

def _silu(x):
    return jax.nn.silu(x)

def _sigmoid(x):
    return jax.nn.sigmoid(x)

def _layernorm(x, axis=-1, eps=1e-05):
    m = jnp.mean(x, axis=axis, keepdims=True)
    v = jnp.var(x, axis=axis, keepdims=True)
    return (x - m) / jnp.sqrt(v + eps)

def _scatter_add(tgt, idx, src, axis=0):
    return tgt.at[idx].add(src)

def _segment_sum(src, seg, n):
    return jax.ops.segment_sum(src, seg, n)
kernel_name = 'mk_xattn_ffn_d2_seqx_r4_86fa63'

def setup_inputs(seed: int=0):
    np.random.seed(seed)
    _w = jnp.asarray

    def _rec_inputs():
        import jax
        import jax.numpy as jnp
        _rk = jax.random.key(seed)
        x = 7.22e-05 + 1 * jax.random.normal(jax.random.fold_in(_rk, 1), (2, 1024, 256), jnp.float32)
        _lenS = 1024 - jax.random.randint(jax.random.fold_in(_rk, 7), (2,), 0, max(1, 1024 // 4) + 1, jnp.int32)
        _lenS2 = 77 - jax.random.randint(jax.random.fold_in(_rk, 8), (2,), 0, max(1, 77 // 4) + 1, jnp.int32)
        _ctx_1024P = jax.random.normal(jax.random.fold_in(_rk, 11), (2, 16, 256), jnp.float32)
        _ctx_1024c = jax.random.dirichlet(jax.random.fold_in(_rk, 511), 0.3 * jnp.ones((16,), jnp.float32), (2, 77))
        _ctx_1024t = jnp.einsum('bsk,bkd->bsd', _ctx_1024c, _ctx_1024P)
        _ctx_1024t = _ctx_1024t * jax.lax.rsqrt(jnp.mean(jnp.square(_ctx_1024t)) + 1e-12) * 0.953939
        ctx_1024 = 4.13588e-05 + 0.999923 * (_ctx_1024t + 0.3 * jax.random.normal(jax.random.fold_in(_rk, 611), (2, 77, 256), jnp.float32))
        _validS = jnp.arange(1024)[None, :] < _lenS[:, None]
        _validS2 = jnp.arange(77)[None, :] < _lenS2[:, None]
        _causal = jnp.tril(jnp.ones((1024, 1024), dtype=bool))
        mask_Bx1x1xS2_ik0 = jnp.where(jnp.broadcast_to(_validS2[:, None, None, :], (2, 1, 1, 77)), 0, 1).astype(jnp.int32)
        return (x, ctx_1024, mask_Bx1x1xS2_ik0)
    x, ctx_1024, mask_Bx1x1xS2_ik0 = _rec_inputs()

    def _L0_xattn_setup():
        import jax, jax.numpy as jnp
        import numpy as np
        FEATURE_DIM = 256
        HEAD_NUM = 16
        HIDDEN_DIM = FEATURE_DIM // HEAD_NUM
        key = jax.random.key(seed)
        ks = jax.random.split(key, 12)
        B, S, D = (4, 512, FEATURE_DIM)
        s = 1.0 / np.sqrt(D)
        inp = {'query': jax.random.normal(ks[0], (B, S, D), jnp.float32), 'key': jax.random.normal(ks[1], (B, S, D), jnp.float32), 'value': jax.random.normal(ks[2], (B, S, D), jnp.float32), 'mask': jax.random.randint(ks[3], (B, 1, 1, S), 0, 2, jnp.int32), 'Wq': jax.random.normal(ks[4], (D, D), jnp.float32) * s, 'bq': jnp.zeros((D,), jnp.float32), 'Wk': jax.random.normal(ks[5], (D, D), jnp.float32) * s, 'bk': jnp.zeros((D,), jnp.float32), 'Wv': jax.random.normal(ks[6], (D, D), jnp.float32) * s, 'bv': jnp.zeros((D,), jnp.float32), 'Wo': jax.random.normal(ks[7], (D, D), jnp.float32) * s, 'bo': jnp.zeros((D,), jnp.float32)}
        return inp
    _L0_xattn_all = _L0_xattn_setup()
    _L0_xattn_in = {k: v for k, v in _L0_xattn_all.items() if k in ('Wq', 'bq', 'Wk', 'bk', 'Wv', 'bv', 'Wo', 'bo')}
    del _L0_xattn_all

    def _L0_ffn_setup():
        import jax, jax.numpy as jnp
        import numpy as np
        N_HEAD = 16
        N_ACTIVE = 4
        D_MODEL = 256
        D_ATTN = 64
        B = 4
        S = 512
        key = jax.random.key(seed)
        ks = jax.random.split(key, 6)
        sc = 1.0 / np.sqrt(D_MODEL).astype(np.float32)
        return {'x': jax.random.normal(ks[0], (B, S, D_MODEL), jnp.float32), 'Wq': jax.random.normal(ks[1], (D_MODEL, N_HEAD * D_ATTN), jnp.float32) * sc, 'bq': jnp.zeros((N_HEAD * D_ATTN,), jnp.float32), 'Wk': jax.random.normal(ks[2], (D_MODEL, N_HEAD * D_ATTN), jnp.float32) * sc, 'bk': jnp.zeros((N_HEAD * D_ATTN,), jnp.float32), 'Wv': jax.random.normal(ks[3], (D_MODEL, N_HEAD * D_ATTN), jnp.float32) * sc, 'bv': jnp.zeros((N_HEAD * D_ATTN,), jnp.float32), 'Wr': jax.random.normal(ks[4], (D_MODEL, N_HEAD), jnp.float32) * sc, 'br': jnp.zeros((N_HEAD,), jnp.float32), 'Wo': jax.random.normal(ks[5], (N_ACTIVE * D_ATTN, D_MODEL), jnp.float32) * (1.0 / np.sqrt(N_ACTIVE * D_ATTN).astype(np.float32)), 'bo': jnp.zeros((D_MODEL,), jnp.float32)}
    _L0_ffn_all = _L0_ffn_setup()
    _L0_ffn_in = {k: v for k, v in _L0_ffn_all.items() if k in ('Wq', 'bq', 'Wk', 'bk', 'Wv', 'bv', 'Wr', 'br', 'Wo', 'bo')}
    del _L0_ffn_all

    def _L1_xattn_setup():
        import jax, jax.numpy as jnp
        import numpy as np
        E, T, H, F = (8, 256, 256, 1024)
        key = jax.random.key(seed)
        k1, k2, k3 = jax.random.split(key, 3)
        x = jax.random.normal(k1, (E, T, H), dtype=jnp.float32)
        w1 = jax.random.normal(k2, (E, F, H), dtype=jnp.float32) * (1.0 / np.sqrt(H))
        w2 = jax.random.normal(k3, (E, F, H), dtype=jnp.float32) * (1.0 / np.sqrt(F))
        return {'x': x, 'w1': w1, 'w2': w2}
    _L1_xattn_all = _L1_xattn_setup()
    _L1_xattn_in = {k: v for k, v in _L1_xattn_all.items() if k in ()}
    del _L1_xattn_all

    def _L1_ffn_setup():
        import jax, jax.numpy as jnp
        import numpy as np
        B, S, H, F, E = (2, 512, 256, 1024, 8)
        key = jax.random.key(seed)
        ks = jax.random.split(key, 4)
        x = jax.random.normal(ks[0], (B, S, H), dtype=jnp.float32)
        w_router = jax.random.normal(ks[1], (H, E), dtype=jnp.float32) * 0.02
        w1 = jax.random.normal(ks[2], (E, H, F), dtype=jnp.float32) * 0.02
        b1 = jnp.zeros((E, F), dtype=jnp.float32)
        w2 = jax.random.normal(ks[3], (E, F, H), dtype=jnp.float32) * 0.02
        b2 = jnp.zeros((E, H), dtype=jnp.float32)
        return {'x': x, 'w_router': w_router, 'w1': w1, 'b1': b1, 'w2': w2, 'b2': b2}
    _L1_ffn_all = _L1_ffn_setup()
    _L1_ffn_in = {k: v for k, v in _L1_ffn_all.items() if k in ('w_router', 'w1', 'b1', 'w2', 'b2')}
    del _L1_ffn_all
    return {'x': x, 'ctx_1024': ctx_1024, 'mask_Bx1x1xS2_ik0': mask_Bx1x1xS2_ik0, 'L0_xattn_Wq': _L0_xattn_in['Wq'], 'L0_xattn_bq': _L0_xattn_in['bq'], 'L0_xattn_Wk': _L0_xattn_in['Wk'], 'L0_xattn_bk': _L0_xattn_in['bk'], 'L0_xattn_Wv': _L0_xattn_in['Wv'], 'L0_xattn_bv': _L0_xattn_in['bv'], 'L0_xattn_Wo': _L0_xattn_in['Wo'], 'L0_xattn_bo': _L0_xattn_in['bo'], 'L0_ffn_Wq': _L0_ffn_in['Wq'], 'L0_ffn_bq': _L0_ffn_in['bq'], 'L0_ffn_Wk': _L0_ffn_in['Wk'], 'L0_ffn_bk': _L0_ffn_in['bk'], 'L0_ffn_Wv': _L0_ffn_in['Wv'], 'L0_ffn_bv': _L0_ffn_in['bv'], 'L0_ffn_Wr': _L0_ffn_in['Wr'], 'L0_ffn_br': _L0_ffn_in['br'], 'L0_ffn_Wo': _L0_ffn_in['Wo'], 'L0_ffn_bo': _L0_ffn_in['bo'], 'L1_ffn_w_router': _L1_ffn_in['w_router'], 'L1_ffn_w1': _L1_ffn_in['w1'], 'L1_ffn_b1': _L1_ffn_in['b1'], 'L1_ffn_w2': _L1_ffn_in['w2'], 'L1_ffn_b2': _L1_ffn_in['b2']}

def reference(x, ctx_1024, mask_Bx1x1xS2_ik0, L0_xattn_Wq, L0_xattn_bq, L0_xattn_Wk, L0_xattn_bk, L0_xattn_Wv, L0_xattn_bv, L0_xattn_Wo, L0_xattn_bo, L0_ffn_Wq, L0_ffn_bq, L0_ffn_Wk, L0_ffn_bk, L0_ffn_Wv, L0_ffn_bv, L0_ffn_Wr, L0_ffn_br, L0_ffn_Wo, L0_ffn_bo, L1_ffn_w_router, L1_ffn_w1, L1_ffn_b1, L1_ffn_w2, L1_ffn_b2):
    import jax
    import jax.numpy as jnp

    def _L0_xattn_ref(query, key, value, mask, Wq, bq, Wk, bk, Wv, bv, Wo, bo):
        import jax, jax.numpy as jnp
        import numpy as np
        FEATURE_DIM = 256
        HEAD_NUM = 16
        HIDDEN_DIM = FEATURE_DIM // HEAD_NUM
        B, Sq, D = query.shape
        H, Hd = (HEAD_NUM, HIDDEN_DIM)
        scale = jnp.sqrt(jnp.asarray(Hd, query.dtype))

        def split_heads(x):
            b, s, _ = x.shape
            return x.reshape(b, s, H, Hd).transpose(0, 2, 1, 3)
        Q = split_heads(query @ Wq.T + bq)
        K = split_heads(key @ Wk.T + bk)
        V = split_heads(value @ Wv.T + bv)
        scores = jnp.einsum('bhqd,bhkd->bhqk', Q, K) / scale
        scores = jnp.where(mask == 0, jnp.asarray(-10000000000.0, scores.dtype), scores)
        attn = jax.nn.softmax(scores, axis=-1)
        h = jnp.einsum('bhqk,bhkd->bhqd', attn, V)
        h = h.transpose(0, 2, 1, 3).reshape(B, Sq, D)
        return h @ Wo.T + bo

    def _L0_ffn_ref(x, Wq, bq, Wk, bk, Wv, bv, Wr, br, Wo, bo):
        import jax, jax.numpy as jnp
        import numpy as np
        N_HEAD = 16
        N_ACTIVE = 4
        D_MODEL = 256
        D_ATTN = 64
        B = 4
        S = 512
        b, s, _ = x.shape
        dist = jax.nn.softmax(jnp.mean(x @ Wr + br, axis=1), axis=-1)
        _, idx = jax.lax.top_k(dist, N_ACTIVE)
        idx = jnp.sort(idx, axis=-1)

        def proj(W, bias):
            return (x @ W + bias).reshape(b, s, N_HEAD, D_ATTN).transpose(0, 2, 1, 3)
        Q = proj(Wq, bq)
        K = proj(Wk, bk)
        V = proj(Wv, bv)
        gather = lambda t: jnp.take_along_axis(t, idx[:, :, None, None], axis=1)
        Qs, Ks, Vs = (gather(Q), gather(K), gather(V))
        scale = 1.0 / jnp.sqrt(jnp.asarray(D_ATTN, x.dtype))
        score = jax.nn.softmax(jnp.einsum('bhqd,bhkd->bhqk', Qs, Ks) * scale, axis=-1)
        O = jnp.einsum('bhqk,bhkd->bhqd', score, Vs)
        O = O.transpose(0, 2, 1, 3).reshape(b, s, N_ACTIVE * D_ATTN)
        return O @ Wo + bo

    def _L1_xattn_ref(x, w1, w2):
        import jax, jax.numpy as jnp
        import numpy as np
        E, T, H, F = (8, 256, 256, 1024)
        h = jnp.einsum('eth,efh->etf', x, w1)
        g = jax.nn.gelu(h, approximate=True)
        out = jnp.einsum('etf,efh->eth', g, w2)
        return out

    def _L1_ffn_ref(x, w_router, w1, b1, w2, b2):
        import jax, jax.numpy as jnp
        import numpy as np
        B, S, H, F, E = (2, 512, 256, 1024, 8)
        'Top-1 MoE layer: route -> per-expert FFN -> weighted combine.\n\n            Faithful to ExpertParallelWrapper._process_moe_layer on a single group:\n            router picks one expert per token with a routing weight; tokens are\n            dispatched to experts (here expressed as a static mask over the fixed\n            expert set), processed by the expert FFN, and scatter-combined back\n            weighted by the routing probability.\n            '
        Bs, Ss, Hs = x.shape
        n_experts = w1.shape[0]
        logits = jnp.einsum('bsh,he->bse', x, w_router)
        probs = jax.nn.softmax(logits, axis=-1)
        sel = jnp.argmax(probs, axis=-1)
        wgt = jnp.take_along_axis(probs, sel[..., None], axis=-1)[..., 0]
        xt = x.reshape(-1, Hs)
        sel_t = sel.reshape(-1)
        wgt_t = wgt.reshape(-1)
        out = jnp.zeros_like(xt)
        for e in range(n_experts):
            h = jax.nn.relu(xt @ w1[e] + b1[e])
            y = h @ w2[e] + b2[e]
            m = (sel_t == e).astype(xt.dtype) * wgt_t
            out = out + m[:, None] * y
        return out.reshape(Bs, Ss, Hs)
    x = x + _L0_xattn_ref(_layernorm(x, axis=-1), ctx_1024, ctx_1024, mask_Bx1x1xS2_ik0, L0_xattn_Wq, L0_xattn_bq, L0_xattn_Wk, L0_xattn_bk, L0_xattn_Wv, L0_xattn_bv, L0_xattn_Wo, L0_xattn_bo)
    x = x + _L0_ffn_ref(_layernorm(x, axis=-1), L0_ffn_Wq, L0_ffn_bq, L0_ffn_Wk, L0_ffn_bk, L0_ffn_Wv, L0_ffn_bv, L0_ffn_Wr, L0_ffn_br, L0_ffn_Wo, L0_ffn_bo)
    x = x + _L1_xattn_ref(_layernorm(x, axis=-1), ctx_1024, ctx_1024)
    x = x + _L1_ffn_ref(_layernorm(x, axis=-1), L1_ffn_w_router, L1_ffn_w1, L1_ffn_b1, L1_ffn_w2, L1_ffn_b2)
    return x

_drawn_inputs = setup_inputs


def setup_inputs(seed=0):
    import zlib

    import numpy as np

    out = dict(_drawn_inputs(seed))
    spreads = {'L0_xattn_bq': (0.0, 0.29),
     'L0_xattn_bk': (0.0, 2.0),
     'L0_xattn_bv': (0.0, 0.1),
     'L0_xattn_bo': (0.0, 0.1),
     'L0_ffn_bq': (0.0, 0.8),
     'L0_ffn_bk': (0.0, 2.0),
     'L0_ffn_bv': (0.0, 0.293),
     'L0_ffn_br': (0.0, 0.1),
     'L0_ffn_bo': (0.0, 0.1),
     'L1_ffn_b1': (0.0, 2.0),
     'L1_ffn_b2': (0.0, 2.0)}
    factors = {'L1_ffn_w_router': 23.652, 'L1_ffn_w1': 26.631, 'L1_ffn_w2': 21.982}
    for name, (base, spread) in spreads.items():
        noise = np.random.default_rng([zlib.crc32(name.encode()), seed]).standard_normal(out[name].shape)
        drawn = base * np.exp(spread * noise) if base else spread * noise
        out[name] = jnp.asarray(drawn.astype(out[name].dtype))
    for name, factor in factors.items():
        out[name] = (out[name] * factor).astype(out[name].dtype)
    return out
```

```python
from contextlib import ExitStack

import concourse.bass as bass
from concourse import mybir

ALU = mybir.AluOpType
ACT = mybir.ActivationFunctionType
AX = mybir.AxisListType
F32 = mybir.dt.float32
F32R = mybir.dt.float32r
BF16 = mybir.dt.bfloat16
I32 = mybir.dt.int32
U32 = mybir.dt.uint32

P = 128
B, S, D = 2, 1024, 256
KD = D // P
T = B * S // P
CH = 4
NC = T // CH
CW = CH * P
EPS = 1e-5
L = 77
H1, HD1 = 16, 16
HH = H1 // 2
GH = 4
HL = HH * L
VC = 5
VR = -(-HL // VC)
H2, HD2, NA = 16, 64, 4
NE, FF = 8, 1024
FB = FF // P
ROW = D + 4
MT = B * S // P + NE - 1
TG = MT + 2
TABLE = 2 * TG + NE + 1
TILES, LAST = 2 * TG + NE - 1, 2 * TG + NE
WE = KD * FF + FB * D


class Link:

    def __init__(self, eng, sem):
        self.eng, self.sem, self.n, self.reg = eng, sem, 0, 0

    def __call__(self, ins):
        ins.then_inc(self.sem, 1)
        self.n += 1
        self.eng.wait_ge(self.sem, self.n + self.reg)


def layernorm_stats(vec, link, x_tiles, stats, mv):
    for j, x in enumerate(x_tiles):
        ins = vec.bn_stats(stats[:, j, :], x)
    link(ins)
    for j in range(len(x_tiles)):
        ins = vec.bn_aggr(mv[:, j, :], stats[:, j, :])
    return ins


def cross_attention(nc, top, t, io):
    with ExitStack() as ctx:
        def sb(name, shape, dt=F32):
            return ctx.enter_context(nc.sbuf_tensor(name, shape, dt))

        def sem(name):
            return top.enter_context(nc.semaphore(name))

        x_all, ident = t["x_all"], t["ident"]
        wq, wk, wv, wo = (sb(f"a_{n}", [P, KD, D]) for n in ("wq", "wk", "wv", "wo"))
        bq, bk, bk4 = sb("a_bq", [P, KD]), sb("a_bk", [P, KD]), sb("a_bk4", [P, KD])
        bv, bo = sb("a_bv", [P, D]), sb("a_bo", [P, D])
        ctxT = sb("a_ctxT", [P, B, KD, L])
        mask_i, keep = sb("a_mask", [P, B, L], I32), sb("a_keep", [P, B, L])
        drop = sb("a_drop", [3, B, GH, L], BF16)
        fill = sb("a_fill", [3, P], BF16)
        kT = sb("a_kT", [P, KD, B, L])
        kblk = sb("a_kblk", [P, KD, B, HH, L])
        sel = sb("a_sel", [L, VC * VR])
        v_sb = sb("a_v", [L, B, D])
        vblk = sb("a_vblk", [VR, B * KD, VC, P])
        stats, mv = sb("a_stats", [P, CH, 6]), sb("a_mv", [P, T, 2])
        rstd, mhalf = sb("a_rstd", [P, T]), sb("a_mhalf", [P, CH])
        xn = sb("a_xn", [P, CH, D])
        xnT, qT, hT = sb("a_xnT", [P, KD, CW]), sb("a_qT", [P, KD, CW]), sb("a_hT", [P, KD, CW])
        pr = sb("a_p", [P, 4, VC * VR])
        mx, sm, rs = sb("a_mx", [P, 4, HH]), sb("a_sm", [P, 4, HH]), sb("a_rs", [P, 4, HH])
        pT = sb("a_pT", [VR, KD, VC, CW])
        psA = ctx.enter_context(nc.psum_tensor("a_psA", [P, KD, CW], F32))
        psS = [ctx.enter_context(nc.psum_tensor(f"a_psS{m}", [P, 2, 512], F32)) for m in range(2)]
        psT = ctx.enter_context(nc.psum_tensor("a_psT", [P, 2, 512], F32))

        x_in, w_in, c_in = sem("a_x_in"), sem("a_w_in"), sem("a_c_in")
        dve, pool_sem = sem("a_dve"), sem("a_pool")
        var_ready, rstd_ready, xn_ready, bo_added = sem("a_var"), sem("a_rstd_s"), sem("a_xn_s"), sem("a_bo_s")
        pool_consts, keep_ready, k_ps, k_sb = sem("a_consts"), sem("a_keep_s"), sem("a_k_ps"), sem("a_k_sb")
        kcopy, k_ready = sem("a_kcopy"), sem("a_k_ready")
        v_ps, v_ready, vrep_ps, vrep_sb, vblk_ready = (sem(f"a_{n}") for n in ("v_ps", "v_rdy", "vrep_ps", "vrep_sb", "vblk_s"))
        xT_ps, xT_sb, q_ps, q_sb = sem("a_xT_ps"), sem("a_xT_sb"), sem("a_q_ps"), sem("a_q_sb")
        s_ps, sub_done, exp_done, rs_ready, pn_ready = (sem(f"a_{n}") for n in ("s_ps", "sub", "exp", "rs_s", "pn"))
        pT_ps, pT_sb, h_ps, h_sb, o_ps, x_done = (sem(f"a_{n}") for n in ("pT_ps", "pT_sb", "h_ps", "h_sb", "o_ps", "x_done"))
        U = CH * KD

        block = ctx.enter_context(nc.Block())

        @block.sync
        def _(sp):
            sp.dma_start(x_all[:, 0:CH, 0:D], io["x"][:, 0:CH, :]).then_inc(x_in, 16)
            sp.dma_start(ctxT[:], io["ctxT"]).then_inc(c_in, 16)
            sp.dma_start(wk[:], io["xa_wk"]).then_inc(c_in, 16)
            sp.dma_start(mask_i[:], io["mask"]).then_inc(c_in, 16)
            sp.dma_start(bk[:], io["xa_bk"]).then_inc(c_in, 16)
            sp.dma_start(wq[:], io["xa_wq"]).then_inc(w_in, 16)
            sp.dma_start(wo[:], io["xa_wo"]).then_inc(w_in, 16)

        @block.scalar
        def _(act):
            act.dma_start(x_all[:, CH:T, 0:D], io["x"][:, CH:T, :]).then_inc(x_in, 16)
            act.dma_start(wv[:], io["xa_wv"]).then_inc(c_in, 16)
            act.dma_start(bv[:], io["xa_bv"]).then_inc(c_in, 16)
            act.dma_start(bq[:], io["xa_bq"]).then_inc(w_in, 16)
            act.dma_start(bo[:], io["xa_bo"]).then_inc(w_in, 16)
            act.wait_ge(keep_ready, 1)
            act.wait_ge(k_ps, 1)
            for m in range(KD):
                act.activation(kT[:, m], psA[:, m, 0:B * L].rearrange("p (b l) -> p b l", b=B),
                               ACT.Identity, bias=bk4[:, m:m + 1], scale=HD1 ** -0.5).then_inc(k_sb, 1)
            for i in range(B * KD):
                act.wait_ge(vrep_ps, i + 1)
                act.copy(vblk[:, i], psS[i % 2][0:VR].rearrange("p a b -> p (a b)")[:, 0:VC * P]
                         .rearrange("p (c n) -> p c n", c=VC)).then_inc(vrep_sb, 1)
            act.wait_ge(w_in, 64)
            for b in range(B):
                with act.Fori(0, NC // B) as cc:
                    n = cc + b * (NC // B)
                    act.wait_ge(xT_ps, n + 1)
                    act.copy(xnT[:], psA[:]).then_inc(xT_sb, 1)
                    act.wait_ge(q_ps, n + 1)
                    for m in range(KD):
                        act.activation(qT[:, m], psA[:, m], ACT.Identity, bias=bq[:, m:m + 1],
                                       scale=1.0).then_inc(q_sb, 1)
                    for u in range(U + 3):
                        if u < U:
                            act.wait_ge(sub_done, n * U + (u + 1))
                            act.activation(pr[:, u % 4, 0:HL], pr[:, u % 4, 0:HL], ACT.Exp).then_inc(exp_done, 1)
                        if u >= 3:
                            j, m = divmod(u - 3, KD)
                            act.wait_ge(pT_ps, n * U + (u - 2))
                            act.copy(pT[:, m, :, j * P:(j + 1) * P],
                                     psT[0:VR].rearrange("p a b -> p (a b)")[:, 0:VC * P]
                                     .rearrange("p (c n) -> p c n", c=VC)).then_inc(pT_sb, 1)
                    act.wait_ge(h_ps, n + 1)
                    act.copy(hT[:], psA[:]).then_inc(h_sb, 1)

        @block.gpsimd
        def _(pool):
            link = Link(pool, pool_sem)
            link(pool.memset(ident[:], 0.0))
            link(pool.affine_select(out=ident[:], in_=ident[:], compare_op=ALU.not_equal, fill=1.0, base=0,
                                    pattern=[[-1, P]], channel_multiplier=1))
            pool.memset(mhalf[:], -0.5)
            link(pool.memset(sel[:], 0.0))
            s3 = sel[:, 0:HL].rearrange("p (h l) -> p h l", h=HH)
            pool.affine_select(out=s3, in_=s3, compare_op=ALU.not_equal, fill=1.0, base=0,
                               pattern=[[0, HH], [-1, L]], channel_multiplier=1)
            link(pool.memset(fill[:], -1024.0 * 9764864))
            link(pool.affine_select(out=fill[:], in_=fill[:], compare_op=ALU.is_gt, fill=-1024.0 * 760, base=1,
                                    pattern=[[0, P]], channel_multiplier=-1))
            link(pool.affine_select(out=fill[:], in_=fill[:], compare_op=ALU.is_gt, fill=-1024.0, base=2,
                                    pattern=[[0, P]], channel_multiplier=-1))
            pool.memset(pr[:, :, HL:], 0.0).then_inc(pool_consts, 1)
            pool.wait_ge(pool_consts, 1)
            for n in range(NC):
                pool.wait_ge(var_ready, n + 1)
                pool.tensor_tensor(rstd[:, n * CH:(n + 1) * CH], rstd[:, n * CH:(n + 1) * CH], mhalf[:],
                                   ALU.pow).then_inc(rstd_ready, 1)
            pool.wait_ge(kcopy, B * KD)
            k4 = kblk[:].rearrange("p m b h l -> p (m b) h l")
            link(pool.affine_select(out=k4, in_=k4, compare_op=ALU.is_ge, fill=0.0, base=0,
                                    pattern=[[0, KD * B], [-HD1, HH], [0, L]], channel_multiplier=1))
            pool.affine_select(out=k4, in_=k4, compare_op=ALU.is_ge, fill=0.0, base=HD1 - 1,
                               pattern=[[0, KD * B], [HD1, HH], [0, L]], channel_multiplier=-1).then_inc(k_ready, 1)
            pool.wait_ge(vrep_sb, B * KD)
            for i in range(B * KD):
                v4 = vblk[:, i].rearrange("p c (h d) -> p c h d", h=HH)
                link(pool.affine_select(out=v4, in_=v4, compare_op=ALU.is_ge, fill=0.0, base=0,
                                        pattern=[[VR, VC], [-L, HH], [0, HD1]], channel_multiplier=1))
                pool.affine_select(out=v4, in_=v4, compare_op=ALU.is_ge, fill=0.0, base=L - 1,
                                   pattern=[[-VR, VC], [L, HH], [0, HD1]], channel_multiplier=-1).then_inc(vblk_ready, 1)
            pool.wait_ge(w_in, 64)
            with pool.Fori(0, NC) as n:
                pool.wait_ge(xn_ready, n + 1)
                xc = x_all[:, bass.ds(n * CH, CH), 0:D]
                pool.tensor_tensor(xc, xc, bo[:].unsqueeze(1).to_broadcast([P, CH, D]), ALU.add).then_inc(bo_added, 1)
                for u in range(U):
                    pool.wait_ge(rs_ready, n * U + (u + 1))
                    p3 = pr[:, u % 4, 0:HL].rearrange("p (h l) -> p h l", h=HH)
                    pool.tensor_tensor(p3, p3, rs[:, u % 4, :].unsqueeze(2).to_broadcast([P, HH, L]),
                                       ALU.mult).then_inc(pn_ready, 1)

        @block.vector
        def _(vec):
            link = Link(vec, dve)
            for n in range(NC):
                vec.wait_ge(x_in, 32)
                link(layernorm_stats(vec, link, [x_all[:, n * CH + j, 0:D] for j in range(CH)], stats,
                                     mv[:, n * CH:(n + 1) * CH]))
                vec.tensor_scalar(rstd[:, n * CH:(n + 1) * CH], mv[:, n * CH:(n + 1) * CH, 1], EPS, None,
                                  ALU.add).then_inc(var_ready, 1)
            vec.wait_ge(c_in, 96)
            link(vec.tensor_scalar(keep[:], mask_i[:], 0, None, ALU.not_equal))
            vec.tensor_scalar(drop[:], keep[0:3].unsqueeze(2).to_broadcast([3, B, GH, L]), -1.0, 1.0,
                              ALU.mult, ALU.add)
            vec.tensor_scalar(bk4[:], bk[:], HD1 ** -0.5, None, ALU.mult).then_inc(keep_ready, 1)
            vec.wait_ge(v_ps, 1)
            vec.tensor_tensor(v_sb[:], psT[0:L, 0, :].rearrange("p (b d) -> p b d", b=B),
                              bv[0:L].unsqueeze(1).to_broadcast([L, B, D]), ALU.add).then_inc(v_ready, 1)
            vec.wait_ge(k_sb, KD)
            for m in range(KD):
                for b in range(B):
                    vec.tensor_tensor(kblk[:, m, b], kT[:, m, b].unsqueeze(1).to_broadcast([P, HH, L]),
                                      keep[:, b].unsqueeze(1).to_broadcast([P, HH, L]), ALU.mult).then_inc(kcopy, 1)
            vec.wait_ge(pool_consts, 1)
            before = link.n
            with vec.Fori(0, NC) as n:
                link.reg = n * (2 * U)
                vec.wait_ge(rstd_ready, n + 1)
                vec.wait_ge(xT_ps, n)
                for j in range(CH):
                    ins = vec.tensor_scalar(xn[:, j], x_all[:, n * CH + j, 0:D], mv[:, n * CH + j, 0:1],
                                            rstd[:, bass.ds(n * CH + j, 1)], ALU.subtract, ALU.mult)
                ins.then_inc(xn_ready, 1)
                for u in range(U + 1):
                    if u < U:
                        m = u % KD
                        s4 = psS[m][:, :, 0:GH * L].rearrange("p a (g l) -> p a g l", g=GH)
                        vec.wait_ge(s_ps, n * U + (u + 1))
                        link(vec.tensor_reduce(mx[:, u % 4].rearrange("p (a g) -> p a g", a=2), s4, AX.X, ALU.max))
                        vec.wait_ge(pT_ps, n * U + max(u - 3, 0))
                        vec.tensor_tensor(pr[:, u % 4, 0:HL].rearrange("p (a g l) -> p a g l", a=2, g=GH), s4,
                                          mx[:, u % 4].rearrange("p (a g) -> p a g", a=2).unsqueeze(3)
                                          .to_broadcast([P, 2, GH, L]), ALU.subtract).then_inc(sub_done, 1)
                    if u >= 1:
                        w = (u - 1) % 4
                        vec.wait_ge(exp_done, n * U + u)
                        link(vec.tensor_reduce(sm[:, w], pr[:, w, 0:HL].rearrange("p (h l) -> p h l", h=HH),
                                               AX.X, ALU.add))
                        vec.reciprocal(rs[:, w], sm[:, w]).then_inc(rs_ready, 1)
                assert link.n == before + 2 * U
                vec.wait_ge(o_ps, n + 1)
                vec.wait_ge(bo_added, n + 1)
                xc = x_all[:, bass.ds(n * CH, CH), 0:D]
                vec.tensor_tensor(xc, psT[:].rearrange("p a (b d) -> p (a b) d", d=D), xc, ALU.add).then_inc(x_done, 1)
            vec.wait_ge(x_done, NC)

        @block.tensor
        def _(pe):
            pe.wait_ge(c_in, 96)
            for m in range(KD):
                for b in range(B):
                    for k in range(KD):
                        ins = pe.matmul(psA[:, m, b * L:(b + 1) * L], wk[:, k, m * P:(m + 1) * P], ctxT[:, b, k, :],
                                        start=(k == 0), stop=(k == KD - 1))
            ins.then_inc(k_ps, 1)
            for b in range(B):
                for k in range(KD):
                    ins = pe.matmul(psT[0:L, 0, b * D:(b + 1) * D], ctxT[:, b, k, :], wv[:, k, :],
                                    start=(k == 0), stop=(k == KD - 1))
            ins.then_inc(v_ps, 1)
            pe.wait_ge(v_ready, 1)
            pe.wait_ge(pool_consts, 1)
            for i in range(B * KD):
                b, m = divmod(i, KD)
                if i >= 2:
                    pe.wait_ge(vrep_sb, i - 1)
                for c in range(VC):
                    ins = pe.matmul(psS[i % 2][0:VR].rearrange("p a b -> p (a b)")[:, c * P:(c + 1) * P],
                                    sel[:, c * VR:(c + 1) * VR], v_sb[:, b, m * P:(m + 1) * P], start=True, stop=True)
                ins.then_inc(vrep_ps, 1)
            pe.wait_ge(k_sb, KD)
            pe.wait_ge(vrep_sb, B * KD)
            pe.wait_ge(w_in, 64)
            pe.wait_ge(k_ready, 1)
            pe.wait_ge(vblk_ready, B * KD)

            for b in range(B):
                with pe.Fori(0, NC // B) as cc:
                    n = cc + b * (NC // B)
                    pe.wait_ge(xn_ready, n + 1)
                    pe.wait_ge(h_sb, n)
                    for k in range(KD):
                        for j in range(CH):
                            ins = pe.transpose(psA[:, k, j * P:(j + 1) * P], xn[:, j, k * P:(k + 1) * P], ident[:])
                    ins.then_inc(xT_ps, 1)
                    pe.wait_ge(xT_sb, n + 1)
                    for m in range(KD):
                        for k in range(KD):
                            ins = pe.matmul(psA[:, m], wq[:, k, m * P:(m + 1) * P], xnT[:, k],
                                            start=(k == 0), stop=(k == KD - 1))
                    ins.then_inc(q_ps, 1)
                    pe.wait_ge(q_sb, n * KD + KD)
                    for u in range(U + 3):
                        if u < U:
                            j, m = divmod(u, KD)
                            pe.wait_ge(sub_done, n * U + max(u - 1, 0))
                            for g in range(2):
                                pe.matmul(psS[m][:, g, 0:GH * L], fill[:], drop[:, b], start=True, stop=False)
                                ins = pe.matmul(psS[m][:, g, 0:GH * L], qT[:, m, j * P:(j + 1) * P],
                                                kblk[:, m, b, g * GH:(g + 1) * GH, :], start=False, stop=True)
                            ins.then_inc(s_ps, 1)
                        if u >= 3:
                            w = u - 3
                            pe.wait_ge(pn_ready, n * U + (w + 1))
                            pe.wait_ge(pT_sb, n * U + w)
                            if w == 0:
                                pe.wait_ge(x_done, n)
                            for c in range(VC):
                                ins = pe.transpose(psT[0:VR].rearrange("p a b -> p (a b)")[:, c * P:(c + 1) * P],
                                                   pr[:, w % 4, c * VR:(c + 1) * VR], ident[:])
                            ins.then_inc(pT_ps, 1)
                    pe.wait_ge(pT_sb, n * U + U)
                    for m in range(KD):
                        for c in range(VC):
                            ins = pe.matmul(psA[:, m], vblk[:, b * KD + m, c, :], pT[:, m, c, :],
                                            start=(c == 0), stop=(c == VC - 1))
                    ins.then_inc(h_ps, 1)
                    pe.wait_ge(h_sb, n + 1)
                    for j in range(CH):
                        for m in range(KD):
                            ins = pe.matmul(psT[:].rearrange("p a (b d) -> p (a b) d", d=D)[:, j],
                                            hT[:, m, j * P:(j + 1) * P], wo[:, m, :],
                                            start=(m == 0), stop=(m == KD - 1))
                    ins.then_inc(o_ps, 1)


def gate_and_project(nc, top, t, io):
    with ExitStack() as ctx:
        def sb(name, shape, dt=F32):
            return ctx.enter_context(nc.sbuf_tensor(name, shape, dt))

        def sem(name):
            return top.enter_context(nc.semaphore(name))

        x_all, ident, xnT, v_all, head_col = t["x_all"], t["ident"], t["xnT"], t["v_all"], t["head_col"]
        stats, mv = sb("g_stats", [P, CH, 6]), sb("g_mv", [P, T, 2])
        rstd, mhalf = sb("g_rstd", [P, T]), sb("g_mhalf", [P, CH])
        xn = sb("g_xn", [P, 2, CH, D])
        part = sb("g_part", [P, KD, NC])
        mean = sb("g_mean", [P, KD, B])
        wr, br = sb("g_wr", [P, KD, H2]), sb("g_br", [1, H2])
        wv = sb("g_wv", [P, B, KD, NA * HD2])
        dist, e, cand, rank, act_h, slot_of, weighted = (sb(f"g_{n}", [1, B, H2]) for n in
                                                         ("dist", "e", "cand", "rank", "acth", "slot", "wtd"))
        top1, tot = sb("g_top1", [1, B]), sb("g_tot", [1, B])
        above, same = sb("g_above", [1, B, H2, H2]), sb("g_same", [1, B, H2, H2])
        lower = sb("g_lower", [1, H2, H2])
        numi, num = sb("g_numi", [1, H2], I32), sb("g_num", [1, H2])
        pick = sb("g_pick", [1, B, NA, H2])
        col = sb("g_col", [1, B * NA + 1])
        psX = [ctx.enter_context(nc.psum_tensor(f"g_psX{m}", [P, KD, CW], F32)) for m in range(2)]
        psV = [ctx.enter_context(nc.psum_tensor(f"g_psV{m}", [P, 512], F32)) for m in range(2)]
        psG = ctx.enter_context(nc.psum_tensor("g_psG", [1, 512], F32))
        w_in, dve, pool_sem = sem("g_w_in"), sem("g_dve"), sem("g_pool")
        consts, var_ready, rstd_ready, xn_ready = (sem(f"g_{n}") for n in ("consts", "var", "rstd_s", "xn_s"))
        xT_ps, xT_sb, mean_ready, logit_ps = (sem(f"g_{n}") for n in ("xT_ps", "xT_sb", "mean_s", "logit"))
        shifted, exp_done, col_ready, wv_in, v_ps, v_sb = (sem(f"g_{n}") for n in
                                                          ("shift", "exp", "col_s", "wv_in", "v_ps", "v_sb"))
        vpad = sem("g_vpad")
        block = ctx.enter_context(nc.Block())

        @block.sync
        def _(sp):
            sp.dma_start(wr[:], io["f_wr"]).then_inc(w_in, 16)
            sp.dma_start(br[:], io["f_br"]).then_inc(w_in, 16)
            sp.wait_ge(col_ready, 1)
            for b in range(B):
                for s in range(NA):
                    r = sp.value_load(head_col[0:1, b * NA + s:b * NA + s + 1], min_val=0, max_val=(H2 - 1) * HD2)
                    sp.dma_start(wv[:, b, :, s * HD2:(s + 1) * HD2],
                                 io["f_wv"][:, :, bass.ds(r, HD2)]).then_inc(wv_in, 16)

        @block.gpsimd
        def _(pool):
            link = Link(pool, pool_sem)
            pool.memset(mhalf[:], -0.5)
            pool.memset(v_all[:, B * NA], 0.0).then_inc(vpad, 1)
            pool.iota(numi[:], pattern=[[1, H2]], base=0, channel_multiplier=0)
            link(pool.memset(lower[:], 1.0))
            pool.affine_select(out=lower[:], in_=lower[:], compare_op=ALU.is_gt, fill=0.0, base=0,
                               pattern=[[1, H2], [-1, H2]], channel_multiplier=0).then_inc(consts, 1)
            pool.wait_ge(consts, 1)
            for n in range(NC):
                pool.wait_ge(var_ready, n + 1)
                pool.tensor_tensor(rstd[:, n * CH:(n + 1) * CH], rstd[:, n * CH:(n + 1) * CH], mhalf[:],
                                   ALU.pow).then_inc(rstd_ready, 1)

        @block.scalar
        def _(act):
            with act.Fori(0, NC // 2) as h:
                for par in range(2):
                    n = h * 2 + par
                    act.wait_ge(xT_ps, n + 1)
                    for k in range(KD):
                        act.activation(xnT[:, k, bass.ds(n * CW, CW)], psX[par][:, k], ACT.Identity,
                                       accum_out=part[:, k, bass.ds(n, 1)]).then_inc(xT_sb, 1)
            act.wait_ge(shifted, 1)
            act.activation(e[:], e[:], ACT.Exp).then_inc(exp_done, 1)
            for i in range(T):
                b, kt = divmod(i, T // B)
                act.wait_ge(v_ps, i + 1)
                act.copy(v_all[:, b * NA:(b + 1) * NA, kt, :],
                         psV[i % 2][:, 0:NA * HD2].rearrange("p (h d) -> p h d", h=NA)).then_inc(v_sb, 1)

        @block.vector
        def _(vec):
            link = Link(vec, dve)
            for n in range(NC):
                link(layernorm_stats(vec, link, [x_all[:, n * CH + j, 0:D] for j in range(CH)], stats,
                                     mv[:, n * CH:(n + 1) * CH]))
                vec.tensor_scalar(rstd[:, n * CH:(n + 1) * CH], mv[:, n * CH:(n + 1) * CH, 1], EPS, None,
                                  ALU.add).then_inc(var_ready, 1)
            with vec.Fori(0, NC // 2) as h:
                for par in range(2):
                    n = h * 2 + par
                    vec.wait_ge(rstd_ready, n + 1)
                    vec.wait_ge(xT_ps, h * 2)
                    for j in range(CH):
                        ins = vec.tensor_scalar(xn[:, par, j], x_all[:, n * CH + j, 0:D], mv[:, n * CH + j, 0:1],
                                                rstd[:, bass.ds(n * CH + j, 1)], ALU.subtract, ALU.mult)
                    ins.then_inc(xn_ready, 1)
            vec.wait_ge(xT_sb, NC * KD)
            link(vec.tensor_reduce(mean[:], part[:].rearrange("p k (b c) -> p k b c", b=B), AX.X, ALU.add))
            vec.tensor_scalar(mean[:], mean[:], 1.0 / S, None, ALU.mult).then_inc(mean_ready, 1)
            vec.wait_ge(w_in, 32)
            vec.wait_ge(logit_ps, 1)
            link(vec.tensor_tensor(dist[:], psG[0:1, 0:B * H2].rearrange("p (b h) -> p b h", b=B),
                                   br[:].unsqueeze(1).to_broadcast([1, B, H2]), ALU.add))
            link(vec.tensor_reduce(top1[:], dist[:], AX.X, ALU.max))
            vec.tensor_tensor(e[:], dist[:], top1[:].unsqueeze(2).to_broadcast([1, B, H2]),
                              ALU.subtract).then_inc(shifted, 1)
            vec.wait_ge(exp_done, 1)
            link(vec.tensor_reduce(tot[:], e[:], AX.X, ALU.add))
            link(vec.reciprocal(tot[:], tot[:]))
            link(vec.tensor_tensor(dist[:], e[:], tot[:].unsqueeze(2).to_broadcast([1, B, H2]), ALU.mult))
            full = [1, B, H2, H2]
            other, own = dist[:].unsqueeze(2).to_broadcast(full), dist[:].unsqueeze(3).to_broadcast(full)
            vec.tensor_tensor(above[:], other, own, ALU.is_gt)
            link(vec.tensor_tensor(same[:], other, own, ALU.is_equal))
            vec.wait_ge(consts, 1)
            low = lower[:].unsqueeze(1).to_broadcast(full)
            link(vec.tensor_tensor(same[:], same[:], low, ALU.mult))
            link(vec.tensor_tensor(above[:], above[:], same[:], ALU.add))
            link(vec.tensor_reduce(rank[:], above[:], AX.X, ALU.add))
            link(vec.tensor_scalar(act_h[:], rank[:], NA - 0.5, None, ALU.is_lt))
            link(vec.tensor_tensor(same[:], act_h[:].unsqueeze(2).to_broadcast(full), low, ALU.mult))
            link(vec.tensor_reduce(slot_of[:], same[:], AX.X, ALU.add))
            link(vec.tensor_copy(num[:], numi[:]))
            link(vec.tensor_tensor(weighted[:], act_h[:], num[:].unsqueeze(1).to_broadcast([1, B, H2]), ALU.mult))
            part_s = [1, B, NA, H2]
            link(vec.tensor_tensor(pick[:], slot_of[:].unsqueeze(2).to_broadcast(part_s),
                                   num[:, 0:NA].unsqueeze(1).unsqueeze(3).to_broadcast(part_s), ALU.is_equal))
            link(vec.tensor_tensor(pick[:], pick[:], weighted[:].unsqueeze(2).to_broadcast(part_s), ALU.mult))
            link(vec.memset(col[:], 0.0))
            link(vec.tensor_reduce(col[:, 0:B * NA].rearrange("p (b s) -> p b s", b=B), pick[:], AX.X, ALU.add))
            vec.tensor_scalar(head_col[:], col[:], float(HD2), None, ALU.mult).then_inc(col_ready, 1)

        @block.tensor
        def _(pe):
            with pe.Fori(0, NC // 2) as h:
                for par in range(2):
                    n = h * 2 + par
                    pe.wait_ge(xn_ready, n + 1)
                    pe.wait_ge(xT_sb, h * 2 * KD)
                    for k in range(KD):
                        for j in range(CH):
                            ins = pe.transpose(psX[par][:, k, j * P:(j + 1) * P], xn[:, par, j, k * P:(k + 1) * P],
                                               ident[:])
                    ins.then_inc(xT_ps, 1)
            pe.wait_ge(mean_ready, 1)
            pe.wait_ge(w_in, 32)
            for b in range(B):
                for k in range(KD):
                    ins = pe.matmul(psG[0:1, b * H2:(b + 1) * H2], mean[:, k, b:b + 1], wr[:, k, :],
                                    start=(k == 0), stop=(k == KD - 1))
            ins.then_inc(logit_ps, 1)
            pe.wait_ge(wv_in, 16 * B * NA)
            for i in range(T):
                b = i // (T // B)
                if i >= 2:
                    pe.wait_ge(v_sb, i - 1)
                for k in range(KD):
                    ins = pe.matmul(psV[i % 2][:, 0:NA * HD2], xnT[:, k, i * P:(i + 1) * P], wv[:, b, k, :],
                                    start=(k == 0), stop=(k == KD - 1))
                ins.then_inc(v_ps, 1)


def gated_attention(nc, top, t, io):
    with ExitStack() as ctx:
        def sb(name, shape, dt=F32):
            return ctx.enter_context(nc.sbuf_tensor(name, shape, dt))

        def sem(name):
            return top.enter_context(nc.semaphore(name))

        x_all, ident, xnT, v_all, head_col = t["x_all"], t["ident"], t["xnT"], t["v_all"], t["head_col"]
        NI = B * NA
        NQ = S // P
        KT = S // P
        HK = KT // 2
        QP = 2
        SW = 2 * NQ
        GW = SW // QP
        LAG = 2
        wqk = [sb(f"h_wqk{i}", [P, KD, P]) for i in range(2)]
        bqk, bv = sb("h_bqk", [P, NI + 1]), sb("h_bv", [P, NI + 1])
        qs = [sb(f"h_qs{i}", [P, S], F32R) for i in range(2)]
        kh = [sb(f"h_kh{i}", [P, S], F32R) for i in range(2)]
        kl = [sb(f"h_kl{i}", [P, S], F32R) for i in range(2)]
        vs = [sb(f"h_vs{i}", [P, KT, 2, HD2], F32R) for i in range(2)]
        pr = sb("h_p", [P, 4, S])
        nmx, sm, rs = sb("h_nmx", [P, SW]), sb("h_sm", [P, SW]), sb("h_rs", [P, SW])
        pTh = [sb(f"h_pTh{i}", [P, KT, QP * P], F32R) for i in range(2)]
        pTl = [sb(f"h_pTl{i}", [P, KT, QP * P], F32R) for i in range(2)]
        oT = sb("h_oT", [P, NI * S])
        wo = sb("h_wo", [P, NA, D])
        bo = sb("h_bo", [P, D])
        psS = [ctx.enter_context(nc.psum_tensor(f"h_psS{m}", [P, S], F32)) for m in range(2)]
        psT = [ctx.enter_context(nc.psum_tensor(f"h_psT{m}", [P, HK, P], F32)) for m in range(2)]
        psP = ctx.enter_context(nc.psum_tensor("h_psP", [P, 512], F32))
        psO = ctx.enter_context(nc.psum_tensor("h_psO", [P, 512], F32))

        names = ("w_in", "b_in", "zeroed", "bscaled", "scaled", "qk_ps", "qk_hi", "qk_lo", "qk_ready", "vh_ready",
                 "v_ready", "s_ps", "max_ready", "exp_done", "rs_ready", "pn_ready", "pT_ps", "pT_hi", "pT_lo",
                 "o_ps", "o_sb", "y_ps", "y_sb", "bo_added")
        (w_in, b_in, zeroed, bscaled, scaled, qk_ps, qk_hi, qk_lo, qk_ready, vh_ready, v_ready, s_ps, max_ready,
         exp_done, rs_ready, pn_ready, pT_ps, pT_hi, pT_lo, o_ps, o_sb, y_ps, y_sb, bo_added) = (
             sem("h_" + n) for n in names)
        w_par = [sem(f"h_w_par{i}") for i in range(2)]

        def upto(eng, s, n, per, c, held=None):
            count = n * per + c
            if not isinstance(n, int):
                count = eng.to_reg(count)
            if held is not None:
                eng.wait_ge(held, 1)
            if not isinstance(n, int) or count > 0:
                eng.wait_ge(s, count)

        def iterations(eng, body):
            body(0)
            with eng.Fori(1, NI // 2) as n:
                body(n)

        block = ctx.enter_context(nc.Block())


        @block.sync
        def _(sp):
            sp.dma_start(wo[0:HD2], io["f_wo"]).then_inc(w_in, 16)
            sp.dma_start(wo[HD2:P], io["f_wo"]).then_inc(w_in, 16)
            sp.dma_start(bo[:], io["f_bo"]).then_inc(w_in, 16)

            def fetch(i, par):
                r = sp.value_load(head_col[0:1, bass.ds(i, 1)], min_val=0, max_val=(H2 - 1) * HD2)
                sp.dma_start(wqk[par][:, :, 0:HD2], io["f_wq"][:, :, bass.ds(r, HD2)]).then_inc(w_par[par], 16)
                sp.dma_start(wqk[par][:, :, HD2:P], io["f_wk"][:, :, bass.ds(r, HD2)]).then_inc(w_par[par], 16)

            fetch(0, 0)
            fetch(1, 1)
            sp.wait_ge(zeroed, 1)
            for i in range(NI + 1):
                r = sp.value_load(head_col[0:1, i:i + 1], min_val=0, max_val=(H2 - 1) * HD2)
                sp.dma_start(bqk[0:HD2, i:i + 1], io["f_bq"][bass.ds(r, HD2)]).then_inc(b_in, 16)
                sp.dma_start(bqk[HD2:P, i:i + 1], io["f_bk"][bass.ds(r, HD2)]).then_inc(b_in, 16)
                sp.dma_start(bv[0:HD2, i:i + 1], io["f_bv"][bass.ds(r, HD2)]).then_inc(b_in, 16)
            with sp.Fori(0, NI // 2 - 1) as n:
                for par in range(2):
                    sp.wait_ge(qk_ps, n * 4 + (2 * par + 2))
                    fetch(n * 2 + (par + 2), par)
            sp.wait_ge(qk_ps, 2 * (NI - 1))
            fetch(NI, 0)

        @block.gpsimd
        def _(pool):
            pool.memset(bv[:], 0.0).then_inc(zeroed, 1)
            pool.wait_ge(w_in, 48)
            for n in range(NC):
                xc = x_all[:, n * CH:(n + 1) * CH, 0:D]
                pool.tensor_tensor(xc, xc, bo[:].unsqueeze(1).to_broadcast([P, CH, D]), ALU.add).then_inc(bo_added, 1)
            pool.wait_ge(b_in, 48 * (NI + 1))
            pool.tensor_scalar(bqk[0:HD2], bqk[0:HD2], HD2 ** -0.5, 0.0, ALU.mult, ALU.add).then_inc(bscaled, 1)

            def scale_q(n, c, par):
                upto(pool, w_par[par], n, 32, 32 * (c // 2 + 1), held=zeroed)
                pool.tensor_scalar(wqk[par][:, :, 0:HD2], wqk[par][:, :, 0:HD2], HD2 ** -0.5, 0.0,
                                   ALU.mult, ALU.add).then_inc(scaled, 1)

            scale_q(0, 0, 0)

            def body(n):
                for c in range(SW):
                    i, q = divmod(c, NQ)
                    upto(pool, rs_ready, n, SW, c + 1, held=zeroed)
                    pool.tensor_scalar(pr[:, c % 4], pr[:, c % 4], rs[:, c:c + 1], 0.0, ALU.mult,
                                       ALU.add).then_inc(pn_ready, 1)
                    if q == 1:
                        scale_q(n, i + 1, (i + 1) % 2)

            iterations(pool, body)

        @block.scalar
        def _(act):
            def project(n, c, par, ch):
                upto(act, qk_ps, n, 4, 2 * c + ch + 1, held=bscaled)
                upto(act, s_ps, n, SW, NQ * (c - 1))
                cols = slice(ch * CW, (ch + 1) * CW)
                bias = [bqk[h, bass.ds(n * 2 + c, 1)] for h in (slice(0, HD2), slice(HD2, P))]
                act.activation(qs[par][0:HD2, cols], psP[0:HD2], ACT.Identity, bias=bias[0], scale=1.0)
                act.activation(kh[par][HD2:P, cols], psP[HD2:P], ACT.Identity, bias=bias[1],
                               scale=1.0).then_inc(qk_hi, 1)

            def split_v(n, c, par):
                upto(act, o_ps, n, GW, (c - 1) * NQ // QP, held=bscaled)
                v = v_all[:, 2 * n + c] if isinstance(n, int) else \
                    v_all[:, bass.ds(n * 2 + c, 1)].rearrange("p a k d -> p (a k) d")
                act.copy(vs[par][:, :, 0, :], v).then_inc(vh_ready, 1)

            def high(n, c):
                for hf in range(2):
                    upto(act, pT_ps, n, 2 * SW, 2 * c + hf + 1)
                    upto(act, o_ps, n, GW, c // QP - 1)
                    act.copy(pTh[c // QP % 2][:, hf * HK:(hf + 1) * HK, c % QP * P:(c % QP + 1) * P],
                             psT[hf][:]).then_inc(pT_hi, 1)

            def output(n, g):
                upto(act, o_ps, n, GW, g + 1)
                act.activation(oT[:, bass.ds(n * (GW * QP * P) + g * QP * P, QP * P)], psO[:, 0:QP * P],
                               ACT.Identity, bias=bv[:, bass.ds(n * 2 + g * QP // NQ, 1)], scale=1.0).then_inc(o_sb, 1)

            project(0, 0, 0, 0)
            project(0, 0, 0, 1)
            split_v(0, 0, 0)

            def body(n):
                for c in range(SW):
                    i, q = divmod(c, NQ)
                    upto(act, max_ready, n, SW, c + 1)
                    upto(act, pT_ps, n, 2 * SW, 2 * (c - 3))
                    act.activation(pr[:, c % 4], psS[c % 2][:], ACT.Exp, bias=nmx[:, c:c + 1], scale=1.0,
                                   accum_out=sm[:, c:c + 1]).then_inc(exp_done, 1)
                    if not (isinstance(n, int) and c < LAG):
                        high(n, c - LAG)
                    if q in (4, 6):
                        project(n, i + 1, (i + 1) % 2, q // 2 - 2)
                    if q == 4:
                        split_v(n, i + 1, (i + 1) % 2)
                    if c % 2 == 1 and not (isinstance(n, int) and c < 5):
                        output(n, (c - 5) // 2)

            iterations(act, body)
            last = NI // 2
            high(last, -2)
            high(last, -1)
            output(last, -2)
            output(last, -1)

        @block.vector
        def _(vec):
            def project(n, c, par, ch):
                upto(vec, qk_hi, n, 4, 2 * c + ch + 1)
                cols = slice(ch * CW, (ch + 1) * CW)
                bias = [bqk[h, bass.ds(n * 2 + c, 1)] for h in (slice(0, HD2), slice(HD2, P))]
                vec.scalar_tensor_tensor(qs[par][HD2:P, cols], psP[0:HD2], bias[0], qs[par][0:HD2, cols],
                                         ALU.add, ALU.subtract)
                vec.scalar_tensor_tensor(kl[par][HD2:P, cols], psP[HD2:P], bias[1], kh[par][HD2:P, cols],
                                         ALU.add, ALU.subtract).then_inc(qk_lo, 1)

            def duplicate(n, c, par):
                upto(vec, qk_lo, n, 4, 2 * c + 2)
                vec.tensor_copy(kh[par][0:HD2], kh[par][HD2:P])
                vec.tensor_copy(kl[par][0:HD2], kl[par][HD2:P]).then_inc(qk_ready, 1)

            def split_v(n, c, par):
                upto(vec, vh_ready, n, 2, c + 1)
                v = v_all[:, 2 * n + c] if isinstance(n, int) else \
                    v_all[:, bass.ds(n * 2 + c, 1)].rearrange("p a k d -> p (a k) d")
                vec.tensor_tensor(vs[par][:, :, 1, :], v, vs[par][:, :, 0, :], ALU.subtract).then_inc(v_ready, 1)

            def low(n, c):
                for hf in range(2):
                    upto(vec, pT_hi, n, 2 * SW, 2 * c + hf + 1)
                    part = (slice(None), slice(hf * HK, (hf + 1) * HK), slice(c % QP * P, (c % QP + 1) * P))
                    vec.tensor_tensor(pTl[c // QP % 2][part], psT[hf][:], pTh[c // QP % 2][part],
                                      ALU.subtract).then_inc(pT_lo, 1)

            def invert(n, c):
                upto(vec, exp_done, n, SW, c + 1)
                vec.reciprocal(rs[:, c % SW:c % SW + 1], sm[:, c % SW:c % SW + 1]).then_inc(rs_ready, 1)

            project(0, 0, 0, 0)
            project(0, 0, 0, 1)
            duplicate(0, 0, 0)
            split_v(0, 0, 0)

            def body(n):
                for c in range(SW):
                    i, q = divmod(c, NQ)
                    upto(vec, s_ps, n, SW, c + 1)
                    vec.tensor_reduce(nmx[:, c:c + 1], psS[c % 2][:], AX.X, ALU.max, negate=True).then_inc(max_ready, 1)
                    invert(n, c)
                    if not (isinstance(n, int) and c < LAG):
                        low(n, c - LAG)
                    if q in (4, 6):
                        project(n, i + 1, (i + 1) % 2, q // 2 - 2)
                    if q == 5:
                        split_v(n, i + 1, (i + 1) % 2)
                    if q == 7:
                        duplicate(n, i + 1, (i + 1) % 2)

            iterations(vec, body)
            low(NI // 2, -2)
            low(NI // 2, -1)
            vec.wait_ge(bo_added, NC)
            for r in range(T // 2):
                vec.wait_ge(y_ps, r + 1)
                xc = x_all[:, 2 * r:2 * r + 2, 0:D]
                vec.tensor_tensor(xc, (psP, psO)[r % 2][:].rearrange("p (a d) -> p a d", a=2), xc,
                                  ALU.add).then_inc(y_sb, 1)

        @block.tensor
        def _(pe):
            def project(n, c, par, ch):
                upto(pe, scaled, n, 2, c + 1)
                upto(pe, qk_hi, n, 4, 2 * c + ch)
                upto(pe, qk_lo, n, 4, 2 * c + ch)
                batch = (2 * n + c) // NA if isinstance(n, int) else ((n * 2 + c) // NA) % B
                for k in range(KD):
                    ins = pe.matmul(psP[:], wqk[par][:, k, :], xnT[:, k, bass.ds(batch * S + ch * CW, CW)],
                                    start=(k == 0), stop=(k == KD - 1))
                ins.then_inc(qk_ps, 1)

            def transposes(n, c):
                for hf in range(2):
                    upto(pe, pn_ready, n, SW, c + 1)
                    upto(pe, pT_lo, n, 2 * SW, 2 * c + hf - 1)
                    for k in range(HK):
                        ins = pe.transpose(psT[hf][:, k], pr[:, c % 4, (hf * HK + k) * P:(hf * HK + k + 1) * P], ident[:])
                    ins.then_inc(pT_ps, 1)

            def values(n, g):
                par = g * QP // NQ % 2
                upto(pe, pT_lo, n, 2 * SW, 2 * QP * (g + 1))
                upto(pe, v_ready, n, 2, g * QP // NQ + 1)
                upto(pe, o_sb, n, GW, g)
                for k in range(KT):
                    for part in (pTh, pTl):
                        ins = pe.matmul(psO[:, 0:QP * P], vs[par][:, k], part[g % 2][:, k],
                                        start=(k == 0 and part is pTh), stop=(k == KT - 1 and part is pTl))
                ins.then_inc(o_ps, 1)

            project(0, 0, 0, 0)
            project(0, 0, 0, 1)

            def body(n):
                for c in range(SW):
                    i, q = divmod(c, NQ)
                    if q == 0:
                        upto(pe, qk_ready, n, 2, i + 1)
                    upto(pe, exp_done, n, SW, c - 1)
                    for hf in range(2):
                        for part in (kh, kl):
                            ins = pe.matmul(psS[c % 2][:, hf * CW:(hf + 1) * CW], qs[i][:, q * P:(q + 1) * P],
                                            part[i][:, hf * CW:(hf + 1) * CW], start=(part is kh), stop=(part is kl))
                    ins.then_inc(s_ps, 1)
                    if not (isinstance(n, int) and c < LAG):
                        transposes(n, c - LAG)
                    if c % 2 == 0 and not (isinstance(n, int) and c < 4):
                        values(n, c // 2 - 2)
                    if q in (3, 5):
                        project(n, i + 1, (i + 1) % 2, q // 2 - 1)

            iterations(pe, body)
            last = NI // 2
            transposes(last, -2)
            values(last, -2)
            transposes(last, -1)
            values(last, -1)
            pe.wait_ge(w_in, 48)
            pe.wait_ge(o_sb, NI * NQ // QP)
            pe.wait_ge(qk_hi, 2 * (NI + 1))
            pe.wait_ge(qk_lo, 2 * (NI + 1))
            for r in range(T // 2):
                if r >= 2:
                    pe.wait_ge(y_sb, r - 1)
                for j in range(2):
                    b, q = divmod(2 * r + j, NQ)
                    for s in range(NA):
                        ins = pe.matmul((psP, psO)[r % 2][:, j * D:(j + 1) * D],
                                        oT[:, (b * NA + s) * S + q * P:(b * NA + s) * S + (q + 1) * P], wo[:, s, :],
                                        start=(s == 0), stop=(s == NA - 1))
                ins.then_inc(y_ps, 1)


def context_mlp(nc, top, t, io):
    with ExitStack() as ctx:
        def sb(name, shape, dt=F32):
            return ctx.enter_context(nc.sbuf_tensor(name, shape, dt))

        def sem(name):
            return top.enter_context(nc.semaphore(name))

        x_all, ident, table, slot = t["x_all"], t["ident"], t["table"], t["slot"]
        ctxT, ctxs = sb("c_ctxT", [P, B, KD, L]), sb("c_ctx", [L, B, D])
        wr = sb("c_wr", [P, KD, NE])
        stats = sb("c_stats", [P, 2, CH, 6])
        mv, rstd, mhalf = sb("c_mv", [P, T, 2]), sb("c_rstd", [P, T]), sb("c_mhalf", [P, CH])
        mv4 = sb("c_mv4", [P, T, 2])
        xn, xnT = sb("c_xn", [P, 2, CH, D]), sb("c_xnT", [P, 2, KD, CW])
        sq, inner, th, g = (sb(f"c_{n}", [L, 2, CW]) for n in ("sq", "inner", "th", "g"))
        lg, e, first, oh, rank, base = (sb(f"c_{n}", [P, T, NE]) for n in ("lg", "e", "first", "oh", "rank", "base"))
        scan = sb("c_scan", [P, 2, T, NE])
        best, tot = sb("c_best", [P, T]), sb("c_tot", [P, T])
        low = sb("c_low", [P, T])
        before, ones = sb("c_before", [P, P]), sb("c_ones", [P, P])
        numi, num = sb("c_numi", [P, 32], I32), sb("c_num", [P, 32])
        steps = sb("c_steps", [P, T])
        tok = sb("c_tok", [P, T], I32)
        fits = sb("c_fits", [P, NE, T])
        tiles, ends = sb("c_tiles", [P, NE]), sb("c_ends", [P, 2, NE])
        slotf = sb("c_slotf", [P, T])
        tabf, done_e = sb("c_tabf", [1, TABLE]), sb("c_done_e", [1, TG, NE])
        blank, cleared = sb("c_blank", [P, ROW]), sem("c_cleared")
        w_high = sem("c_w_high")
        psX = ctx.enter_context(nc.psum_tensor("c_psX", [P, KD, CW], F32))
        psH = ctx.enter_context(nc.psum_tensor("c_psH", [L, CW], F32))
        psO = ctx.enter_context(nc.psum_tensor("c_psO", [P, CH, D], F32))
        psR = ctx.enter_context(nc.psum_tensor("c_psR", [P, T, NE], F32))
        psC = ctx.enter_context(nc.psum_tensor("c_psC", [P, 2, T, NE], F32))
        names = ("w_in", "dve", "pool", "consts", "var", "rstd_s", "xn_s", "xT_ps", "xT_sb", "h_ps", "sq_s",
                 "inner_s", "th_s", "g_s", "o_ps", "x_done", "r_ps", "shift", "exp", "oh_s", "count_ps", "slot_s")
        (w_in, dve, pool_sem, consts, var_ready, rstd_ready, xn_ready, xT_ps, xT_sb, h_ps, sq_ready, inner_ready,
         th_ready, g_ready, o_ps, x_done, r_ps, shifted, exp_done, oh_ready, count_ps, slot_ready) = (
             sem("c_" + n) for n in names)
        ORDER = [("mlp", 0)] + [w for n in range(1, NC) for w in (("mlp", n), ("route", n - 1))] + [("route", NC - 1)]
        AT = {w: i for i, w in enumerate(ORDER)}
        block = ctx.enter_context(nc.Block())

        @block.sync
        def _(sp):
            sp.dma_start(ctxT[:], io["ctxT"]).then_inc(w_in, 16)
            sp.dma_start(ctxs[:], io["ctx"]).then_inc(w_in, 16)
            sp.dma_start(wr[:], io["m_wr"]).then_inc(w_in, 16)
            for e in range(2):
                fetch_expert(sp, t, io, e)
            sp.wait_ge(cleared, 1)
            sp.dma_start(t["rows"].rearrange("(g p) r -> p g r", p=P),
                         blank[:].unsqueeze(1).to_broadcast([P, TG, ROW])).then_inc(t["rows_cleared"], 16)

        @block.gpsimd
        def _(pool):
            link = Link(pool, pool_sem)
            link(pool.memset(blank[:], 0.0))
            pool.memset(blank[:, D + 3:], float(2 * B * S)).then_inc(cleared, 1)
            pool.memset(mhalf[:], -0.5)
            pool.iota(numi[:], pattern=[[1, 32]], base=0, channel_multiplier=0)
            pool.iota(tok[:], pattern=[[P, T]], base=0, channel_multiplier=1)
            pool.memset(ones[:], 1.0)
            link(pool.memset(before[:], 1.0))
            pool.affine_select(out=before[:], in_=before[:], compare_op=ALU.is_gt, fill=0.0, base=0,
                               pattern=[[1, P]], channel_multiplier=-1).then_inc(consts, 1)
            pool.wait_ge(consts, 1)
            for i, (kind, n) in enumerate([("mlp", n) for n in range(NC)] + [("route", n) for n in range(NC)]):
                pool.wait_ge(var_ready, i + 1)
                pool.tensor_tensor(rstd[:, n * CH:(n + 1) * CH], rstd[:, n * CH:(n + 1) * CH], mhalf[:],
                                   ALU.pow).then_inc(rstd_ready, 1)
                x, q = divmod(i, NC)
                part = slice(q * WE // NC, (q + 1) * WE // NC)
                pool.wait_ge(w_high, x + 1)
                pool.tensor_tensor(t["wl"][:, x, part], t["wst"][:, x, part], t["wh"][:, x, part],
                                   ALU.subtract).then_inc(t["w_ready"] if q == NC - 1 else t["w_split"], 1)

        @block.scalar
        def _(act):
            for x in range(2):
                act.wait_ge(t["w_in"][x], 32)
                act.copy(t["wh"][:, x], t["wst"][:, x]).then_inc(w_high, 1)
            for i, (kind, n) in enumerate(ORDER):
                act.wait_ge(xT_ps, i + 1)
                if i >= 2:
                    act.wait_ge(r_ps if ORDER[i - 2][0] == "route" else h_ps, ORDER[i - 2][1] + 1)
                act.copy(xnT[:, i % 2], psX[:]).then_inc(xT_sb, 1)
                if kind == "mlp":
                    act.wait_ge(h_ps, n + 1)
                    act.activation(sq[:, n % 2], psH[:], ACT.Square).then_inc(sq_ready, 1)
                    act.wait_ge(inner_ready, n + 1)
                    act.activation(th[:, n % 2], inner[:, n % 2], ACT.Tanh, bias=0.0,
                                   scale=0.7978845608028654).then_inc(th_ready, 1)
            act.wait_ge(shifted, 1)
            act.activation(e[:], e[:], ACT.Exp).then_inc(exp_done, 1)

        @block.vector
        def _(vec):
            link = Link(vec, dve)

            def variances(n, mv_, par):
                link(layernorm_stats(vec, link, [x_all[:, n * CH + j, 0:D] for j in range(CH)], stats[:, par],
                                     mv_[:, n * CH:(n + 1) * CH]))
                vec.tensor_scalar(rstd[:, n * CH:(n + 1) * CH], mv_[:, n * CH:(n + 1) * CH, 1], EPS, None,
                                  ALU.add).then_inc(var_ready, 1)

            def normalise(i, n, mv_, count):
                vec.wait_ge(rstd_ready, count)
                if i >= 2:
                    vec.wait_ge(xT_ps, i - 1)
                for j in range(CH):
                    t_ = n * CH + j
                    ins = vec.tensor_scalar(xn[:, i % 2, j], x_all[:, t_, 0:D], mv_[:, t_, 0:1], rstd[:, t_:t_ + 1],
                                            ALU.subtract, ALU.mult)
                ins.then_inc(xn_ready, 1)

            for n in range(NC):
                variances(n, mv, 0)
            normalise(0, 0, mv, 1)
            for i, (kind, n) in enumerate(ORDER):
                if kind == "mlp":
                    if n + 1 < NC:
                        normalise(AT["mlp", n + 1], n + 1, mv, n + 2)
                    p = n % 2
                    vec.wait_ge(sq_ready, n + 1)
                    link(vec.tensor_scalar(inner[:, p], sq[:, p], 0.044715, 1.0, ALU.mult, ALU.add))
                    vec.tensor_tensor(inner[:, p], psH[:], inner[:, p], ALU.mult).then_inc(inner_ready, 1)
                    vec.wait_ge(th_ready, n + 1)
                    vec.scalar_tensor_tensor(g[:, p], th[:, p], 1.0, psH[:], ALU.add, ALU.mult).then_inc(g_ready, 1)
                    vec.wait_ge(o_ps, n + 1)
                    xc = x_all[:, n * CH:(n + 1) * CH, 0:D]
                    vec.scalar_tensor_tensor(xc, psO[:], 0.5, xc, ALU.mult, ALU.add).then_inc(x_done, 1)
                    vec.wait_ge(x_done, n + 1)
                    variances(n, mv4, 1)
                    normalise(AT["route", n], n, mv4, NC + n + 1)
            vec.wait_ge(rstd_ready, 2 * NC)
            vec.wait_ge(consts, 1)
            vec.tensor_copy(x_all[:, :, D], mv4[:, :, 0])
            vec.tensor_copy(x_all[:, :, D + 1], rstd[:])
            vec.tensor_copy(x_all[:, :, D + 3], tok[:])
            link(vec.tensor_copy(num[:], numi[:]))
            vec.wait_ge(r_ps, NC)
            link(vec.tensor_copy(lg[:], psR[:]))
            full = [P, T, NE]
            link(vec.tensor_reduce(best[:], lg[:], AX.X, ALU.max))
            vec.tensor_tensor(e[:], lg[:], best[:].unsqueeze(2).to_broadcast(full), ALU.subtract).then_inc(shifted, 1)
            vec.wait_ge(exp_done, 1)
            link(vec.tensor_reduce(tot[:], e[:], AX.X, ALU.add))
            link(vec.reciprocal(tot[:], tot[:]))
            link(vec.tensor_tensor(e[:], e[:], tot[:].unsqueeze(2).to_broadcast(full), ALU.mult))
            link(vec.tensor_reduce(x_all[:, :, D + 2], e[:], AX.X, ALU.max))
            link(vec.tensor_tensor(first[:], e[:], x_all[:, :, D + 2:D + 3].to_broadcast(full), ALU.is_equal))
            link(vec.tensor_scalar(first[:], first[:], -float(NE), None, ALU.mult))
            link(vec.tensor_tensor(first[:], first[:], num[:, 0:NE].unsqueeze(1).to_broadcast(full), ALU.add))
            link(vec.tensor_reduce(low[:], first[:], AX.X, ALU.min))
            vec.tensor_tensor(oh[:], first[:], low[:].unsqueeze(2).to_broadcast(full), ALU.is_equal).then_inc(oh_ready, 1)
            vec.wait_ge(count_ps, 1)
            vec.tensor_copy(rank[:], psC[:, 0])
            link(vec.tensor_copy(scan[:, 0], psC[:, 1]))
            a = 0
            for d in (1, 2, 4, 8):
                vec.tensor_copy(scan[:, 1 - a, 0:d], scan[:, a, 0:d])
                link(vec.tensor_tensor(scan[:, 1 - a, d:T], scan[:, a, d:T], scan[:, a, 0:T - d], ALU.add))
                a = 1 - a
            vec.tensor_tensor(base[:], psC[:, 1], scan[:, a], ALU.subtract)
            link(vec.tensor_scalar(steps[:], num[:, 0:T], float(P), None, ALU.mult))
            link(vec.tensor_tensor(fits[:], scan[:, a, T - 1].unsqueeze(2).to_broadcast([P, NE, T]),
                                   steps[:].unsqueeze(1).to_broadcast([P, NE, T]), ALU.is_gt))
            link(vec.tensor_reduce(tiles[:], fits[:], AX.X, ALU.add))
            link(vec.tensor_scalar(tiles[:], tiles[:], 1.0, None, ALU.max))
            link(vec.tensor_copy(ends[:, 0], tiles[:]))
            a = 0
            for d in (1, 2, 4):
                vec.tensor_copy(ends[:, 1 - a, 0:d], ends[:, a, 0:d])
                link(vec.tensor_tensor(ends[:, 1 - a, d:NE], ends[:, a, d:NE], ends[:, a, 0:NE - d], ALU.add))
                a = 1 - a
            end = ends[:, a]
            link(vec.tensor_tensor(tiles[:], end, tiles[:], ALU.subtract))
            link(vec.tensor_scalar(tiles[:], tiles[:], float(P), None, ALU.mult))
            link(vec.tensor_tensor(rank[:], rank[:], base[:], ALU.subtract))
            link(vec.tensor_tensor(rank[:], rank[:], tiles[:].unsqueeze(1).to_broadcast(full), ALU.add))
            link(vec.tensor_tensor(rank[:], rank[:], oh[:], ALU.mult))
            link(vec.tensor_reduce(slotf[:], rank[:], AX.X, ALU.add))
            vec.tensor_copy(slot[:], slotf[:]).then_inc(slot_ready, 1)
            link(vec.tensor_tensor(done_e[:], end[0:1].unsqueeze(1).to_broadcast([1, TG, NE]),
                                   num[0:1, 0:TG].unsqueeze(2).to_broadcast([1, TG, NE]), ALU.is_le))
            link(vec.tensor_reduce(tabf[:, 0:TG], done_e[:], AX.X, ALU.add))
            link(vec.tensor_scalar(tabf[:, 0:TG], tabf[:, 0:TG], float(NE - 1), None, ALU.min))
            vec.tensor_scalar(tabf[:, TG:2 * TG], num[0:1, 0:TG], 1.0, end[0:1, NE - 1:NE], ALU.add, ALU.min)
            vec.tensor_copy(tabf[:, 2 * TG:LAST], end[0:1])
            link(vec.tensor_scalar(tabf[:, LAST:], end[0:1, NE - 1:NE], -1.0, None, ALU.add))
            vec.tensor_copy(table[:], tabf[:])

        @block.tensor
        def _(pe):
            pe.wait_ge(w_in, 48)
            pe.wait_ge(consts, 1)
            for i, (kind, n) in enumerate(ORDER):
                pe.wait_ge(xn_ready, i + 1)
                if i >= 1:
                    pe.wait_ge(xT_sb, i)
                for k in range(KD):
                    for j in range(CH):
                        ins = pe.transpose(psX[:, k, j * P:(j + 1) * P], xn[:, i % 2, j, k * P:(k + 1) * P], ident[:])
                ins.then_inc(xT_ps, 1)
                pe.wait_ge(xT_sb, i + 1)
                if kind == "mlp":
                    b = n // (NC // B)
                    if n >= 1:
                        pe.wait_ge(g_ready, n)
                    for k in range(KD):
                        ins = pe.matmul(psH[:], ctxT[:, b, k, :], xnT[:, i % 2, k], start=(k == 0), stop=(k == KD - 1))
                    ins.then_inc(h_ps, 1)
                    pe.wait_ge(g_ready, n + 1)
                    if n >= 1:
                        pe.wait_ge(x_done, n)
                    for j in range(CH):
                        ins = pe.matmul(psO[:, j], g[:, n % 2, j * P:(j + 1) * P], ctxs[:, b], start=True, stop=True)
                    ins.then_inc(o_ps, 1)
                else:
                    for j in range(CH):
                        for k in range(KD):
                            ins = pe.matmul(psR[:, n * CH + j], xnT[:, i % 2, k, j * P:(j + 1) * P], wr[:, k],
                                            start=(k == 0), stop=(k == KD - 1))
                    ins.then_inc(r_ps, 1)
            pe.wait_ge(oh_ready, 1)
            pe.matmul(psC[:, 0], before[:], oh[:], start=True, stop=True)
            pe.matmul(psC[:, 1], ones[:], oh[:], start=True, stop=True).then_inc(count_ps, 1)


def sort_rows(nc, top, t, io):
    scattered = top.enter_context(nc.semaphore("s_scattered"))
    back = [top.enter_context(nc.semaphore(f"s_back{i}")) for i in range(2)]
    t["back"] = back
    with nc.Block() as block:
        @block.gpsimd
        def _(pool):
            pool.wait_ge(t["rows_cleared"], 16)
            for i in range(T):
                pool.indirect_dma_start(out=t["rows"], out_offset=bass.IndirectOffsetOnAxis(
                    ap=t["slot"][:, i:i + 1].bitcast(U32), axis=0), in_=t["x_all"][:, i, :], in_offset=None,
                    bounds_check=TG * P - 1, oob_is_err=False).then_inc(scattered, 16)

        @block.sync
        def _(sp):
            sp.wait_ge(scattered, 16 * T)
            rows = t["rows"].rearrange("(g p) r -> p g r", p=P)
            sp.dma_start(t["xg"][:, 0:2], rows[:, 0:2]).then_inc(back[0], 16)
            sp.dma_start(t["xg"][:, 2:TG], rows[:, 2:TG]).then_inc(back[1], 16)


def experts(nc, top, t, io):
    with ExitStack() as ctx:
        def sb(name, shape, dt=F32):
            return ctx.enter_context(nc.sbuf_tensor(name, shape, dt))

        def sem(name):
            return top.enter_context(nc.semaphore(name))

        ident, table, xg, wst, wh, wl = (t[n] for n in ("ident", "table", "xg", "wst", "wh", "wl"))
        b1, b2 = sb("e_b1", [P, NE * FF]), sb("e_b2", [P, NE * D])
        xn = sb("e_xn", [P, D])
        xh, xl = sb("e_xh", [P, KD, P], F32R), sb("e_xl", [P, KD, P], F32R)
        h = sb("e_h", [P, 2, 512])
        hh, hl = sb("e_hh", [P, FB, P], F32R), sb("e_hl", [P, FB, P], F32R)
        y = sb("e_y", [P, D])
        tokid = sb("e_tokid", [P, MT], I32)
        psX = ctx.enter_context(nc.psum_tensor("e_psX", [P, KD, P], F32))
        psH = [ctx.enter_context(nc.psum_tensor(f"e_psH{i}", [P, 512], F32)) for i in range(2)]
        psT = [ctx.enter_context(nc.psum_tensor(f"e_psT{i}", [P, FB // 2, P], F32)) for i in range(2)]
        psY = ctx.enter_context(nc.psum_tensor("e_psY", [P, 512], F32))
        names = ("b_in", "dve", "w_high", "xn_s", "xT_ps", "xh_s", "xl_s", "h_ps", "h_sb", "hT_ps", "hh_s", "hl_s",
                 "y_ps", "y_s", "y_done", "tok_s", "out_s", "hgone")
        (b_in, dve, w_high, xn_ready, xT_ps, xh_ready, xl_ready, h_ps, h_sb, hT_ps, hh_ready, hl_ready, y_ps, y_sb,
         y_done, tok_ready, out_done, hgone) = (sem("e_" + n) for n in names)
        w_in, w_ready, back = t["w_in"], t["w_ready"], t["back"]
        block = ctx.enter_context(nc.Block())

        def upto(eng, s, n, per, c):
            if not isinstance(n, int):
                eng.wait_ge(s, n * per + c)
            elif per * n + c > 0:
                eng.wait_ge(s, per * n + c)

        def load(eng, at, top_value, least=0):
            return eng.value_load(table[0:1, bass.ds(at, 1)], min_val=least, max_val=top_value)

        def tiles(eng, body):
            body(0)
            with eng.Fori(1, load(eng, TILES, MT, NE)) as g:
                body(g)

        @block.sync
        def _(sp):
            sp.dma_start(b1[:], io["m_b1"]).then_inc(b_in, 16)
            sp.dma_start(b2[:], io["m_b2"]).then_inc(b_in, 16)
            for e in range(2, NE):
                sp.wait_ge(w_ready, e - 1)
                fetch_expert(sp, t, io, e)
            sp.wait_ge(out_done, 16 * MT)

        @block.gpsimd
        def _(pool):
            for e in range(2, NE):
                through = load(pool, 2 * TG + e - 2, MT)
                pool.wait_ge(w_in[e % 2], 32 * (e // 2 + 1))
                pool.wait_ge(y_ps, through)
                pool.tensor_scalar(wh[:, e % 2], wst[:, e % 2], 1.0, 0.0, ALU.mult, ALU.add).then_inc(w_high, 1)
                pool.wait_ge(w_high, e - 1)
                pool.tensor_tensor(wl[:, e % 2], wst[:, e % 2], wh[:, e % 2], ALU.subtract).then_inc(w_ready, 1)
            most = pool.to_reg(B * S - 1)
            for g in range(MT):
                through = load(pool, TG + g, MT)
                pool.wait_ge(tok_ready, 1)
                pool.wait_ge(y_done, through)
                pool.indirect_dma_start(out=io["out"], out_offset=bass.IndirectOffsetOnAxis(
                    ap=tokid[:, g:g + 1].bitcast(U32), axis=0), in_=xg[:, g, 0:D], in_offset=None,
                    bounds_check=most, oob_is_err=False).then_inc(out_done, 16)

        @block.scalar
        def _(act):
            def x_high(g):
                upto(act, xT_ps, g, 1, 1)
                upto(act, h_ps, g, 2, 0)
                act.copy(xh[:], psX[:]).then_inc(xh_ready, 1)

            x_high(0)

            def body(g):
                x_high(g + 1)
                for hf in range(2):
                    upto(act, hT_ps, g, 2, hf + 1)
                    upto(act, y_ps, g, 1, 0)
                    act.activation(hh[:, hf * FB // 2:(hf + 1) * FB // 2], psT[hf][:], ACT.Relu).then_inc(hh_ready, 1)

            tiles(act, body)

        @block.vector
        def _(vec):
            link = Link(vec, dve)

            def normalise(g):
                upto(vec, xT_ps, g, 1, 0)
                row = xg[:, bass.ds(g, 1), :].rearrange("p a r -> p (a r)")
                vec.tensor_scalar(xn[:], row[:, 0:D], row[:, D:D + 1], row[:, D + 1:D + 2], ALU.subtract,
                                  ALU.mult).then_inc(xn_ready, 1)

            def x_low(g):
                upto(vec, xh_ready, g, 1, 1)
                vec.tensor_tensor(xl[:], psX[:], xh[:], ALU.subtract).then_inc(xl_ready, 1)

            def finish(g):
                e = load(vec, g, NE - 1)
                upto(vec, y_ps, g, 1, 1)
                row = xg[:, bass.ds(g, 1), :].rearrange("p a r -> p (a r)")
                vec.tensor_tensor(y[:], psY[:, 0:D], b2[:, bass.ds(e * D, D)], ALU.add).then_inc(y_sb, 1)
                upto(vec, y_sb, g, 1, 1)
                vec.scalar_tensor_tensor(row[:, 0:D], y[:], row[:, D + 2:D + 3], row[:, 0:D], ALU.mult,
                                         ALU.add).then_inc(y_done, 1)

            vec.wait_ge(back[0], 16)
            vec.wait_ge(back[1], 16)
            vec.tensor_copy(tokid[:], xg[:, 0:MT, D + 3]).then_inc(tok_ready, 1)
            vec.wait_ge(b_in, 32)
            normalise(0)
            x_low(0)
            normalise(1)

            def body(g):
                e = load(vec, g, NE - 1)
                for hf in range(2):
                    upto(vec, h_ps, g, 2, hf + 1)
                    upto(vec, hT_ps, g, 2, 0)
                    vec.tensor_tensor(h[:, hf], psH[hf][:], b1[:, bass.ds(e * FF + hf * 512, 512)],
                                      ALU.add).then_inc(h_sb, 1)
                if not isinstance(g, int):
                    finish(g - 1)
                x_low(g + 1)
                for hf in range(2):
                    upto(vec, hh_ready, g, 2, hf + 1)
                    part = slice(hf * FB // 2, (hf + 1) * FB // 2)
                    vec.scalar_tensor_tensor(hl[:, part], psT[hf][:], 0.0, hh[:, part], ALU.max,
                                             ALU.subtract).then_inc(hl_ready, 1)
                normalise(g + 2)

            tiles(vec, body)
            finish(load(vec, LAST, MT - 1, NE - 1))

        @block.tensor
        def _(pe):
            def transpose_x(g):
                upto(pe, xn_ready, g, 1, 1)
                upto(pe, xl_ready, g, 1, 0)
                for k in range(KD):
                    ins = pe.transpose(psX[:, k], xn[:, k * P:(k + 1) * P], ident[:])
                ins.then_inc(xT_ps, 1)

            def hidden(g):
                e = load(pe, g, NE - 1)
                pe.wait_ge(w_ready, e + 1)
                upto(pe, xl_ready, g, 1, 1)
                for hf in range(2):
                    upto(pe, h_sb, g, 2, hf - 1)
                    for k in range(KD):
                        off = (e % 2) * WE + (k * FF + hf * 512)
                        for n, (x_, w_) in enumerate(((xh, wh), (xl, wh), (xh, wl))):
                            ins = pe.matmul(psH[hf][:], x_[:, k], w_[:].rearrange("p a w -> p (a w)")[:, bass.ds(off, 512)],
                                            start=(k == 0 and n == 0), stop=(k == KD - 1 and n == 2))
                    ins.then_inc(h_ps, 1)

            def transpose_h(g):
                for hf in range(2):
                    upto(pe, h_sb, g, 2, hf + 1)
                    upto(pe, hl_ready, g, 2, hf - 1)
                    for k in range(FB // 2):
                        ins = pe.transpose(psT[hf][:, k], h[:, hf, k * P:(k + 1) * P], ident[:])
                    ins.then_inc(hT_ps, 1)

            def output(g):
                e = load(pe, g, NE - 1)
                upto(pe, hl_ready, g, 2, 2)
                upto(pe, y_sb, g, 1, 0)
                for k in range(FB):
                    off = (e % 2) * WE + (KD * FF + k * D)
                    for n, (h_, w_) in enumerate(((hh, wh), (hl, wh), (hh, wl))):
                        ins = pe.matmul(psY[:, 0:D], h_[:, k], w_[:].rearrange("p a w -> p (a w)")[:, bass.ds(off, D)],
                                        start=(k == 0 and n == 0), stop=(k == FB - 1 and n == 2))
                ins.then_inc(y_ps, 1)

            transpose_x(0)

            def body(g):
                hidden(g)
                if not isinstance(g, int):
                    output(g - 1)
                transpose_x(g + 1)
                transpose_h(g)

            tiles(pe, body)
            output(load(pe, LAST, MT - 1, NE - 1))


def fetch_expert(sp, t, io, e):
    sp.dma_start(t["wst"][:, e % 2, 0:KD * FF], io["m_w1"][e]).then_inc(t["w_in"][e % 2], 16)
    sp.dma_start(t["wst"][:, e % 2, KD * FF:WE], io["m_w2"][e]).then_inc(t["w_in"][e % 2], 16)


def program(nc, io):
    with ExitStack() as top:
        def sb(name, shape, dt=F32):
            return top.enter_context(nc.sbuf_tensor(name, shape, dt))

        t = {"x_all": sb("x_all", [P, T, ROW]), "ident": sb("ident", [P, P])}
        t["table"], t["slot"] = sb("table", [1, TABLE], I32), sb("slot", [P, T], I32)
        t["w_in"] = [top.enter_context(nc.semaphore(f"w_in{i}")) for i in range(2)]
        for name in ("w_ready", "w_split", "rows_cleared"):
            t[name] = top.enter_context(nc.semaphore(name))
        t["rows"] = nc.dram_tensor("rows", (TG * P, ROW), F32, kind="Internal").ap()
        cross_attention(nc, top, t, io)
        with ExitStack() as attention:
            for name, shape, dt in (("xnT", [P, KD, B * S], F32), ("v_all", [P, B * NA + 1, S // P, HD2], F32),
                                    ("head_col", [1, B * NA + 1], I32)):
                t[name] = attention.enter_context(nc.sbuf_tensor(name, shape, dt))
            gate_and_project(nc, top, t, io)
            gated_attention(nc, top, t, io)
        for name, shape, dt in (("wst", [P, 2, WE], F32), ("wh", [P, 2, WE], F32R), ("wl", [P, 2, WE], F32R),
                                ("xg", [P, TG, ROW], F32)):
            t[name] = sb(name, shape, dt)
        context_mlp(nc, top, t, io)
        sort_rows(nc, top, t, io)
        experts(nc, top, t, io)


def kernel(**inputs):
    import numpy as np
    import concourse.bacc as bacc
    from concourse.bass_utils import run_bass_kernel_spmd

    def blocks(w):
        return w.reshape(-1, P, w.shape[-1]).transpose(1, 0, 2)

    def rows(v, n=P):
        return np.broadcast_to(v, (n,) + v.shape)

    a = {k: np.asarray(v) for k, v in inputs.items()}
    ctx_ = a["ctx_1024"]
    arrays = {
        "x": a["x"].reshape(T, P, D).transpose(1, 0, 2),
        "ctxT": ctx_.reshape(B, L, KD, P).transpose(3, 0, 2, 1),
        "mask": rows(a["mask_Bx1x1xS2_ik0"].reshape(B, L)),
        "xa_wq": blocks(a["L0_xattn_Wq"].T), "xa_wk": blocks(a["L0_xattn_Wk"].T),
        "xa_wv": blocks(a["L0_xattn_Wv"].T), "xa_wo": blocks(a["L0_xattn_Wo"].T),
        "xa_bq": a["L0_xattn_bq"].reshape(KD, P).T, "xa_bk": a["L0_xattn_bk"].reshape(KD, P).T,
        "xa_bv": rows(a["L0_xattn_bv"]), "xa_bo": rows(a["L0_xattn_bo"]),
        "ctx": ctx_.transpose(1, 0, 2),
        "m_wr": blocks(a["L1_ffn_w_router"]),
        "m_w1": a["L1_ffn_w1"].reshape(NE, KD, P, FF).transpose(0, 2, 1, 3).reshape(NE, P, KD * FF),
        "m_w2": a["L1_ffn_w2"].reshape(NE, FB, P, D).transpose(0, 2, 1, 3).reshape(NE, P, FB * D),
        "m_b1": rows(a["L1_ffn_b1"].reshape(-1)), "m_b2": rows(a["L1_ffn_b2"].reshape(-1)),
        "f_wq": blocks(a["L0_ffn_Wq"]), "f_wk": blocks(a["L0_ffn_Wk"]), "f_wv": blocks(a["L0_ffn_Wv"]),
        "f_wr": blocks(a["L0_ffn_Wr"]), "f_br": a["L0_ffn_br"][None],
        "f_bq": a["L0_ffn_bq"][:, None], "f_bk": a["L0_ffn_bk"][:, None], "f_bv": a["L0_ffn_bv"][:, None],
        "f_wo": a["L0_ffn_Wo"].reshape(NA, HD2, D).transpose(1, 0, 2), "f_bo": rows(a["L0_ffn_bo"]),
    }
    nc = bacc.Bacc("TRN2", target_bir_lowering=False, num_devices=1)
    io = {}
    for name, v in arrays.items():
        arrays[name] = v = np.ascontiguousarray(v)
        io[name] = nc.dram_tensor(f"in_{name}", v.shape, mybir.dt.from_np(v.dtype), kind="ExternalInput").ap()
    io["out"] = nc.dram_tensor("out", (B * S, D), F32, kind="ExternalOutput").ap()
    program(nc, io)
    r = run_bass_kernel_spmd(nc, [{f"in_{k}": v for k, v in arrays.items()}], core_ids=[0])
    return r.results[0]["out"].reshape(B, S, D)
```

```python
from contextlib import ExitStack

import concourse.bass as bass
from concourse import mybir

ALU = mybir.AluOpType
ACT = mybir.ActivationFunctionType
AX = mybir.AxisListType
F32 = mybir.dt.float32
F32R = mybir.dt.float32r
BF16 = mybir.dt.bfloat16
I32 = mybir.dt.int32
U32 = mybir.dt.uint32

P = 128
B, S, D = 2, 1024, 256
KD = D // P
T = B * S // P
CH = 4
NC = T // CH
CW = CH * P
EPS = 1e-5
L = 77
H1, HD1 = 16, 16
HH = H1 // 2
GH = 4
HL = HH * L
VC = 5
VR = -(-HL // VC)
H2, HD2, NA = 16, 64, 4
NE, FF = 8, 1024
FB = FF // P
ROW = D + 4
MT = B * S // P + NE - 1
TG = MT + 2
TABLE = 2 * TG + NE + 1
TILES, LAST = 2 * TG + NE - 1, 2 * TG + NE
WE = KD * FF + FB * D
NB = 4


class Link:

    def __init__(self, eng, sem):
        self.eng, self.sem, self.n, self.reg = eng, sem, 0, 0

    def __call__(self, ins, held=None):
        ins.then_inc(self.sem, 1)
        self.n += 1
        count = self.n + self.reg
        if held is not None and not isinstance(self.reg, int):
            count = self.eng.to_reg(count)
            self.eng.wait_ge(held, 1)
        self.eng.wait_ge(self.sem, count)


def layernorm_stats(vec, link, x_tiles, stats, mv):
    for j, x in enumerate(x_tiles):
        ins = vec.bn_stats(stats[:, j, :], x)
    link(ins)
    for j in range(len(x_tiles)):
        ins = vec.bn_aggr(mv[:, j, :], stats[:, j, :])
    return ins


def cross_attention(nc, top, t, io):
    with ExitStack() as ctx:
        def sb(name, shape, dt=F32):
            return ctx.enter_context(nc.sbuf_tensor(name, shape, dt))

        def sem(name):
            return top.enter_context(nc.semaphore(name))

        NT = T // B
        W = B * P
        U = B * KD
        HP = P // 2
        LAG = 3
        x_all, ident = t["x_all"], t["ident"]
        xv = x_all[:].rearrange("p (b t) r -> p b t r", b=B)
        wk = sb("a_wk", [P, KD, KD, 2, P])
        wq, wv, wo = (sb(f"a_{n}", [P, KD, D]) for n in ("wq", "wv", "wo"))
        bq, bk, bk4 = sb("a_bq", [P, KD]), sb("a_bk", [P, KD, 2]), sb("a_bk4", [P, KD, 2])
        bv, bo = sb("a_bv", [P, D]), sb("a_bo", [P, D])
        ctxT = sb("a_ctxT", [P, B, KD, L])
        mask_i, keep = sb("a_mask", [P, B, L], I32), sb("a_keep", [P, B, L])
        heads8, heads4 = sb("a_heads8", [P, HH]), sb("a_heads4", [P, GH])
        kmask = sb("a_kmask", [P, B, GH, L])
        drop, fill = sb("a_drop", [3, B, GH, L], BF16), sb("a_fill", [3, P], BF16)
        kT = sb("a_kT", [P, KD, 2, B, L])
        khT, klT = sb("a_khT", [P, KD, 2, B, L], F32R), sb("a_klT", [P, KD, 2, B, L], F32R)
        kh, kl = sb("a_kh", [P, KD, 2, B, GH, L], F32R), sb("a_kl", [P, KD, 2, B, GH, L], F32R)
        sel, v_sb = sb("a_sel", [L, VC * VR]), sb("a_v", [L, B, D])
        vmask, vblk = sb("a_vmask", [VR, VC, HH]), sb("a_vblk", [VR, B, KD, VC, P])
        stats, mv = sb("a_stats", [P, 2, B, 6]), sb("a_mv", [P, 2, B, 2])
        rstd, mhalf = sb("a_rstd", [P, 2, B]), sb("a_mhalf", [P, B])
        xn, xnT, hT = sb("a_xn", [P, B, D]), sb("a_xnT", [P, KD, W]), sb("a_hT", [P, KD, W])
        qs = [sb(f"a_qs{i}", [P, 2, KD, W], F32R) for i in range(2)]
        pr = sb("a_p", [P, U, VC * VR])
        mx, sm, rs = sb("a_mx", [P, U, HH]), sb("a_sm", [P, U, HH]), sb("a_rs", [P, U, HH])
        pT = sb("a_pT", [VR, 2, KD, VC, W])
        psS = [ctx.enter_context(nc.psum_tensor(f"a_psS{m}", [P, 2, 512], F32)) for m in range(2)]
        psT = ctx.enter_context(nc.psum_tensor("a_psT", [P, 2, 512], F32))
        psX = ctx.enter_context(nc.psum_tensor("a_psX", [P, 2, W], F32))
        psQ = ctx.enter_context(nc.psum_tensor("a_psQ", [P, KD, W], F32))

        names = ("x_first", "x_rest", "w_in", "c_in", "v_in", "warm", "dve", "pool", "var", "rstd_s", "xn_s", "bo_added", "heads_s",
                 "ident_s", "consts", "keep_s", "k_ps", "k_sb", "klT_s", "kh_s", "kl_s", "v_ps", "v_s", "vrep_ps",
                 "vblk_s", "xT_ps", "x_read", "q_ps", "q_hi", "q_lo", "s_ps", "sub_done", "exp_done", "rs_s", "pn_s",
                 "pT_ps", "pT_sb", "h_ps", "h_sb", "o_ps")
        (x_first, x_rest, w_in, c_in, v_in, warm, dve, pool_sem, var_ready, rstd_ready, xn_ready, bo_added, heads_ready,
         ident_ready, consts, keep_ready, k_ps, k_sb, klT_ready, kh_ready, kl_ready, v_ps, v_ready, vrep_ps,
         vblk_ready, xT_ps, x_read, q_ps, q_hi, q_lo, s_ps, sub_done, exp_done, rs_ready, pn_ready,
         pT_ps, pT_sb, h_ps, h_sb, o_ps) = (sem("a_" + n) for n in names)

        def iterations(eng, body):
            body(0)
            with eng.Fori(1, NT // 2 - 1) as i:
                body(i)
            body(NT // 2 - 1)

        def upto(eng, s, i, per, c):
            if not isinstance(i, int) or per * i + c > 0:
                eng.wait_ge(s, i * per + c)

        def reads(n):
            return min(n + 2, NT) + max(n - 2, 0) if isinstance(n, int) else n * 2

        def wide(ps):
            return ps[0:VR].rearrange("p a b -> p (a b)")[:, 0:VC * P]

        block = ctx.enter_context(nc.Block())

        @block.sync
        def _(sp):
            io_x = io["x"].rearrange("p (b t) r -> p b t r", b=B)
            sp.dma_start(ctxT[:], io["ctxT"]).then_inc(c_in, 16)
            for b in range(B):
                sp.dma_start(xv[:, b, 0:2, 0:D], io_x[:, b, 0:2, :]).then_inc(x_first, 16)
            for b in range(B):
                sp.dma_start(xv[:, b, 2:NT, 0:D], io_x[:, b, 2:NT, :]).then_inc(x_rest, 16)
            sp.dma_start(wo[:], io["xa_wo"]).then_inc(w_in, 16)
            sp.dma_start(bo[:], io["xa_bo"]).then_inc(w_in, 16)

        @block.scalar
        def _(act):
            act.dma_start(wk[:], io["xa_wk"]).then_inc(c_in, 16)
            act.dma_start(mask_i[:], io["mask"]).then_inc(c_in, 16)
            act.dma_start(bk[:], io["xa_bk"]).then_inc(c_in, 16)
            act.dma_start(wv[:], io["xa_wv"]).then_inc(v_in, 16)
            act.dma_start(bv[:], io["xa_bv"]).then_inc(v_in, 16)
            act.wait_ge(warm, 1)
            act.activation(bk4[:, 0], bk4[:, 0], ACT.Exp).then_inc(warm, 1)
            act.dma_start(wq[:], io["xa_wq"]).then_inc(w_in, 16)
            act.dma_start(bq[:], io["xa_bq"]).then_inc(w_in, 16)

            def copy_x(i, n):
                upto(act, xT_ps, i, 2, n + 1)
                act.copy(xnT[:], psX[:]).then_inc(x_read, 1)

            def query_high(i, n):
                upto(act, q_ps, i, 2, n + 1)
                for a in range(2):
                    for m in range(KD):
                        half = slice(a * HP, (a + 1) * HP)
                        ins = act.activation(qs[n % 2][half, a, m], psQ[half, m], ACT.Identity,
                                             bias=bq[half, m:m + 1], scale=1.0)
                ins.then_inc(q_hi, 1)

            def copy_h(i, n):
                upto(act, h_ps, i, 2, n + 1)
                act.copy(hT[:], psQ[:]).then_inc(h_sb, 1)

            def copy_p(i, g):
                upto(act, pT_ps, i, 2 * U, g + 1)
                b, m = divmod(g % U, KD)
                act.copy(pT[:, g // U % 2, m, :, b * P:(b + 1) * P],
                         wide(psT).rearrange("p (c n) -> p c n", c=VC)).then_inc(pT_sb, 1)

            act.wait_ge(keep_ready, 1)
            act.wait_ge(k_ps, 1)
            for m in range(KD):
                for a in range(2):
                    ins = act.activation(kT[:, m, a], psS[m][:, a, 0:B * L].rearrange("p (b l) -> p b l", b=B),
                                         ACT.Identity, bias=bk4[:, m, a:a + 1], scale=HD1 ** -0.5)
            ins.then_inc(k_sb, 1)
            copy_x(0, 0)
            act.wait_ge(w_in, 64)
            query_high(0, 0)
            copy_x(0, 1)

            def body(i):
                for g in range(2 * U):
                    c, u = divmod(g, U)
                    n = 2 * i + c if isinstance(i, int) else 2
                    if not (isinstance(i, int) and 2 * U * i + g < LAG):
                        copy_p(i, g - LAG)
                    if u == 0 and n >= 2:
                        copy_h(i, c - 2)
                    upto(act, sub_done, i, 2 * U, g + 1)
                    act.activation(pr[:, u, 0:HL], pr[:, u, 0:HL], ACT.Exp).then_inc(exp_done, 1)
                    if u == 0 and n + 1 < NT:
                        query_high(i, c + 1)
                    if u == 3 and n + 2 < NT:
                        copy_x(i, c + 2)

            iterations(act, body)
            end = NT // 2
            copy_p(end, -3)
            copy_h(end, -2)
            copy_p(end, -2)
            copy_p(end, -1)
            copy_h(end, -1)

        @block.gpsimd
        def _(pool):
            link = Link(pool, pool_sem)

            def power(i, n):
                upto(pool, var_ready, i, 2, n + 1)
                r = rstd[:, n % 2]
                pool.tensor_tensor(r, r, mhalf[:], ALU.pow).then_inc(rstd_ready, 1)

            pool.memset(mhalf[:], -0.5)
            link(pool.memset(heads8[:], 1.0))
            link(pool.affine_select(out=heads8[:], in_=heads8[:], compare_op=ALU.is_ge, fill=0.0, base=0,
                                    pattern=[[-HD1, HH]], channel_multiplier=1))
            link(pool.affine_select(out=heads8[:], in_=heads8[:], compare_op=ALU.is_ge, fill=0.0, base=HD1 - 1,
                                    pattern=[[HD1, HH]], channel_multiplier=-1))
            pool.tensor_tensor(heads4[:], heads8[:, 0:GH], heads8[:, GH:HH], ALU.add).then_inc(heads_ready, 1)
            link(pool.memset(ident[:], 0.0))
            pool.affine_select(out=ident[:], in_=ident[:], compare_op=ALU.not_equal, fill=1.0, base=0,
                               pattern=[[-1, P]], channel_multiplier=1).then_inc(ident_ready, 1)
            power(0, 0)
            link(pool.memset(sel[:], 0.0))
            s3 = sel[:, 0:HL].rearrange("p (h l) -> p h l", h=HH)
            pool.affine_select(out=s3, in_=s3, compare_op=ALU.not_equal, fill=1.0, base=0,
                               pattern=[[0, HH], [-1, L]], channel_multiplier=1)
            link(pool.memset(fill[:], -1024.0 * 9764864))
            link(pool.affine_select(out=fill[:], in_=fill[:], compare_op=ALU.is_gt, fill=-1024.0 * 760, base=1,
                                    pattern=[[0, P]], channel_multiplier=-1))
            link(pool.affine_select(out=fill[:], in_=fill[:], compare_op=ALU.is_gt, fill=-1024.0, base=2,
                                    pattern=[[0, P]], channel_multiplier=-1))
            link(pool.memset(vmask[:], 1.0))
            link(pool.affine_select(out=vmask[:], in_=vmask[:], compare_op=ALU.is_ge, fill=0.0, base=0,
                                    pattern=[[VR, VC], [-L, HH]], channel_multiplier=1))
            link(pool.affine_select(out=vmask[:], in_=vmask[:], compare_op=ALU.is_ge, fill=0.0, base=L - 1,
                                    pattern=[[-VR, VC], [L, HH]], channel_multiplier=-1))
            pool.memset(pr[:, :, HL:], 0.0).then_inc(consts, 1)
            pool.wait_ge(klT_ready, 1)
            power(0, 1)
            for m, a in ((0, 0), (0, 1), (1, 0)):
                pool.tensor_tensor(kl[:, m, a], klT[:, m, a].unsqueeze(2).to_broadcast([P, B, GH, L]), kmask[:],
                                   ALU.mult).then_inc(kl_ready, 1)
            pool.wait_ge(w_in, 64)

            def body(i):
                for g in range(2 * U):
                    c, u = divmod(g, U)
                    n = 2 * i + c if isinstance(i, int) else 2
                    if u == 0:
                        upto(pool, xn_ready, i, 2, c + 1)
                        xc = xv[:, :, 2 * i + c, 0:D] if isinstance(i, int) else \
                            xv[:, :, bass.ds(i * 2 + c, 1), 0:D].rearrange("p b a d -> p (b a) d")
                        pool.tensor_tensor(xc, xc, bo[:].unsqueeze(1).to_broadcast([P, B, D]),
                                           ALU.add).then_inc(bo_added, 1)
                    if u == 1 and n + 2 < NT:
                        power(i, c + 2)
                    upto(pool, rs_ready, i, 2 * U, g + 1)
                    p3 = pr[:, u, 0:HL].rearrange("p (h l) -> p h l", h=HH)
                    pool.tensor_tensor(p3, p3, rs[:, u, :].unsqueeze(2).to_broadcast([P, HH, L]),
                                       ALU.mult).then_inc(pn_ready, 1)

            iterations(pool, body)

        @block.vector
        def _(vec):
            link = Link(vec, dve)

            def variance(i, n):
                at = i * 2 + n
                par = n % 2
                for b in range(B):
                    ins = vec.bn_stats(stats[:, par, b, :], x_all[:, at + b * NT, 0:D])
                link(ins, held=keep_ready)
                for b in range(B):
                    ins = vec.bn_aggr(mv[:, par, b, :], stats[:, par, b, :])
                link(ins)
                vec.tensor_scalar(rstd[:, par, :], mv[:, par, :, 1], EPS, None, ALU.add).then_inc(var_ready, 1)

            def normalise(i, n):
                at = i * 2 + n
                upto(vec, rstd_ready, i, 2, n + 1)
                upto(vec, xT_ps, i, 2, n)
                for b in range(B):
                    ins = vec.tensor_scalar(xn[:, b], x_all[:, at + b * NT, 0:D], mv[:, n % 2, b, 0:1],
                                            rstd[:, n % 2, b:b + 1], ALU.subtract, ALU.mult)
                ins.then_inc(xn_ready, 1)

            def query_low(i, n):
                upto(vec, q_hi, i, 2, n + 1)
                for a in range(2):
                    for m in range(KD):
                        half, other = slice(a * HP, (a + 1) * HP), slice((1 - a) * HP, (2 - a) * HP)
                        ins = vec.scalar_tensor_tensor(qs[n % 2][other, a, m], psQ[half, m], bq[half, m:m + 1],
                                                       qs[n % 2][half, a, m], ALU.add, ALU.subtract)
                ins.then_inc(q_lo, 1)

            def add_output(i, n):
                upto(vec, o_ps, i, 2, n + 1)
                upto(vec, bo_added, i, 2, n + 1)
                xc = xv[:, :, 2 * i + n, 0:D] if isinstance(i, int) else \
                    xv[:, :, bass.ds(i * 2 + n, 1), 0:D].rearrange("p b a d -> p (b a) d")
                vec.tensor_tensor(xc, psX[:], xc, ALU.add).then_inc(x_read, 1)

            def sums(i, g):
                upto(vec, exp_done, i, 2 * U, g + 1)
                w = g % U
                link(vec.tensor_reduce(sm[:, w], pr[:, w, 0:HL].rearrange("p (h l) -> p h l", h=HH), AX.X, ALU.add))
                vec.reciprocal(rs[:, w], sm[:, w]).then_inc(rs_ready, 1)

            vec.memset(bk4[:, 0], 0.0).then_inc(warm, 1)
            vec.wait_ge(x_first, 32)
            variance(0, 0)
            variance(0, 1)
            vec.wait_ge(c_in, 64)
            vec.wait_ge(warm, 2)
            vec.tensor_scalar(bk4[:], bk[:], HD1 ** -0.5, None, ALU.mult)
            link(vec.tensor_scalar(keep[:], mask_i[:], 0, None, ALU.not_equal))
            vec.tensor_scalar(drop[:], keep[0:3].unsqueeze(2).to_broadcast([3, B, GH, L]), -1.0, 1.0,
                              ALU.mult, ALU.add)
            vec.wait_ge(heads_ready, 1)
            for b in range(B):
                ins = vec.tensor_tensor(kmask[:, b], keep[:, b].unsqueeze(1).to_broadcast([P, GH, L]),
                                        heads4[:].unsqueeze(2).to_broadcast([P, GH, L]), ALU.mult)
            ins.then_inc(keep_ready, 1)
            normalise(0, 0)
            vec.wait_ge(v_in, 32)
            vec.wait_ge(v_ps, 1)
            vec.tensor_tensor(v_sb[:], psT[0:L, 0, :].rearrange("p (b d) -> p b d", b=B),
                              bv[0:L].unsqueeze(1).to_broadcast([L, B, D]), ALU.add).then_inc(v_ready, 1)
            vec.wait_ge(k_sb, 1)
            link(vec.tensor_copy(khT[:], kT[:]))
            vec.tensor_tensor(klT[:], kT[:], khT[:], ALU.subtract).then_inc(klT_ready, 1)
            vec.wait_ge(keep_ready, 1)
            for src, dst, m, a in ((khT, kh, 0, 0), (khT, kh, 0, 1), (khT, kh, 1, 0), (khT, kh, 1, 1), (klT, kl, 1, 1)):
                vec.tensor_tensor(dst[:, m, a], src[:, m, a].unsqueeze(2).to_broadcast([P, B, GH, L]), kmask[:],
                                  ALU.mult).then_inc(kh_ready, 1)
                if (m, a) == (1, 0):
                    vec.wait_ge(klT_ready, 1)
            query_low(0, 0)
            normalise(0, 1)
            vec.wait_ge(consts, 1)

            def value_block(i):
                b, m = divmod(i, KD)
                vec.wait_ge(vrep_ps, i + 1)
                vec.tensor_tensor(vblk[:, b, m].rearrange("p c (h d) -> p (c h) d", h=HH),
                                  wide(psT).rearrange("p (c d) -> p c d", d=HD1),
                                  vmask[:].rearrange("p c h -> p (c h)").unsqueeze(2)
                                  .to_broadcast([VR, VC * HH, HD1]), ALU.mult).then_inc(vblk_ready, 1)

            value_block(0)
            vec.wait_ge(x_rest, 32)

            def body(i):
                start = link.n
                if not isinstance(i, int):
                    link.reg = (i - 1) * per_pair
                for g in range(2 * U):
                    c, u = divmod(g, U)
                    n = 2 * i + c if isinstance(i, int) else 2
                    s4 = psS[u % KD][:, :, 0:GH * L].rearrange("p a (g l) -> p a g l", g=GH)
                    upto(vec, s_ps, i, 2 * U, g + 1)
                    link(vec.tensor_reduce(mx[:, u].rearrange("p (a g) -> p a g", a=2), s4, AX.X, ALU.max))
                    upto(vec, pT_ps, i, 2 * U, g + 1 - U)
                    vec.tensor_tensor(pr[:, u, 0:HL].rearrange("p (a g l) -> p a g l", a=2, g=GH), s4,
                                      mx[:, u].rearrange("p (a g) -> p a g", a=2).unsqueeze(3)
                                      .to_broadcast([P, 2, GH, L]), ALU.subtract).then_inc(sub_done, 1)
                    if not (isinstance(i, int) and 2 * U * i + g == 0):
                        sums(i, g - 1)
                    if n == 0 and isinstance(i, int) and u < 3:
                        value_block(u + 1)
                    if u == 0 and n + 2 < NT:
                        variance(i, c + 2)
                    if u == 1 and n + 1 < NT:
                        query_low(i, c + 1)
                    if u == 2 and n >= 2:
                        add_output(i, c - 2)
                    if u == 2 and n + 2 < NT:
                        normalise(i, c + 2)
                return link.n - start

            per_pair = 2 * (2 * U) + 2 * 2
            body(0)
            with vec.Fori(1, NT // 2 - 1) as i:
                assert body(i) == per_pair
            link.reg, link.n = 0, link.n + (NT // 2 - 3) * per_pair
            body(NT // 2 - 1)
            end = NT // 2
            sums(end, -1)
            add_output(end, -2)
            add_output(end, -1)

        @block.tensor
        def _(pe):
            def transpose_x(i, n):
                upto(pe, xn_ready, i, 2, n + 1)
                for k in range(KD):
                    for b in range(B):
                        ins = pe.transpose(psX[:, k, b * P:(b + 1) * P], xn[:, b, k * P:(k + 1) * P], ident[:])
                ins.then_inc(xT_ps, 1)

            def query(i, n):
                for m in range(KD):
                    for k in range(KD):
                        ins = pe.matmul(psQ[:, m], wq[:, k, m * P:(m + 1) * P], xnT[:, k],
                                        start=(k == 0), stop=(k == KD - 1))
                ins.then_inc(q_ps, 1)

            def transpose_p(i, g):
                if isinstance(i, int) and i == g == 0:
                    pe.wait_ge(vblk_ready, U)
                upto(pe, pn_ready, i, 2 * U, g + 1)
                upto(pe, pT_sb, i, 2 * U, g)
                for c in range(VC):
                    ins = pe.transpose(wide(psT)[:, c * P:(c + 1) * P], pr[:, g % U, c * VR:(c + 1) * VR], ident[:])
                ins.then_inc(pT_ps, 1)

            def values(i, n, m):
                upto(pe, pT_sb, i, 2 * U, (n + 1) * U - (KD - 1 - m))
                for b in range(B):
                    for c in range(VC):
                        ins = pe.matmul(psQ[:, m, b * P:(b + 1) * P], vblk[:, b, m, c, :],
                                        pT[:, n % 2, m, c, b * P:(b + 1) * P], start=(c == 0), stop=(c == VC - 1))
                if m == KD - 1:
                    ins.then_inc(h_ps, 1)

            def output(i, n):
                for b in range(B):
                    for m in range(KD):
                        ins = pe.matmul(psX[:, b], hT[:, m, b * P:(b + 1) * P], wo[:, m, :],
                                        start=(m == 0), stop=(m == KD - 1))
                ins.then_inc(o_ps, 1)

            pe.wait_ge(c_in, 64)
            for m in range(KD):
                for a in range(2):
                    for k in range(KD):
                        ins = pe.matmul(psS[m][:, a, 0:B * L].rearrange("p (b l) -> p b l", b=B), wk[:, k, m, a, :],
                                        ctxT[:, :, k, :], start=(k == 0), stop=(k == KD - 1))
            ins.then_inc(k_ps, 1)
            pe.wait_ge(v_in, 32)
            for b in range(B):
                for k in range(KD):
                    ins = pe.matmul(psT[0:L, 0, b * D:(b + 1) * D], ctxT[:, b, k, :], wv[:, k, :],
                                    start=(k == 0), stop=(k == KD - 1))
            ins.then_inc(v_ps, 1)
            pe.wait_ge(ident_ready, 1)
            transpose_x(0, 0)
            pe.wait_ge(x_read, 1)
            pe.wait_ge(w_in, 64)
            query(0, 0)
            pe.wait_ge(consts, 1)
            pe.wait_ge(v_ready, 1)

            def repeat_values(i):
                b, m = divmod(i, KD)
                if i:
                    pe.wait_ge(vblk_ready, i)
                for c in range(VC):
                    ins = pe.matmul(wide(psT)[:, c * P:(c + 1) * P],
                                    sel[:, c * VR:(c + 1) * VR], v_sb[:, b, m * P:(m + 1) * P], start=True, stop=True)
                ins.then_inc(vrep_ps, 1)

            repeat_values(0)
            transpose_x(0, 1)

            def body(i):
                for g in range(2 * U):
                    c, u = divmod(g, U)
                    b, m = divmod(u, KD)
                    n = 2 * i + c if isinstance(i, int) else 2
                    if n == 0 and isinstance(i, int) and u < 2:
                        pe.wait_ge(kh_ready, (2, U + 1)[u])
                        pe.wait_ge(kl_ready, (2, U - 1)[u])
                    if u == 0:
                        upto(pe, q_lo, i, 2, c + 1)
                    upto(pe, sub_done, i, 2 * U, g - 1)
                    for a in range(2):
                        pe.matmul(psS[m][:, a, 0:GH * L], fill[:], drop[:, b], start=True, stop=False)
                        for part in (kh, kl):
                            ins = pe.matmul(psS[m][:, a, 0:GH * L], qs[c][:, a, m, b * P:(b + 1) * P],
                                            part[:, m, a, b], start=False, stop=(part is kl))
                    ins.then_inc(s_ps, 1)
                    if not (isinstance(i, int) and 2 * U * i + g < LAG):
                        transpose_p(i, g - LAG)
                    if n == 0 and isinstance(i, int) and u < 3:
                        repeat_values(u + 1)
                    if u == 0 and n + 1 < NT:
                        pe.wait_ge(x_read, reads(i * 2 + c))
                        upto(pe, h_sb, i, 2, c - 1)
                        query(i, c + 1)
                    if u == 1 and n >= 2:
                        pe.wait_ge(x_read, reads(i * 2 + c))
                        upto(pe, h_sb, i, 2, c - 1)
                        output(i, c - 2)
                    if u == 2 and n >= 1:
                        upto(pe, q_lo, i, 2, c + 2 if n + 1 < NT else c + 1)
                        upto(pe, h_sb, i, 2, c - 1)
                        values(i, c - 1, 0)
                    if u == 3 and n + 2 < NT:
                        pe.wait_ge(x_read, reads(i * 2 + c) + (1 if n >= 2 else 0))
                        transpose_x(i, c + 2)
                    if u == 3 and n >= 1:
                        values(i, c - 1, 1)

            iterations(pe, body)
            end = NT // 2
            transpose_p(end, -3)
            pe.wait_ge(x_read, reads(NT))
            pe.wait_ge(h_sb, NT - 1)
            output(end, -2)
            transpose_p(end, -2)
            values(end, -1, 0)
            transpose_p(end, -1)
            values(end, -1, 1)
            pe.wait_ge(h_sb, NT)
            pe.wait_ge(x_read, reads(NT) + 1)
            output(end, -1)


def gate_and_project(nc, top, t, io):
    with ExitStack() as ctx:
        def sb(name, shape, dt=F32):
            return ctx.enter_context(nc.sbuf_tensor(name, shape, dt))

        def sem(name):
            return top.enter_context(nc.semaphore(name))

        x_all, ident, xnT, v_all = t["x_all"], t["ident"], t["xnT"], t["v_all"]
        whead, bqk, bv = t["whead"], t["bqk"], t["bv"]
        NI = B * NA
        head_col = sb("g_head_col", [1, NI], I32)
        bo = sb("g_bo", [P, D])
        bqk_all, bv_all = sb("g_bqk_all", [P, H2]), sb("g_bv_all", [P, H2])
        one, onehot = sb("g_one", [1, P]), sb("g_onehot", [1, NI, H2])
        bsel = sb("g_bsel", [P, 2, NI, H2])
        stats, mv = sb("g_stats", [P, CH, 6]), sb("g_mv", [P, T, 2])
        rstd, mhalf = sb("g_rstd", [P, T]), sb("g_mhalf", [P, CH])
        xn = sb("g_xn", [P, 2, CH, D])
        part = sb("g_part", [P, KD, NC])
        mean = sb("g_mean", [P, KD, B])
        wr, br = sb("g_wr", [P, KD, H2]), sb("g_br", [1, H2])
        dist, e, cand, rank, act_h, slot_of, weighted = (sb(f"g_{n}", [1, B, H2]) for n in
                                                         ("dist", "e", "cand", "rank", "acth", "slot", "wtd"))
        top1, tot = sb("g_top1", [1, B]), sb("g_tot", [1, B])
        above, same = sb("g_above", [1, B, H2, H2]), sb("g_same", [1, B, H2, H2])
        lower = sb("g_lower", [1, H2, H2])
        numi, num = sb("g_numi", [1, H2], I32), sb("g_num", [1, H2])
        pick = sb("g_pick", [1, B, NA, H2])
        col = sb("g_col", [1, NI])
        psX = [ctx.enter_context(nc.psum_tensor(f"g_psX{m}", [P, KD, CW], F32)) for m in range(2)]
        psV = [ctx.enter_context(nc.psum_tensor(f"g_psV{m}", [P, 512], F32)) for m in range(2)]
        psG = ctx.enter_context(nc.psum_tensor("g_psG", [1, 512], F32))
        psB = ctx.enter_context(nc.psum_tensor("g_psB", [P, 512], F32))
        w_in, dve, pool_sem = sem("g_w_in"), sem("g_dve"), sem("g_pool")
        consts, var_ready, rstd_ready, xn_ready = (sem(f"g_{n}") for n in ("consts", "var", "rstd_s", "xn_s"))
        xT_ps, xT_sb, mean_ready, logit_ps = (sem(f"g_{n}") for n in ("xT_ps", "xT_sb", "mean_s", "logit"))
        shifted, exp_done, col_ready, v_ps, v_sb = (sem(f"g_{n}") for n in ("shift", "exp", "col_s", "v_ps", "v_sb"))
        vpad, bias_in, bo_in, onehot_ready, onehot_ps, bo_added = (sem(f"g_{n}") for n in (
            "vpad", "bias_in", "bo_in", "onehot_s", "onehot_ps", "bo_added"))
        w_head = [sem(f"g_w_head{b}") for b in range(B)]
        block = ctx.enter_context(nc.Block())

        def fetch_heads(eng, par):
            eng.wait_ge(col_ready, 1)
            for i in range(par, NI, 2):
                r = eng.value_load(head_col[0:1, i:i + 1], min_val=0, max_val=H2 - 1)
                eng.dma_start(whead[:, i], io["f_w"][:, :, bass.ds(r, 1), :]
                              .rearrange("p k a c -> p k (a c)")).then_inc(w_head[i // NA], 16)

        @block.sync
        def _(sp):
            sp.dma_start(wr[:], io["f_wr"]).then_inc(w_in, 16)
            sp.dma_start(br[:], io["f_br"]).then_inc(w_in, 16)
            sp.dma_start(bqk_all[:], io["f_bqk"]).then_inc(bias_in, 16)
            sp.dma_start(bv_all[0:HD2], io["f_bv"]).then_inc(bias_in, 16)
            sp.dma_start(bo[:], io["f_bo"]).then_inc(bo_in, 16)
            fetch_heads(sp, 0)

        @block.gpsimd
        def _(pool):
            link = Link(pool, pool_sem)
            pool.memset(mhalf[:], -0.5)
            pool.memset(v_all[:, NI], 0.0)
            pool.memset(whead[:, NI], 0.0)
            pool.memset(bqk[:, NI:], 0.0)
            pool.memset(bv[:, NI:], 0.0)
            pool.memset(one[:], 1.0).then_inc(vpad, 1)
            pool.iota(numi[:], pattern=[[1, H2]], base=0, channel_multiplier=0)
            link(pool.memset(lower[:], 1.0))
            pool.affine_select(out=lower[:], in_=lower[:], compare_op=ALU.is_gt, fill=0.0, base=0,
                               pattern=[[1, H2], [-1, H2]], channel_multiplier=0).then_inc(consts, 1)
            pool.wait_ge(consts, 1)
            for n in range(NC):
                pool.wait_ge(var_ready, n + 1)
                pool.tensor_tensor(rstd[:, n * CH:(n + 1) * CH], rstd[:, n * CH:(n + 1) * CH], mhalf[:],
                                   ALU.pow).then_inc(rstd_ready, 1)
            pool.wait_ge(bo_in, 16)
            for n in range(NC):
                pool.wait_ge(xn_ready, n + 1)
                xc = x_all[:, n * CH:(n + 1) * CH, 0:D]
                pool.tensor_tensor(xc, xc, bo[:].unsqueeze(1).to_broadcast([P, CH, D]), ALU.add).then_inc(bo_added, 1)

        @block.scalar
        def _(act):
            with act.Fori(0, NC // 2) as h:
                for par in range(2):
                    n = h * 2 + par
                    act.wait_ge(xT_ps, n + 1)
                    for k in range(KD):
                        act.activation(xnT[:, k, bass.ds(n * CW, CW)], psX[par][:, k], ACT.Identity,
                                       accum_out=part[:, k, bass.ds(n, 1)]).then_inc(xT_sb, 1)
            act.wait_ge(shifted, 1)
            act.activation(e[:], e[:], ACT.Exp).then_inc(exp_done, 1)
            fetch_heads(act, 1)
            for i in range(T):
                b, kt = divmod(i, T // B)
                act.wait_ge(v_ps, i + 1)
                act.copy(v_all[:, b * NA:(b + 1) * NA, kt, :],
                         psV[i % 2][:, 0:NA * HD2].rearrange("p (h d) -> p h d", h=NA)).then_inc(v_sb, 1)

        @block.vector
        def _(vec):
            link = Link(vec, dve)
            vec.memset(bv_all[HD2:P], 0.0)
            for n in range(NC + 1):
                if n < NC:
                    link(layernorm_stats(vec, link, [x_all[:, n * CH + j, 0:D] for j in range(CH)], stats,
                                         mv[:, n * CH:(n + 1) * CH]))
                    vec.tensor_scalar(rstd[:, n * CH:(n + 1) * CH], mv[:, n * CH:(n + 1) * CH, 1], EPS, None,
                                      ALU.add).then_inc(var_ready, 1)
                if n >= 1:
                    vec.wait_ge(rstd_ready, n)
                    if n >= 3:
                        vec.wait_ge(xT_ps, n - 2)
                    for j in range((n - 1) * CH, n * CH):
                        ins = vec.tensor_scalar(xn[:, (n - 1) % 2, j % CH], x_all[:, j, 0:D], mv[:, j, 0:1],
                                                rstd[:, j:j + 1], ALU.subtract, ALU.mult)
                    ins.then_inc(xn_ready, 1)
            vec.wait_ge(xT_sb, NC * KD)
            link(vec.tensor_reduce(mean[:], part[:].rearrange("p k (b c) -> p k b c", b=B), AX.X, ALU.add))
            vec.tensor_scalar(mean[:], mean[:], 1.0 / S, None, ALU.mult).then_inc(mean_ready, 1)
            vec.wait_ge(w_in, 32)
            vec.wait_ge(logit_ps, 1)
            link(vec.tensor_tensor(dist[:], psG[0:1, 0:B * H2].rearrange("p (b h) -> p b h", b=B),
                                   br[:].unsqueeze(1).to_broadcast([1, B, H2]), ALU.add))
            link(vec.tensor_reduce(top1[:], dist[:], AX.X, ALU.max))
            vec.tensor_tensor(e[:], dist[:], top1[:].unsqueeze(2).to_broadcast([1, B, H2]),
                              ALU.subtract).then_inc(shifted, 1)
            vec.wait_ge(exp_done, 1)
            link(vec.tensor_reduce(tot[:], e[:], AX.X, ALU.add))
            link(vec.reciprocal(tot[:], tot[:]))
            link(vec.tensor_tensor(dist[:], e[:], tot[:].unsqueeze(2).to_broadcast([1, B, H2]), ALU.mult))
            full = [1, B, H2, H2]
            other, own = dist[:].unsqueeze(2).to_broadcast(full), dist[:].unsqueeze(3).to_broadcast(full)
            vec.tensor_tensor(above[:], other, own, ALU.is_gt)
            link(vec.tensor_tensor(same[:], other, own, ALU.is_equal))
            vec.wait_ge(consts, 1)
            low = lower[:].unsqueeze(1).to_broadcast(full)
            link(vec.tensor_tensor(same[:], same[:], low, ALU.mult))
            link(vec.tensor_tensor(above[:], above[:], same[:], ALU.add))
            link(vec.tensor_reduce(rank[:], above[:], AX.X, ALU.add))
            link(vec.tensor_scalar(act_h[:], rank[:], NA - 0.5, None, ALU.is_lt))
            link(vec.tensor_tensor(same[:], act_h[:].unsqueeze(2).to_broadcast(full), low, ALU.mult))
            link(vec.tensor_reduce(slot_of[:], same[:], AX.X, ALU.add))
            link(vec.tensor_copy(num[:], numi[:]))
            link(vec.tensor_tensor(weighted[:], act_h[:], num[:].unsqueeze(1).to_broadcast([1, B, H2]), ALU.mult))
            part_s = [1, B, NA, H2]
            link(vec.tensor_tensor(pick[:], slot_of[:].unsqueeze(2).to_broadcast(part_s),
                                   num[:, 0:NA].unsqueeze(1).unsqueeze(3).to_broadcast(part_s), ALU.is_equal))
            link(vec.tensor_tensor(pick[:], pick[:], weighted[:].unsqueeze(2).to_broadcast(part_s), ALU.mult))
            link(vec.tensor_reduce(col[:].rearrange("p (b s) -> p b s", b=B), pick[:], AX.X, ALU.add))
            vec.tensor_copy(head_col[:], col[:]).then_inc(col_ready, 1)
            vec.tensor_tensor(onehot[:], num[:].unsqueeze(1).to_broadcast([1, NI, H2]),
                              col[:].unsqueeze(2).to_broadcast([1, NI, H2]), ALU.is_equal).then_inc(onehot_ready, 1)
            vec.wait_ge(bias_in, 32)
            vec.wait_ge(vpad, 1)
            vec.wait_ge(onehot_ps, 1)
            for x, every in enumerate((bqk_all, bv_all)):
                ins = vec.tensor_tensor(bsel[:, x], psB[:, 0:NI * H2].rearrange("p (i h) -> p i h", i=NI),
                                        every[:].unsqueeze(1).to_broadcast([P, NI, H2]), ALU.mult)
            link(ins)
            for x, chosen in enumerate((bv, bqk)):
                ins = vec.tensor_reduce(chosen[:, 0:NI], bsel[:, 1 - x], AX.X, ALU.add)
            link(ins)
            vec.tensor_scalar(bqk[0:HD2], bqk[0:HD2], HD2 ** -0.5, None, ALU.mult)

        @block.tensor
        def _(pe):
            with pe.Fori(0, NC // 2) as h:
                for par in range(2):
                    n = h * 2 + par
                    pe.wait_ge(xn_ready, n + 1)
                    pe.wait_ge(xT_sb, h * 2 * KD)
                    for k in range(KD):
                        for j in range(CH):
                            ins = pe.transpose(psX[par][:, k, j * P:(j + 1) * P], xn[:, par, j, k * P:(k + 1) * P],
                                               ident[:])
                    ins.then_inc(xT_ps, 1)
            pe.wait_ge(mean_ready, 1)
            pe.wait_ge(w_in, 32)
            for b in range(B):
                for k in range(KD):
                    ins = pe.matmul(psG[0:1, b * H2:(b + 1) * H2], mean[:, k, b:b + 1], wr[:, k, :],
                                    start=(k == 0), stop=(k == KD - 1))
            ins.then_inc(logit_ps, 1)
            pe.wait_ge(vpad, 1)
            pe.wait_ge(onehot_ready, 1)
            pe.matmul(psB[:, 0:NI * H2], one[:], onehot[:].rearrange("p i h -> p (i h)"), start=True,
                      stop=True).then_inc(onehot_ps, 1)
            for i in range(T):
                b = i // (T // B)
                if i % (T // B) == 0:
                    pe.wait_ge(w_head[b], 16 * NA)
                if i >= 2:
                    pe.wait_ge(v_sb, i - 1)
                for k in range(KD):
                    ins = pe.matmul(psV[i % 2][:, 0:NA * HD2].rearrange("p (s d) -> p s d", s=NA), xnT[:, k, i * P:(i + 1) * P],
                                    whead[:, b * NA:(b + 1) * NA, k, 2 * HD2:3 * HD2],
                                    start=(k == 0), stop=(k == KD - 1))
                ins.then_inc(v_ps, 1)


def gated_attention(nc, top, t, io):
    with ExitStack() as ctx:
        def sb(name, shape, dt=F32):
            return ctx.enter_context(nc.sbuf_tensor(name, shape, dt))

        def sem(name):
            return top.enter_context(nc.semaphore(name))

        x_all, ident, xnT, v_all = t["x_all"], t["ident"], t["xnT"], t["v_all"]
        whead, bqk, bv = t["whead"], t["bqk"], t["bv"]
        NI = B * NA
        NQ = S // P
        KT = S // P
        HK = KT // 2
        QP = 2
        SW = 2 * NQ
        GW = SW // QP
        LAG = 2
        wqk = [sb(f"h_wqk{i}", [P, KD, P]) for i in range(2)]
        qs = [sb(f"h_qs{i}", [P, S], F32R) for i in range(2)]
        kh = [sb(f"h_kh{i}", [P, S], F32R) for i in range(2)]
        kl = [sb(f"h_kl{i}", [P, S], F32R) for i in range(2)]
        vs = [sb(f"h_vs{i}", [P, KT, 2, HD2], F32R) for i in range(2)]
        pr = sb("h_p", [P, 4, S])
        nmx, sm, rs = sb("h_nmx", [P, SW]), sb("h_sm", [P, SW]), sb("h_rs", [P, SW])
        pTh = [sb(f"h_pTh{i}", [P, KT, QP * P], F32R) for i in range(2)]
        pTl = [sb(f"h_pTl{i}", [P, KT, QP * P], F32R) for i in range(2)]
        oT = sb("h_oT", [P, NI * S])
        wo = sb("h_wo", [P, NA, D])
        psS = [ctx.enter_context(nc.psum_tensor(f"h_psS{m}", [P, S], F32)) for m in range(2)]
        psT = [ctx.enter_context(nc.psum_tensor(f"h_psT{m}", [P, HK, P], F32)) for m in range(2)]
        psP = ctx.enter_context(nc.psum_tensor("h_psP", [P, 512], F32))
        psO = ctx.enter_context(nc.psum_tensor("h_psO", [P, 512], F32))

        names = ("w_in", "scaled", "qk_ps", "qk_hi", "qk_lo", "vh_ready",
                 "v_ready", "s_ps", "max_ready", "exp_done", "rs_ready", "pn_ready", "pT_ps", "pT_hi", "pT_lo",
                 "o_ps", "o_sb", "y_ps", "y_sb")
        (w_in, scaled, qk_ps, qk_hi, qk_lo, vh_ready, v_ready, s_ps, max_ready,
         exp_done, rs_ready, pn_ready, pT_ps, pT_hi, pT_lo, o_ps, o_sb, y_ps, y_sb) = (
             sem("h_" + n) for n in names)

        def upto(eng, s, n, per, c, held=None):
            count = n * per + c
            if not isinstance(n, int):
                count = eng.to_reg(count)
            if held is not None and not isinstance(n, int):
                eng.wait_ge(held, 1)
            if not isinstance(n, int) or count > 0:
                eng.wait_ge(s, count)

        def iterations(eng, body):
            body(0)
            with eng.Fori(1, NI // 2) as n:
                body(n)

        block = ctx.enter_context(nc.Block())


        @block.sync
        def _(sp):
            sp.dma_start(wo[0:HD2], io["f_wo"]).then_inc(w_in, 16)
            sp.dma_start(wo[HD2:P], io["f_wo"]).then_inc(w_in, 16)

        @block.gpsimd
        def _(pool):
            def body(n):
                for c in range(SW):
                    i, q = divmod(c, NQ)
                    upto(pool, rs_ready, n, SW, c + 1, held=scaled)
                    pool.tensor_scalar(pr[:, c % 4], pr[:, c % 4], rs[:, c:c + 1], 0.0, ALU.mult,
                                       ALU.add).then_inc(pn_ready, 1)

            iterations(pool, body)

        @block.scalar
        def _(act):
            def scale_q(n, c, par):
                upto(act, qk_ps, n, 4, 2 * c - 2, held=scaled)
                w = whead[:, 2 * n + c] if isinstance(n, int) else \
                    whead[:, bass.ds(n * 2 + c, 1)].rearrange("p a k c -> p (a k) c")
                act.mul(wqk[par][:, :, 0:HD2], w[:, :, 0:HD2], HD2 ** -0.5)
                act.copy(wqk[par][:, :, HD2:P], w[:, :, HD2:P]).then_inc(scaled, 1)

            def project(n, c, par, ch, ps=psP):
                upto(act, qk_ps, n, 4, 2 * c + ch + 1, held=qk_ps)
                upto(act, s_ps, n, SW, NQ * (c - 1))
                cols = slice(ch * CW, (ch + 1) * CW)
                bias = [bqk[h, bass.ds(n * 2 + c, 1)] for h in (slice(0, HD2), slice(HD2, P))]
                act.activation(qs[par][0:HD2, cols], ps[0:HD2], ACT.Identity, bias=bias[0], scale=1.0)
                act.activation(kh[par][HD2:P, cols], ps[HD2:P], ACT.Identity, bias=bias[1], scale=1.0)
                act.activation(kh[par][0:HD2, cols], ps[HD2:P], ACT.Identity, bias=bias[1],
                               scale=1.0).then_inc(qk_hi, 1)

            def split_v(n, c, par):
                upto(act, o_ps, n, GW, (c - 1) * NQ // QP, held=qk_ps)
                v = v_all[:, 2 * n + c] if isinstance(n, int) else \
                    v_all[:, bass.ds(n * 2 + c, 1)].rearrange("p a k d -> p (a k) d")
                act.copy(vs[par][:, :, 0, :], v).then_inc(vh_ready, 1)

            def high(n, c):
                for hf in range(2):
                    upto(act, pT_ps, n, 2 * SW, 2 * c + hf + 1)
                    upto(act, o_ps, n, GW, c // QP - 1)
                    act.copy(pTh[c // QP % 2][:, hf * HK:(hf + 1) * HK, c % QP * P:(c % QP + 1) * P],
                             psT[hf][:]).then_inc(pT_hi, 1)

            def output(n, g):
                upto(act, o_ps, n, GW, g + 1)
                act.activation(oT[:, bass.ds(n * (GW * QP * P) + g * QP * P, QP * P)], psO[:, 0:QP * P],
                               ACT.Identity, bias=bv[:, bass.ds(n * 2 + g * QP // NQ, 1)], scale=1.0).then_inc(o_sb, 1)

            scale_q(0, 0, 0)
            project(0, 0, 0, 0)
            project(0, 0, 0, 1, psO)
            split_v(0, 0, 0)

            def body(n):
                for c in range(SW):
                    i, q = divmod(c, NQ)
                    if q == 0:
                        scale_q(n, i + 1, (i + 1) % 2)
                    if not (isinstance(n, int) and c < LAG):
                        high(n, c - LAG)
                    upto(act, max_ready, n, SW, c + 1)
                    upto(act, pT_ps, n, 2 * SW, 2 * (c - 3))
                    act.activation(pr[:, c % 4], psS[c % 2][:], ACT.Exp, bias=nmx[:, c:c + 1], scale=1.0,
                                   accum_out=sm[:, c:c + 1]).then_inc(exp_done, 1)
                    if c % 2 == 1 and not (isinstance(n, int) and c < 5):
                        output(n, (c - 5) // 2)
                    if q in (2, 5):
                        project(n, i + 1, (i + 1) % 2, q // 3)
                    if q == 3:
                        split_v(n, i + 1, (i + 1) % 2)

            iterations(act, body)
            last = NI // 2
            high(last, -2)
            high(last, -1)
            output(last, -2)
            output(last, -1)

        @block.vector
        def _(vec):
            def project(n, c, par, ch, ps=psP):
                upto(vec, qk_hi, n, 4, 2 * c + ch + 1)
                cols = slice(ch * CW, (ch + 1) * CW)
                bias = [bqk[h, bass.ds(n * 2 + c, 1)] for h in (slice(0, HD2), slice(HD2, P))]
                vec.scalar_tensor_tensor(qs[par][HD2:P, cols], ps[0:HD2], bias[0], qs[par][0:HD2, cols],
                                         ALU.add, ALU.subtract)
                vec.scalar_tensor_tensor(kl[par][HD2:P, cols], ps[HD2:P], bias[1], kh[par][HD2:P, cols],
                                         ALU.add, ALU.subtract)
                vec.scalar_tensor_tensor(kl[par][0:HD2, cols], ps[HD2:P], bias[1], kh[par][HD2:P, cols],
                                         ALU.add, ALU.subtract).then_inc(qk_lo, 1)

            def split_v(n, c, par):
                upto(vec, vh_ready, n, 2, c + 1)
                v = v_all[:, 2 * n + c] if isinstance(n, int) else \
                    v_all[:, bass.ds(n * 2 + c, 1)].rearrange("p a k d -> p (a k) d")
                vec.tensor_tensor(vs[par][:, :, 1, :], v, vs[par][:, :, 0, :], ALU.subtract).then_inc(v_ready, 1)

            def low(n, c):
                for hf in range(2):
                    upto(vec, pT_hi, n, 2 * SW, 2 * c + hf + 1)
                    part = (slice(None), slice(hf * HK, (hf + 1) * HK), slice(c % QP * P, (c % QP + 1) * P))
                    vec.tensor_tensor(pTl[c // QP % 2][part], psT[hf][:], pTh[c // QP % 2][part],
                                      ALU.subtract).then_inc(pT_lo, 1)

            def invert(n, c):
                upto(vec, exp_done, n, SW, c + 1)
                vec.reciprocal(rs[:, c % SW:c % SW + 1], sm[:, c % SW:c % SW + 1]).then_inc(rs_ready, 1)

            project(0, 0, 0, 0)
            project(0, 0, 0, 1, psO)
            split_v(0, 0, 0)

            def body(n):
                for c in range(SW):
                    i, q = divmod(c, NQ)
                    upto(vec, s_ps, n, SW, c + 1)
                    vec.tensor_reduce(nmx[:, c:c + 1], psS[c % 2][:], AX.X, ALU.max, negate=True).then_inc(max_ready, 1)
                    if not (isinstance(n, int) and c == 0):
                        invert(n, c - 1)
                    if not (isinstance(n, int) and c < LAG):
                        low(n, c - LAG)
                    if q in (3, 6):
                        project(n, i + 1, (i + 1) % 2, q // 3 - 1)
                    if q == 5:
                        split_v(n, i + 1, (i + 1) % 2)

            iterations(vec, body)
            invert(NI // 2, -1)
            low(NI // 2, -2)
            low(NI // 2, -1)
            for r in range(T // 2):
                vec.wait_ge(y_ps, r + 1)
                xc = x_all[:, 2 * r:2 * r + 2, 0:D]
                vec.tensor_tensor(xc, (psP, psO)[r % 2][:].rearrange("p (a d) -> p a d", a=2), xc,
                                  ALU.add).then_inc(y_sb, 1)

        @block.tensor
        def _(pe):
            def project(n, c, par, ch, ps=psP):
                upto(pe, scaled, n, 2, c + 1)
                if ps is psP:
                    upto(pe, qk_hi, n, 4, 2 * c + ch)
                    upto(pe, qk_lo, n, 4, 2 * c + ch)
                batch = (2 * n + c) // NA if isinstance(n, int) else ((n * 2 + c) // NA) % B
                for k in range(KD):
                    ins = pe.matmul(ps[:], wqk[par][:, k, :], xnT[:, k, bass.ds(batch * S + ch * CW, CW)],
                                    start=(k == 0), stop=(k == KD - 1))
                ins.then_inc(qk_ps, 1)

            def transposes(n, c):
                for hf in range(2):
                    upto(pe, pn_ready, n, SW, c + 1)
                    upto(pe, pT_lo, n, 2 * SW, 2 * c + hf - 1)
                    for k in range(HK):
                        ins = pe.transpose(psT[hf][:, k], pr[:, c % 4, (hf * HK + k) * P:(hf * HK + k + 1) * P], ident[:])
                    ins.then_inc(pT_ps, 1)

            def values(n, g, hf):
                par = g * QP // NQ % 2
                if hf == 0:
                    upto(pe, pT_lo, n, 2 * SW, 2 * QP * (g + 1))
                    upto(pe, v_ready, n, 2, g * QP // NQ + 1)
                    upto(pe, o_sb, n, GW, g)
                for k in range(hf * HK, (hf + 1) * HK):
                    for part in (pTh, pTl):
                        ins = pe.matmul(psO[:, 0:QP * P], vs[par][:, k], part[g % 2][:, k],
                                        start=(k == 0 and part is pTh), stop=(k == KT - 1 and part is pTl))
                if hf == 1:
                    ins.then_inc(o_ps, 1)

            project(0, 0, 0, 0)
            project(0, 0, 0, 1, psO)

            def body(n):
                for c in range(SW):
                    i, q = divmod(c, NQ)
                    if q == 0:
                        upto(pe, qk_lo, n, 4, 2 * i + 2)
                    upto(pe, exp_done, n, SW, c - 1)
                    for hf in range(2):
                        for part in (kh, kl):
                            ins = pe.matmul(psS[c % 2][:, hf * CW:(hf + 1) * CW], qs[i][:, q * P:(q + 1) * P],
                                            part[i][:, hf * CW:(hf + 1) * CW], start=(part is kh), stop=(part is kl))
                    ins.then_inc(s_ps, 1)
                    if not (isinstance(n, int) and c < LAG):
                        transposes(n, c - LAG)
                    if not (isinstance(n, int) and c < 4):
                        values(n, c // 2 - 2, c % 2)
                    if q in (1, 4):
                        project(n, i + 1, (i + 1) % 2, q // 3)

            iterations(pe, body)
            last = NI // 2
            transposes(last, -2)
            values(last, -2, 0)
            transposes(last, -1)
            values(last, -2, 1)
            values(last, -1, 0)
            values(last, -1, 1)
            pe.wait_ge(w_in, 32)
            pe.wait_ge(o_sb, NI * NQ // QP)
            pe.wait_ge(qk_hi, 2 * (NI + 1))
            pe.wait_ge(qk_lo, 2 * (NI + 1))
            for r in range(T // 2):
                if r >= 2:
                    pe.wait_ge(y_sb, r - 1)
                for j in range(2):
                    b, q = divmod(2 * r + j, NQ)
                    for s in range(NA):
                        ins = pe.matmul((psP, psO)[r % 2][:, j * D:(j + 1) * D],
                                        oT[:, (b * NA + s) * S + q * P:(b * NA + s) * S + (q + 1) * P], wo[:, s, :],
                                        start=(s == 0), stop=(s == NA - 1))
                ins.then_inc(y_ps, 1)


def context_mlp(nc, top, t, io):
    with ExitStack() as ctx:
        def sb(name, shape, dt=F32):
            return ctx.enter_context(nc.sbuf_tensor(name, shape, dt))

        def sem(name):
            return top.enter_context(nc.semaphore(name))

        x_all, ident, table, slot = t["x_all"], t["ident"], t["table"], t["slot"]
        ctxT, ctxs = sb("c_ctxT", [P, B, KD, L]), sb("c_ctx", [L, B, D])
        wr = sb("c_wr", [P, KD, NE])
        stats = sb("c_stats", [P, 2, CH, 6])
        mv, rstd, mhalf = sb("c_mv", [P, T, 2]), sb("c_rstd", [P, T]), sb("c_mhalf", [P, CH])
        mv4 = sb("c_mv4", [P, T, 2])
        xn, xnT = sb("c_xn", [P, 2, CH, D]), sb("c_xnT", [P, 2, KD, CW])
        sq, inner, th, g = (sb(f"c_{n}", [L, 2, CW]) for n in ("sq", "inner", "th", "g"))
        lg, e, first, oh, rank, base = (sb(f"c_{n}", [P, T, NE]) for n in ("lg", "e", "first", "oh", "rank", "base"))
        scan = sb("c_scan", [P, 2, T, NE])
        best, tot = sb("c_best", [P, T]), sb("c_tot", [P, T])
        low = sb("c_low", [P, T])
        before, ones = sb("c_before", [P, P]), sb("c_ones", [P, P])
        numi, num = sb("c_numi", [P, 32], I32), sb("c_num", [P, 32])
        steps = sb("c_steps", [P, T])
        tok = sb("c_tok", [P, T], I32)
        fits = sb("c_fits", [P, NE, T])
        tiles, ends = sb("c_tiles", [P, NE]), sb("c_ends", [P, 2, NE])
        slotf = sb("c_slotf", [P, T])
        tabf, done_e = sb("c_tabf", [1, TABLE]), sb("c_done_e", [1, TG, NE])
        blank, cleared = sb("c_blank", [P, ROW]), sem("c_cleared")
        w_high = sem("c_w_high")
        psX = ctx.enter_context(nc.psum_tensor("c_psX", [P, KD, CW], F32))
        psH = ctx.enter_context(nc.psum_tensor("c_psH", [L, CW], F32))
        psO = ctx.enter_context(nc.psum_tensor("c_psO", [P, CH, D], F32))
        psR = ctx.enter_context(nc.psum_tensor("c_psR", [P, T, NE], F32))
        psC = ctx.enter_context(nc.psum_tensor("c_psC", [P, 2, T, NE], F32))
        names = ("w_in", "dve", "pool", "consts", "var", "rstd_s", "xn_s", "xT_ps", "xT_sb", "h_ps", "sq_s",
                 "inner_s", "th_s", "g_s", "o_ps", "x_done", "r_ps", "shift", "exp", "oh_s", "count_ps", "slot_s")
        (w_in, dve, pool_sem, consts, var_ready, rstd_ready, xn_ready, xT_ps, xT_sb, h_ps, sq_ready, inner_ready,
         th_ready, g_ready, o_ps, x_done, r_ps, shifted, exp_done, oh_ready, count_ps, slot_ready) = (
             sem("c_" + n) for n in names)
        ORDER = [("mlp", 0)] + [w for n in range(1, NC) for w in (("mlp", n), ("route", n - 1))] + [("route", NC - 1)]
        AT = {w: i for i, w in enumerate(ORDER)}
        block = ctx.enter_context(nc.Block())

        @block.sync
        def _(sp):
            sp.dma_start(ctxT[:], io["ctxT"]).then_inc(w_in, 16)
            sp.dma_start(ctxs[:], io["ctx"]).then_inc(w_in, 16)
            sp.dma_start(wr[:], io["m_wr"]).then_inc(w_in, 16)
            fetch_expert(sp, t, io, 0)
            sp.wait_ge(t["w_in"], 48)
            fetch_expert(sp, t, io, 1)
            sp.wait_ge(cleared, 1)
            sp.dma_start(t["rows"].rearrange("(g p) r -> p g r", p=P),
                         blank[:].unsqueeze(1).to_broadcast([P, TG, ROW])).then_inc(t["rows_cleared"], 16)

        @block.gpsimd
        def _(pool):
            link = Link(pool, pool_sem)
            link(pool.memset(blank[:], 0.0))
            pool.memset(blank[:, D + 3:], float(2 * B * S)).then_inc(cleared, 1)
            pool.memset(mhalf[:], -0.5)
            pool.iota(numi[:], pattern=[[1, 32]], base=0, channel_multiplier=0)
            pool.iota(tok[:], pattern=[[P, T]], base=0, channel_multiplier=1)
            pool.memset(ones[:], 1.0)
            link(pool.memset(before[:], 1.0))
            pool.affine_select(out=before[:], in_=before[:], compare_op=ALU.is_gt, fill=0.0, base=0,
                               pattern=[[1, P]], channel_multiplier=-1).then_inc(consts, 1)
            pool.wait_ge(consts, 1)
            for i, (kind, n) in enumerate([("mlp", n) for n in range(NC)] + [("route", n) for n in range(NC)]):
                pool.wait_ge(var_ready, i + 1)
                pool.tensor_tensor(rstd[:, n * CH:(n + 1) * CH], rstd[:, n * CH:(n + 1) * CH], mhalf[:],
                                   ALU.pow).then_inc(rstd_ready, 1)
                x, q = divmod(i, NC)
                part = slice(q * WE // NC, (q + 1) * WE // NC)
                pool.wait_ge(w_high, x + 1)
                pool.tensor_tensor(t["wl"][:, x, part], t["wst"][:, x, part], t["wh"][:, x, part],
                                   ALU.subtract).then_inc(t[("w_split", "w1_ready", "w_split", "w_ready")[q]], 1)

        @block.scalar
        def _(act):
            for x in range(2):
                act.wait_ge(t["w_in"], 48 * (x + 1))
                act.copy(t["wh"][:, x], t["wst"][:, x]).then_inc(w_high, 1)
            for i, (kind, n) in enumerate(ORDER):
                act.wait_ge(xT_ps, i + 1)
                if i >= 2:
                    act.wait_ge(r_ps if ORDER[i - 2][0] == "route" else h_ps, ORDER[i - 2][1] + 1)
                act.copy(xnT[:, i % 2], psX[:]).then_inc(xT_sb, 1)
                if kind == "mlp":
                    act.wait_ge(h_ps, n + 1)
                    act.activation(sq[:, n % 2], psH[:], ACT.Square).then_inc(sq_ready, 1)
                    act.wait_ge(inner_ready, n + 1)
                    act.activation(th[:, n % 2], inner[:, n % 2], ACT.Tanh, bias=0.0,
                                   scale=0.7978845608028654).then_inc(th_ready, 1)
            act.wait_ge(shifted, 1)
            act.activation(e[:], e[:], ACT.Exp).then_inc(exp_done, 1)

        @block.vector
        def _(vec):
            link = Link(vec, dve)

            def variances(n, mv_, par):
                link(layernorm_stats(vec, link, [x_all[:, n * CH + j, 0:D] for j in range(CH)], stats[:, par],
                                     mv_[:, n * CH:(n + 1) * CH]))
                vec.tensor_scalar(rstd[:, n * CH:(n + 1) * CH], mv_[:, n * CH:(n + 1) * CH, 1], EPS, None,
                                  ALU.add).then_inc(var_ready, 1)

            def normalise(i, n, mv_, count):
                vec.wait_ge(rstd_ready, count)
                if i >= 2:
                    vec.wait_ge(xT_ps, i - 1)
                for j in range(CH):
                    t_ = n * CH + j
                    ins = vec.tensor_scalar(xn[:, i % 2, j], x_all[:, t_, 0:D], mv_[:, t_, 0:1], rstd[:, t_:t_ + 1],
                                            ALU.subtract, ALU.mult)
                ins.then_inc(xn_ready, 1)

            for n in range(NC):
                variances(n, mv, 0)
            normalise(0, 0, mv, 1)
            for i, (kind, n) in enumerate(ORDER):
                if kind == "mlp":
                    if n + 1 < NC:
                        normalise(AT["mlp", n + 1], n + 1, mv, n + 2)
                    p = n % 2
                    vec.wait_ge(sq_ready, n + 1)
                    link(vec.tensor_scalar(inner[:, p], sq[:, p], 0.044715, 1.0, ALU.mult, ALU.add))
                    vec.tensor_tensor(inner[:, p], psH[:], inner[:, p], ALU.mult).then_inc(inner_ready, 1)
                    vec.wait_ge(th_ready, n + 1)
                    vec.scalar_tensor_tensor(g[:, p], th[:, p], 1.0, psH[:], ALU.add, ALU.mult).then_inc(g_ready, 1)
                    vec.wait_ge(o_ps, n + 1)
                    xc = x_all[:, n * CH:(n + 1) * CH, 0:D]
                    vec.scalar_tensor_tensor(xc, psO[:], 0.5, xc, ALU.mult, ALU.add).then_inc(x_done, 1)
                    vec.wait_ge(x_done, n + 1)
                    variances(n, mv4, 1)
                    normalise(AT["route", n], n, mv4, NC + n + 1)
            vec.wait_ge(rstd_ready, 2 * NC)
            vec.wait_ge(consts, 1)
            vec.tensor_copy(x_all[:, :, D], mv4[:, :, 0])
            vec.tensor_copy(x_all[:, :, D + 1], rstd[:])
            vec.tensor_copy(x_all[:, :, D + 3], tok[:])
            link(vec.tensor_copy(num[:], numi[:]))
            vec.wait_ge(r_ps, NC)
            link(vec.tensor_copy(lg[:], psR[:]))
            full = [P, T, NE]
            link(vec.tensor_reduce(best[:], lg[:], AX.X, ALU.max))
            vec.tensor_tensor(e[:], lg[:], best[:].unsqueeze(2).to_broadcast(full), ALU.subtract).then_inc(shifted, 1)
            vec.wait_ge(exp_done, 1)
            link(vec.tensor_reduce(tot[:], e[:], AX.X, ALU.add))
            link(vec.reciprocal(tot[:], tot[:]))
            link(vec.tensor_tensor(e[:], e[:], tot[:].unsqueeze(2).to_broadcast(full), ALU.mult))
            link(vec.tensor_reduce(x_all[:, :, D + 2], e[:], AX.X, ALU.max))
            link(vec.tensor_tensor(first[:], e[:], x_all[:, :, D + 2:D + 3].to_broadcast(full), ALU.is_equal))
            link(vec.tensor_scalar(first[:], first[:], -float(NE), None, ALU.mult))
            link(vec.tensor_tensor(first[:], first[:], num[:, 0:NE].unsqueeze(1).to_broadcast(full), ALU.add))
            link(vec.tensor_reduce(low[:], first[:], AX.X, ALU.min))
            vec.tensor_tensor(oh[:], first[:], low[:].unsqueeze(2).to_broadcast(full), ALU.is_equal).then_inc(oh_ready, 1)
            vec.wait_ge(count_ps, 1)
            vec.tensor_copy(rank[:], psC[:, 0])
            link(vec.tensor_copy(scan[:, 0], psC[:, 1]))
            a = 0
            for d in (1, 2, 4, 8):
                vec.tensor_copy(scan[:, 1 - a, 0:d], scan[:, a, 0:d])
                link(vec.tensor_tensor(scan[:, 1 - a, d:T], scan[:, a, d:T], scan[:, a, 0:T - d], ALU.add))
                a = 1 - a
            vec.tensor_tensor(base[:], psC[:, 1], scan[:, a], ALU.subtract)
            link(vec.tensor_scalar(steps[:], num[:, 0:T], float(P), None, ALU.mult))
            link(vec.tensor_tensor(fits[:], scan[:, a, T - 1].unsqueeze(2).to_broadcast([P, NE, T]),
                                   steps[:].unsqueeze(1).to_broadcast([P, NE, T]), ALU.is_gt))
            link(vec.tensor_reduce(tiles[:], fits[:], AX.X, ALU.add))
            link(vec.tensor_scalar(tiles[:], tiles[:], 1.0, None, ALU.max))
            link(vec.tensor_copy(ends[:, 0], tiles[:]))
            a = 0
            for d in (1, 2, 4):
                vec.tensor_copy(ends[:, 1 - a, 0:d], ends[:, a, 0:d])
                link(vec.tensor_tensor(ends[:, 1 - a, d:NE], ends[:, a, d:NE], ends[:, a, 0:NE - d], ALU.add))
                a = 1 - a
            end = ends[:, a]
            link(vec.tensor_tensor(tiles[:], end, tiles[:], ALU.subtract))
            link(vec.tensor_scalar(tiles[:], tiles[:], float(P), None, ALU.mult))
            link(vec.tensor_tensor(rank[:], rank[:], base[:], ALU.subtract))
            link(vec.tensor_tensor(rank[:], rank[:], tiles[:].unsqueeze(1).to_broadcast(full), ALU.add))
            link(vec.tensor_tensor(rank[:], rank[:], oh[:], ALU.mult))
            link(vec.tensor_reduce(slotf[:], rank[:], AX.X, ALU.add))
            vec.tensor_copy(slot[:], slotf[:]).then_inc(slot_ready, 1)
            link(vec.tensor_tensor(done_e[:], end[0:1].unsqueeze(1).to_broadcast([1, TG, NE]),
                                   num[0:1, 0:TG].unsqueeze(2).to_broadcast([1, TG, NE]), ALU.is_le))
            link(vec.tensor_reduce(tabf[:, 0:TG], done_e[:], AX.X, ALU.add))
            link(vec.tensor_scalar(tabf[:, 0:TG], tabf[:, 0:TG], float(NE - 1), None, ALU.min))
            vec.tensor_scalar(tabf[:, TG:2 * TG], num[0:1, 0:TG], 1.0, end[0:1, NE - 1:NE], ALU.add, ALU.min)
            vec.tensor_copy(tabf[:, 2 * TG:LAST], end[0:1])
            link(vec.tensor_scalar(tabf[:, LAST:], end[0:1, NE - 1:NE], -1.0, None, ALU.add))
            vec.tensor_copy(table[:], tabf[:])

        @block.tensor
        def _(pe):
            pe.wait_ge(w_in, 48)
            pe.wait_ge(consts, 1)
            for i, (kind, n) in enumerate(ORDER):
                pe.wait_ge(xn_ready, i + 1)
                if i >= 1:
                    pe.wait_ge(xT_sb, i)
                for k in range(KD):
                    for j in range(CH):
                        ins = pe.transpose(psX[:, k, j * P:(j + 1) * P], xn[:, i % 2, j, k * P:(k + 1) * P], ident[:])
                ins.then_inc(xT_ps, 1)
                pe.wait_ge(xT_sb, i + 1)
                if kind == "mlp":
                    b = n // (NC // B)
                    if n >= 1:
                        pe.wait_ge(g_ready, n)
                    for k in range(KD):
                        ins = pe.matmul(psH[:], ctxT[:, b, k, :], xnT[:, i % 2, k], start=(k == 0), stop=(k == KD - 1))
                    ins.then_inc(h_ps, 1)
                    pe.wait_ge(g_ready, n + 1)
                    if n >= 1:
                        pe.wait_ge(x_done, n)
                    for j in range(CH):
                        ins = pe.matmul(psO[:, j], g[:, n % 2, j * P:(j + 1) * P], ctxs[:, b], start=True, stop=True)
                    ins.then_inc(o_ps, 1)
                else:
                    for j in range(CH):
                        for k in range(KD):
                            ins = pe.matmul(psR[:, n * CH + j], xnT[:, i % 2, k, j * P:(j + 1) * P], wr[:, k],
                                            start=(k == 0), stop=(k == KD - 1))
                    ins.then_inc(r_ps, 1)
            pe.wait_ge(oh_ready, 1)
            pe.matmul(psC[:, 0], before[:], oh[:], start=True, stop=True)
            pe.matmul(psC[:, 1], ones[:], oh[:], start=True, stop=True).then_inc(count_ps, 1)


def sort_rows(nc, top, t, io):
    scattered = top.enter_context(nc.semaphore("s_scattered"))
    back = [top.enter_context(nc.semaphore(f"s_back{i}")) for i in range(2)]
    t["back"] = back
    with nc.Block() as block:
        @block.gpsimd
        def _(pool):
            pool.wait_ge(t["rows_cleared"], 16)
            for i in range(T):
                pool.indirect_dma_start(out=t["rows"], out_offset=bass.IndirectOffsetOnAxis(
                    ap=t["slot"][:, i:i + 1].bitcast(U32), axis=0), in_=t["x_all"][:, i, :], in_offset=None,
                    bounds_check=TG * P - 1, oob_is_err=False).then_inc(scattered, 16)

        @block.sync
        def _(sp):
            sp.wait_ge(scattered, 16 * T)
            rows = t["rows"].rearrange("(g p) r -> p g r", p=P)
            sp.dma_start(t["xg"][:, 0:2], rows[:, 0:2]).then_inc(back[0], 16)
            sp.dma_start(t["xg"][:, 2:TG], rows[:, 2:TG]).then_inc(back[1], 16)


def experts(nc, top, t, io):
    with ExitStack() as ctx:
        def sb(name, shape, dt=F32):
            return ctx.enter_context(nc.sbuf_tensor(name, shape, dt))

        def sem(name):
            return top.enter_context(nc.semaphore(name))

        ident, table, xg, wst, wh, wl = (t[n] for n in ("ident", "table", "xg", "wst", "wh", "wl"))
        bias = t["bias"]
        xn = sb("e_xn", [P, D])
        xh, xl = sb("e_xh", [P, KD, P], F32R), sb("e_xl", [P, KD, P], F32R)
        h = sb("e_h", [P, 2, 512])
        hh, hl = sb("e_hh", [P, FB, P], F32R), sb("e_hl", [P, FB, P], F32R)
        y = sb("e_y", [P, D])
        tokid = sb("e_tokid", [P, MT], I32)
        psX = ctx.enter_context(nc.psum_tensor("e_psX", [P, KD, P], F32))
        psH = [ctx.enter_context(nc.psum_tensor(f"e_psH{i}", [P, 512], F32)) for i in range(2)]
        psT = [ctx.enter_context(nc.psum_tensor(f"e_psT{i}", [P, FB // 2, P], F32)) for i in range(2)]
        psY = ctx.enter_context(nc.psum_tensor("e_psY", [P, 512], F32))
        names = ("dve", "xn_s", "xT_ps", "xh_s", "xl_s", "h_ps", "h_sb", "hT_ps", "hh_s", "hl_s",
                 "y_ps", "y_s", "y_done", "tok_s", "out_s", "hgone")
        (dve, xn_ready, xT_ps, xh_ready, xl_ready, h_ps, h_sb, hT_ps, hh_ready, hl_ready, y_ps, y_sb,
         y_done, tok_ready, out_done, hgone) = (sem("e_" + n) for n in names)
        w_high = [sem(f"e_w_high{i}") for i in range(2)]
        w_in, w1_ready, w_ready, back = t["w_in"], t["w1_ready"], t["w_ready"], t["back"]
        block = ctx.enter_context(nc.Block())

        def upto(eng, s, n, per, c):
            if not isinstance(n, int):
                eng.wait_ge(s, n * per + c)
            elif per * n + c > 0:
                eng.wait_ge(s, per * n + c)

        def load(eng, at, top_value, least=0):
            return eng.value_load(table[0:1, bass.ds(at, 1)], min_val=least, max_val=top_value)

        def tiles(eng, body):
            body(0)
            with eng.Fori(1, load(eng, TILES, MT, NE)) as g:
                body(g)

        @block.sync
        def _(sp):
            for e in range(2, NE):
                sp.wait_ge(w_in, 48 * e)
                sp.wait_ge(w_ready, e - 1)
                fetch_expert(sp, t, io, e)
            sp.wait_ge(out_done, 16 * MT)

        @block.gpsimd
        def _(pool):
            most = pool.to_reg(B * S - 1)

            def split(g, e, par):
                landed = pool.to_reg(e * 48 + 96)
                pool.wait_ge(y_ps, g)
                pool.wait_ge(w_in, landed)
                for part, cols in enumerate((slice(0, KD * FF), slice(KD * FF, WE))):
                    raw, high, low = (w[:, par, cols] for w in (wst, wh, wl))
                    if part:
                        pool.wait_ge(y_sb, g)
                    pool.tensor_scalar(high, raw, 1.0, 0.0, ALU.mult, ALU.add).then_inc(w_high[part], 1)
                    pool.wait_ge(tok_ready, 1)
                    pool.wait_ge(w_high[part], e)
                    pool.tensor_tensor(low, raw, high, ALU.subtract).then_inc((w1_ready, w_ready)[part], 1)

            for g in range(1, MT + 1):
                if g < MT:
                    e = load(pool, g, NE - 1)
                    with pool.If(e < NE - 1):
                        before = load(pool, g - 1, NE - 1)
                        with pool.If(before < e):
                            e = load(pool, g, NE - 2, 1)
                            for par in range(2):
                                with pool.If(e % 2 == 1 - par):
                                    split(g, e, par)
                through = load(pool, TG + g - 1, MT)
                pool.wait_ge(tok_ready, 1)
                pool.wait_ge(y_done, through)
                pool.indirect_dma_start(out=io["out"], out_offset=bass.IndirectOffsetOnAxis(
                    ap=tokid[:, g - 1:g].bitcast(U32), axis=0), in_=xg[:, g - 1, 0:D], in_offset=None,
                    bounds_check=most, oob_is_err=False).then_inc(out_done, 16)

        @block.scalar
        def _(act):
            def x_high(g):
                upto(act, xT_ps, g, 1, 1)
                upto(act, h_ps, g, 2, 0)
                act.copy(xh[:], psX[:]).then_inc(xh_ready, 1)

            x_high(0)

            def body(g):
                x_high(g + 1)
                for hf in range(2):
                    upto(act, hT_ps, g, 2, hf + 1)
                    upto(act, y_ps, g, 1, 0)
                    act.activation(hh[:, hf * FB // 2:(hf + 1) * FB // 2], psT[hf][:], ACT.Relu).then_inc(hh_ready, 1)

            tiles(act, body)

        @block.vector
        def _(vec):
            link = Link(vec, dve)

            def normalise(g):
                upto(vec, xT_ps, g, 1, 0)
                row = xg[:, bass.ds(g, 1), :].rearrange("p a r -> p (a r)")
                vec.tensor_scalar(xn[:], row[:, 0:D], row[:, D:D + 1], row[:, D + 1:D + 2], ALU.subtract,
                                  ALU.mult).then_inc(xn_ready, 1)

            def x_low(g):
                upto(vec, xh_ready, g, 1, 1)
                vec.tensor_tensor(xl[:], psX[:], xh[:], ALU.subtract).then_inc(xl_ready, 1)

            def finish(g):
                e = load(vec, g, NE - 1)
                upto(vec, y_ps, g, 1, 1)
                row = xg[:, bass.ds(g, 1), :].rearrange("p a r -> p (a r)")
                vec.tensor_tensor(y[:], psY[:, 0:D], bias[:, bass.ds((e % NB) * (FF + D) + FF, D)],
                                  ALU.add).then_inc(y_sb, 1)
                upto(vec, y_sb, g, 1, 1)
                vec.scalar_tensor_tensor(row[:, 0:D], y[:], row[:, D + 2:D + 3], row[:, 0:D], ALU.mult,
                                         ALU.add).then_inc(y_done, 1)

            vec.wait_ge(back[0], 16)
            normalise(0)
            x_low(0)
            normalise(1)
            vec.wait_ge(back[1], 16)
            vec.tensor_copy(tokid[:], xg[:, 0:MT, D + 3]).then_inc(tok_ready, 1)

            def body(g):
                e = load(vec, g, NE - 1)
                for hf in range(2):
                    upto(vec, h_ps, g, 2, hf + 1)
                    upto(vec, hT_ps, g, 2, 0)
                    vec.tensor_tensor(h[:, hf], psH[hf][:], bias[:, bass.ds((e % NB) * (FF + D) + hf * 512, 512)],
                                      ALU.add).then_inc(h_sb, 1)
                if not isinstance(g, int):
                    finish(g - 1)
                x_low(g + 1)
                for hf in range(2):
                    upto(vec, hh_ready, g, 2, hf + 1)
                    part = slice(hf * FB // 2, (hf + 1) * FB // 2)
                    vec.scalar_tensor_tensor(hl[:, part], psT[hf][:], 0.0, hh[:, part], ALU.max,
                                             ALU.subtract).then_inc(hl_ready, 1)
                normalise(g + 2)

            tiles(vec, body)
            finish(load(vec, LAST, MT - 1, NE - 1))

        @block.tensor
        def _(pe):
            def transpose_x(g):
                upto(pe, xn_ready, g, 1, 1)
                upto(pe, xl_ready, g, 1, 0)
                for k in range(KD):
                    ins = pe.transpose(psX[:, k], xn[:, k * P:(k + 1) * P], ident[:])
                ins.then_inc(xT_ps, 1)

            def hidden(g):
                e = load(pe, g, NE - 1)
                pe.wait_ge(w1_ready, e + 1)
                upto(pe, xl_ready, g, 1, 1)
                for hf in range(2):
                    upto(pe, h_sb, g, 2, hf - 1)
                    for k in range(KD):
                        off = (e % 2) * WE + (k * FF + hf * 512)
                        for n, (x_, w_) in enumerate(((xh, wh), (xl, wh), (xh, wl))):
                            ins = pe.matmul(psH[hf][:], x_[:, k], w_[:].rearrange("p a w -> p (a w)")[:, bass.ds(off, 512)],
                                            start=(k == 0 and n == 0), stop=(k == KD - 1 and n == 2))
                    ins.then_inc(h_ps, 1)

            def transpose_h(g):
                for hf in range(2):
                    upto(pe, h_sb, g, 2, hf + 1)
                    upto(pe, hl_ready, g, 2, hf - 1)
                    for k in range(FB // 2):
                        ins = pe.transpose(psT[hf][:, k], h[:, hf, k * P:(k + 1) * P], ident[:])
                    ins.then_inc(hT_ps, 1)

            def output(g):
                e = load(pe, g, NE - 1)
                pe.wait_ge(w_ready, e + 1)
                upto(pe, hl_ready, g, 2, 2)
                upto(pe, y_sb, g, 1, 0)
                for k in range(FB):
                    off = (e % 2) * WE + (KD * FF + k * D)
                    for n, (h_, w_) in enumerate(((hh, wh), (hl, wh), (hh, wl))):
                        ins = pe.matmul(psY[:, 0:D], h_[:, k], w_[:].rearrange("p a w -> p (a w)")[:, bass.ds(off, D)],
                                        start=(k == 0 and n == 0), stop=(k == FB - 1 and n == 2))
                ins.then_inc(y_ps, 1)

            transpose_x(0)

            def body(g):
                hidden(g)
                if not isinstance(g, int):
                    output(g - 1)
                transpose_x(g + 1)
                transpose_h(g)

            tiles(pe, body)
            output(load(pe, LAST, MT - 1, NE - 1))


def fetch_expert(sp, t, io, e):
    sp.dma_start(t["wst"][:, e % 2, 0:KD * FF], io["m_w1"][e]).then_inc(t["w_in"], 16)
    sp.dma_start(t["wst"][:, e % 2, KD * FF:WE], io["m_w2"][e]).then_inc(t["w_in"], 16)
    sp.dma_start(t["bias"][:, e % NB * (FF + D):(e % NB + 1) * (FF + D)], io["m_b"][e]).then_inc(t["w_in"], 16)


def program(nc, io):
    with ExitStack() as top:
        def sb(name, shape, dt=F32):
            return top.enter_context(nc.sbuf_tensor(name, shape, dt))

        t = {"x_all": sb("x_all", [P, T, ROW]), "ident": sb("ident", [P, P])}
        t["table"], t["slot"] = sb("table", [1, TABLE], I32), sb("slot", [P, T], I32)
        for name in ("w_in", "w1_ready", "w_ready", "w_split", "rows_cleared"):
            t[name] = top.enter_context(nc.semaphore(name))
        t["rows"] = nc.dram_tensor("rows", (TG * P, ROW), F32, kind="Internal").ap()
        cross_attention(nc, top, t, io)
        with ExitStack() as attention:
            for name, shape, dt in (("xnT", [P, KD, B * S], F32), ("v_all", [P, B * NA + 1, S // P, HD2], F32),
                                    ("whead", [P, B * NA + 1, KD, 3 * HD2], F32),
                                    ("bqk", [P, B * NA + 1], F32),
                                    ("bv", [P, B * NA + 1], F32)):
                t[name] = attention.enter_context(nc.sbuf_tensor(name, shape, dt))
            gate_and_project(nc, top, t, io)
            gated_attention(nc, top, t, io)
        for name, shape, dt in (("wst", [P, 2, WE], F32), ("wh", [P, 2, WE], F32R), ("wl", [P, 2, WE], F32R),
                                ("xg", [P, TG, ROW], F32), ("bias", [P, NB * (FF + D)], F32)):
            t[name] = sb(name, shape, dt)
        context_mlp(nc, top, t, io)
        sort_rows(nc, top, t, io)
        experts(nc, top, t, io)


def kernel(**inputs):
    import numpy as np
    import concourse.bacc as bacc
    from concourse.bass_utils import run_bass_kernel_spmd

    def blocks(w):
        return w.reshape(-1, P, w.shape[-1]).transpose(1, 0, 2)

    def twice(v):
        return np.concatenate([v, v], -1)

    def rows(v, n=P):
        return np.broadcast_to(v, (n,) + v.shape)

    a = {k: np.asarray(v) for k, v in inputs.items()}
    ctx_ = a["ctx_1024"]
    arrays = {
        "x": a["x"].reshape(T, P, D).transpose(1, 0, 2),
        "ctxT": ctx_.reshape(B, L, KD, P).transpose(3, 0, 2, 1),
        "mask": rows(a["mask_Bx1x1xS2_ik0"].reshape(B, L)),
        "xa_wq": blocks(a["L0_xattn_Wq"].T),
        "xa_wk": twice(blocks(a["L0_xattn_Wk"].T).reshape(P, KD, KD, 2, P // 2)),
        "xa_wv": blocks(a["L0_xattn_Wv"].T), "xa_wo": blocks(a["L0_xattn_Wo"].T),
        "xa_bq": a["L0_xattn_bq"].reshape(KD, P).T, "xa_bk": twice(a["L0_xattn_bk"].reshape(KD, 2, P // 2)).transpose(2, 0, 1),
        "xa_bv": rows(a["L0_xattn_bv"]), "xa_bo": rows(a["L0_xattn_bo"]),
        "ctx": ctx_.transpose(1, 0, 2),
        "m_wr": blocks(a["L1_ffn_w_router"]),
        "m_w1": a["L1_ffn_w1"].reshape(NE, KD, P, FF).transpose(0, 2, 1, 3).reshape(NE, P, KD * FF),
        "m_w2": a["L1_ffn_w2"].reshape(NE, FB, P, D).transpose(0, 2, 1, 3).reshape(NE, P, FB * D),
        "m_b": np.broadcast_to(np.concatenate([a["L1_ffn_b1"], a["L1_ffn_b2"]], -1)[:, None], (NE, P, FF + D)),
        "f_w": np.concatenate([blocks(a[f"L0_ffn_W{n}"]).reshape(P, KD, H2, HD2) for n in "qkv"], -1),
        "f_wr": blocks(a["L0_ffn_Wr"]), "f_br": a["L0_ffn_br"][None],
        "f_bqk": np.concatenate([a[f"L0_ffn_b{n}"].reshape(H2, HD2).T for n in "qk"], 0),
        "f_bv": a["L0_ffn_bv"].reshape(H2, HD2).T,
        "f_wo": a["L0_ffn_Wo"].reshape(NA, HD2, D).transpose(1, 0, 2), "f_bo": rows(a["L0_ffn_bo"]),
    }
    nc = bacc.Bacc("TRN2", target_bir_lowering=False, num_devices=1)
    io = {}
    for name, v in arrays.items():
        arrays[name] = v = np.ascontiguousarray(v)
        io[name] = nc.dram_tensor(f"in_{name}", v.shape, mybir.dt.from_np(v.dtype), kind="ExternalInput").ap()
    io["out"] = nc.dram_tensor("out", (B * S, D), F32, kind="ExternalOutput").ap()
    program(nc, io)
    r = run_bass_kernel_spmd(nc, [{f"in_{k}": v for k, v in arrays.items()}], core_ids=[0])
    return r.results[0]["out"].reshape(B, S, D)
```

```python
from contextlib import ExitStack

import concourse.bass as bass
from concourse import mybir

ALU = mybir.AluOpType
ACT = mybir.ActivationFunctionType
AX = mybir.AxisListType
F32 = mybir.dt.float32
F32R = mybir.dt.float32r
BF16 = mybir.dt.bfloat16
I32 = mybir.dt.int32
U32 = mybir.dt.uint32

P = 128
B, S, D = 2, 1024, 256
KD = D // P
T = B * S // P
CH = 4
NC = T // CH
CW = CH * P
EPS = 1e-5
L = 77
H1, HD1 = 16, 16
HH = H1 // 2
GH = 4
HL = HH * L
VC = 5
VR = -(-HL // VC)
H2, HD2, NA = 16, 64, 4
NE, FF = 8, 1024
FB = FF // P
ROW = D + 4
MT = B * S // P + NE - 1
TG = MT + 2
TABLE = 2 * TG + NE + 1
TILES, LAST = 2 * TG + NE - 1, 2 * TG + NE
WE = KD * FF + FB * D
NB = 4


class Link:

    def __init__(self, eng, sem):
        self.eng, self.sem, self.n, self.reg = eng, sem, 0, 0

    def __call__(self, ins, held=None):
        ins.then_inc(self.sem, 1)
        self.n += 1
        count = self.n + self.reg
        if held is not None and not isinstance(self.reg, int):
            count = self.eng.to_reg(count)
            self.eng.wait_ge(held, 1)
        self.eng.wait_ge(self.sem, count)


def layernorm_stats(vec, link, x_tiles, stats, mv):
    for j, x in enumerate(x_tiles):
        ins = vec.bn_stats(stats[:, j, :], x)
    link(ins)
    for j in range(len(x_tiles)):
        ins = vec.bn_aggr(mv[:, j, :], stats[:, j, :])
    return ins


def cross_attention(nc, top, t, io):
    with ExitStack() as ctx:
        def sb(name, shape, dt=F32):
            return ctx.enter_context(nc.sbuf_tensor(name, shape, dt))

        def sem(name):
            return top.enter_context(nc.semaphore(name))

        NT = T // B
        W = B * P
        U = B * KD
        HP = P // 2
        LAG = 3
        x_all, ident = t["x_all"], t["ident"]
        xv = x_all[:].rearrange("p (b t) r -> p b t r", b=B)
        wk = sb("a_wk", [P, KD, KD, 2, P])
        wq, wv, wo = (sb(f"a_{n}", [P, KD, D]) for n in ("wq", "wv", "wo"))
        bq, bk, bk4 = sb("a_bq", [P, KD]), sb("a_bk", [P, KD, 2]), sb("a_bk4", [P, KD, 2])
        bv, bo = sb("a_bv", [P, D]), sb("a_bo", [P, D])
        ctxT = sb("a_ctxT", [P, B, KD, L])
        mask_i, keep = sb("a_mask", [P, B, L], I32), sb("a_keep", [P, B, L])
        heads8, heads4 = sb("a_heads8", [P, HH]), sb("a_heads4", [P, GH])
        kmask = sb("a_kmask", [P, B, GH, L])
        drop, fill = sb("a_drop", [3, B, GH, L], BF16), sb("a_fill", [3, P], BF16)
        kT = sb("a_kT", [P, KD, 2, B, L])
        khT, klT = sb("a_khT", [P, KD, 2, B, L], F32R), sb("a_klT", [P, KD, 2, B, L], F32R)
        kh, kl = sb("a_kh", [P, KD, 2, B, GH, L], F32R), sb("a_kl", [P, KD, 2, B, GH, L], F32R)
        sel, v_sb = sb("a_sel", [L, VC * VR]), sb("a_v", [L, B, D])
        vmask, vblk = sb("a_vmask", [VR, VC, HH]), sb("a_vblk", [VR, B, KD, VC, P])
        final = sb("a_final", [P, B * (NT - 2), 6])
        stats, mv = sb("a_stats", [P, 2, B, 6]), sb("a_mv", [P, 2, B, 2])
        rstd, mhalf = sb("a_rstd", [P, 2, B]), sb("a_mhalf", [P, B])
        xn, xnT, hT = sb("a_xn", [P, B, D]), sb("a_xnT", [P, KD, W]), sb("a_hT", [P, KD, W])
        qs = [sb(f"a_qs{i}", [P, 2, KD, W], F32R) for i in range(2)]
        pr = sb("a_p", [P, U, VC * VR])
        mx, sm, rs = sb("a_mx", [P, U, HH]), sb("a_sm", [P, U, HH]), sb("a_rs", [P, U, HH])
        pT = sb("a_pT", [VR, 2, KD, VC, W])
        psS = [ctx.enter_context(nc.psum_tensor(f"a_psS{m}", [P, 2, 512], F32)) for m in range(2)]
        psT = ctx.enter_context(nc.psum_tensor("a_psT", [P, 2, 512], F32))
        psX = ctx.enter_context(nc.psum_tensor("a_psX", [P, 2, W], F32))
        psQ = ctx.enter_context(nc.psum_tensor("a_psQ", [P, KD, W], F32))

        names = ("x_first", "x_rest", "w_in", "c_in", "v_in", "warm", "dve", "pool", "var", "rstd_s", "xn_s", "bo_added", "heads_s",
                 "ident_s", "consts", "keep_s", "k_ps", "k_sb", "klT_s", "kh_s", "kl_s", "v_ps", "v_s", "vrep_ps",
                 "vblk_s", "xT_ps", "x_read", "q_ps", "q_hi", "q_lo", "s_ps", "sub_done", "exp_done", "rs_s", "pn_s",
                 "pT_ps", "pT_sb", "h_ps", "h_sb", "o_ps")
        (x_first, x_rest, w_in, c_in, v_in, warm, dve, pool_sem, var_ready, rstd_ready, xn_ready, bo_added, heads_ready,
         ident_ready, consts, keep_ready, k_ps, k_sb, klT_ready, kh_ready, kl_ready, v_ps, v_ready, vrep_ps,
         vblk_ready, xT_ps, x_read, q_ps, q_hi, q_lo, s_ps, sub_done, exp_done, rs_ready, pn_ready,
         pT_ps, pT_sb, h_ps, h_sb, o_ps) = (sem("a_" + n) for n in names)

        def iterations(eng, body):
            body(0)
            with eng.Fori(1, NT // 2 - 1) as i:
                body(i)
            body(NT // 2 - 1)

        def upto(eng, s, i, per, c):
            if not isinstance(i, int) or per * i + c > 0:
                eng.wait_ge(s, i * per + c)

        def reads(n):
            return min(n + 2, NT) + max(n - 2, 0) if isinstance(n, int) else n * 2

        def wide(ps):
            return ps[0:VR].rearrange("p a b -> p (a b)")[:, 0:VC * P]

        block = ctx.enter_context(nc.Block())

        @block.sync
        def _(sp):
            io_x = io["x"].rearrange("p (b t) r -> p b t r", b=B)
            sp.dma_start(ctxT[:], io["ctxT"]).then_inc(c_in, 16)
            for b in range(B):
                sp.dma_start(xv[:, b, 0:2, 0:D], io_x[:, b, 0:2, :]).then_inc(x_first, 16)
            for b in range(B):
                sp.dma_start(xv[:, b, 2:NT, 0:D], io_x[:, b, 2:NT, :]).then_inc(x_rest, 16)
            sp.dma_start(wo[:], io["xa_wo"]).then_inc(w_in, 16)
            sp.dma_start(bo[:], io["xa_bo"]).then_inc(w_in, 16)

        @block.scalar
        def _(act):
            act.dma_start(wk[:], io["xa_wk"]).then_inc(c_in, 16)
            act.dma_start(mask_i[:], io["mask"]).then_inc(c_in, 16)
            act.dma_start(bk[:], io["xa_bk"]).then_inc(c_in, 16)
            act.dma_start(wv[:], io["xa_wv"]).then_inc(v_in, 16)
            act.dma_start(bv[:], io["xa_bv"]).then_inc(v_in, 16)
            act.wait_ge(warm, 1)
            act.activation(bk4[:, 0], bk4[:, 0], ACT.Exp).then_inc(warm, 1)
            act.dma_start(wq[:], io["xa_wq"]).then_inc(w_in, 16)
            act.dma_start(bq[:], io["xa_bq"]).then_inc(w_in, 16)

            def copy_x(i, n):
                upto(act, xT_ps, i, 2, n + 1)
                act.copy(xnT[:], psX[:]).then_inc(x_read, 1)

            def query_high(i, n):
                upto(act, q_ps, i, 2, n + 1)
                for a in range(2):
                    for m in range(KD):
                        half = slice(a * HP, (a + 1) * HP)
                        ins = act.activation(qs[n % 2][half, a, m], psQ[half, m], ACT.Identity,
                                             bias=bq[half, m:m + 1], scale=1.0)
                ins.then_inc(q_hi, 1)

            def copy_h(i, n):
                upto(act, h_ps, i, 2, n + 1)
                act.copy(hT[:], psQ[:]).then_inc(h_sb, 1)

            def copy_p(i, g):
                upto(act, pT_ps, i, 2 * U, g + 1)
                b, m = divmod(g % U, KD)
                act.copy(pT[:, g // U % 2, m, :, b * P:(b + 1) * P],
                         wide(psT).rearrange("p (c n) -> p c n", c=VC)).then_inc(pT_sb, 1)

            act.wait_ge(keep_ready, 1)
            act.wait_ge(k_ps, 1)
            for m in range(KD):
                for a in range(2):
                    ins = act.activation(kT[:, m, a], psS[m][:, a, 0:B * L].rearrange("p (b l) -> p b l", b=B),
                                         ACT.Identity, bias=bk4[:, m, a:a + 1], scale=HD1 ** -0.5)
            ins.then_inc(k_sb, 1)
            copy_x(0, 0)
            act.wait_ge(w_in, 64)
            query_high(0, 0)
            copy_x(0, 1)

            def body(i):
                for g in range(2 * U):
                    c, u = divmod(g, U)
                    n = 2 * i + c if isinstance(i, int) else 2
                    if u == 0 and n >= 2:
                        copy_h(i, c - 2)
                    if not (isinstance(i, int) and 2 * U * i + g < LAG):
                        copy_p(i, g - LAG)
                    upto(act, sub_done, i, 2 * U, g + 1)
                    act.activation(pr[:, u, 0:HL], pr[:, u, 0:HL], ACT.Exp).then_inc(exp_done, 1)
                    if u == 0 and n + 1 < NT:
                        query_high(i, c + 1)
                    if u == 3 and n + 2 < NT:
                        copy_x(i, c + 2)

            iterations(act, body)
            end = NT // 2
            copy_h(end, -2)
            copy_p(end, -3)
            copy_p(end, -2)
            copy_p(end, -1)
            copy_h(end, -1)

        @block.gpsimd
        def _(pool):
            link = Link(pool, pool_sem)

            def power(i, n):
                upto(pool, var_ready, i, 2, n + 1)
                r = rstd[:, n % 2]
                pool.tensor_tensor(r, r, mhalf[:], ALU.pow).then_inc(rstd_ready, 1)

            pool.memset(mhalf[:], -0.5)
            link(pool.memset(heads8[:], 1.0))
            link(pool.affine_select(out=heads8[:], in_=heads8[:], compare_op=ALU.is_ge, fill=0.0, base=0,
                                    pattern=[[-HD1, HH]], channel_multiplier=1))
            link(pool.affine_select(out=heads8[:], in_=heads8[:], compare_op=ALU.is_ge, fill=0.0, base=HD1 - 1,
                                    pattern=[[HD1, HH]], channel_multiplier=-1))
            pool.tensor_tensor(heads4[:], heads8[:, 0:GH], heads8[:, GH:HH], ALU.add).then_inc(heads_ready, 1)
            link(pool.memset(ident[:], 0.0))
            pool.affine_select(out=ident[:], in_=ident[:], compare_op=ALU.not_equal, fill=1.0, base=0,
                               pattern=[[-1, P]], channel_multiplier=1).then_inc(ident_ready, 1)
            power(0, 0)
            link(pool.memset(sel[:], 0.0))
            s3 = sel[:, 0:HL].rearrange("p (h l) -> p h l", h=HH)
            pool.affine_select(out=s3, in_=s3, compare_op=ALU.not_equal, fill=1.0, base=0,
                               pattern=[[0, HH], [-1, L]], channel_multiplier=1)
            link(pool.memset(fill[:], -1024.0 * 9764864))
            link(pool.affine_select(out=fill[:], in_=fill[:], compare_op=ALU.is_gt, fill=-1024.0 * 760, base=1,
                                    pattern=[[0, P]], channel_multiplier=-1))
            link(pool.affine_select(out=fill[:], in_=fill[:], compare_op=ALU.is_gt, fill=-1024.0, base=2,
                                    pattern=[[0, P]], channel_multiplier=-1))
            link(pool.memset(vmask[:], 1.0))
            link(pool.affine_select(out=vmask[:], in_=vmask[:], compare_op=ALU.is_ge, fill=0.0, base=0,
                                    pattern=[[VR, VC], [-L, HH]], channel_multiplier=1))
            link(pool.affine_select(out=vmask[:], in_=vmask[:], compare_op=ALU.is_ge, fill=0.0, base=L - 1,
                                    pattern=[[-VR, VC], [L, HH]], channel_multiplier=-1))
            pool.memset(pr[:, :, HL:], 0.0).then_inc(consts, 1)
            pool.wait_ge(klT_ready, 1)
            power(0, 1)
            for m, a in ((0, 0), (0, 1), (1, 0)):
                pool.tensor_tensor(kl[:, m, a], klT[:, m, a].unsqueeze(2).to_broadcast([P, B, GH, L]), kmask[:],
                                   ALU.mult).then_inc(kl_ready, 1)
            pool.wait_ge(w_in, 64)

            def body(i):
                for g in range(2 * U):
                    c, u = divmod(g, U)
                    n = 2 * i + c if isinstance(i, int) else 2
                    if u == 0:
                        upto(pool, xn_ready, i, 2, c + 1)
                        xc = xv[:, :, 2 * i + c, 0:D] if isinstance(i, int) else \
                            xv[:, :, bass.ds(i * 2 + c, 1), 0:D].rearrange("p b a d -> p (b a) d")
                        pool.tensor_tensor(xc, xc, bo[:].unsqueeze(1).to_broadcast([P, B, D]),
                                           ALU.add).then_inc(bo_added, 1)
                    if u == 1 and n + 2 < NT:
                        power(i, c + 2)
                    upto(pool, rs_ready, i, 2 * U, g + 1)
                    p3 = pr[:, u, 0:HL].rearrange("p (h l) -> p h l", h=HH)
                    pool.tensor_tensor(p3, p3, rs[:, u, :].unsqueeze(2).to_broadcast([P, HH, L]),
                                       ALU.mult).then_inc(pn_ready, 1)

            iterations(pool, body)

        @block.vector
        def _(vec):
            link = Link(vec, dve)

            def variance(i, n):
                at = i * 2 + n
                par = n % 2
                for b in range(B):
                    ins = vec.bn_stats(stats[:, par, b, :], x_all[:, at + b * NT, 0:D])
                link(ins, held=keep_ready)
                for b in range(B):
                    ins = vec.bn_aggr(mv[:, par, b, :], stats[:, par, b, :])
                link(ins)
                vec.tensor_scalar(rstd[:, par, :], mv[:, par, :, 1], EPS, None, ALU.add).then_inc(var_ready, 1)

            def normalise(i, n):
                at = i * 2 + n
                upto(vec, rstd_ready, i, 2, n + 1)
                upto(vec, xT_ps, i, 2, n)
                for b in range(B):
                    ins = vec.tensor_scalar(xn[:, b], x_all[:, at + b * NT, 0:D], mv[:, n % 2, b, 0:1],
                                            rstd[:, n % 2, b:b + 1], ALU.subtract, ALU.mult)
                ins.then_inc(xn_ready, 1)

            def query_low(i, n):
                upto(vec, q_hi, i, 2, n + 1)
                for a in range(2):
                    for m in range(KD):
                        half, other = slice(a * HP, (a + 1) * HP), slice((1 - a) * HP, (2 - a) * HP)
                        ins = vec.scalar_tensor_tensor(qs[n % 2][other, a, m], psQ[half, m], bq[half, m:m + 1],
                                                       qs[n % 2][half, a, m], ALU.add, ALU.subtract)
                ins.then_inc(q_lo, 1)

            def add_output(i, n):
                upto(vec, o_ps, i, 2, n + 1)
                upto(vec, bo_added, i, 2, n + 1)
                xc = xv[:, :, 2 * i + n, 0:D] if isinstance(i, int) else \
                    xv[:, :, bass.ds(i * 2 + n, 1), 0:D].rearrange("p b a d -> p (b a) d")
                vec.tensor_tensor(xc, psX[:], xc, ALU.add).then_inc(x_read, 1)

            def sums(i, g):
                upto(vec, exp_done, i, 2 * U, g + 1)
                w = g % U
                link(vec.tensor_reduce(sm[:, w], pr[:, w, 0:HL].rearrange("p (h l) -> p h l", h=HH), AX.X, ALU.add))
                vec.reciprocal(rs[:, w], sm[:, w]).then_inc(rs_ready, 1)

            vec.memset(bk4[:, 0], 0.0).then_inc(warm, 1)
            vec.wait_ge(x_first, 32)
            variance(0, 0)
            variance(0, 1)
            vec.wait_ge(c_in, 64)
            vec.wait_ge(warm, 2)
            vec.tensor_scalar(bk4[:], bk[:], HD1 ** -0.5, None, ALU.mult)
            link(vec.tensor_scalar(keep[:], mask_i[:], 0, None, ALU.not_equal))
            vec.tensor_scalar(drop[:], keep[0:3].unsqueeze(2).to_broadcast([3, B, GH, L]), -1.0, 1.0,
                              ALU.mult, ALU.add)
            vec.wait_ge(heads_ready, 1)
            for b in range(B):
                ins = vec.tensor_tensor(kmask[:, b], keep[:, b].unsqueeze(1).to_broadcast([P, GH, L]),
                                        heads4[:].unsqueeze(2).to_broadcast([P, GH, L]), ALU.mult)
            ins.then_inc(keep_ready, 1)
            normalise(0, 0)
            vec.wait_ge(v_in, 32)
            vec.wait_ge(v_ps, 1)
            vec.tensor_tensor(v_sb[:], psT[0:L, 0, :].rearrange("p (b d) -> p b d", b=B),
                              bv[0:L].unsqueeze(1).to_broadcast([L, B, D]), ALU.add).then_inc(v_ready, 1)
            vec.wait_ge(k_sb, 1)
            link(vec.tensor_copy(khT[:], kT[:]))
            vec.tensor_tensor(klT[:], kT[:], khT[:], ALU.subtract).then_inc(klT_ready, 1)
            vec.wait_ge(keep_ready, 1)
            for src, dst, m, a in ((khT, kh, 0, 0), (khT, kh, 0, 1), (khT, kh, 1, 0), (khT, kh, 1, 1), (klT, kl, 1, 1)):
                vec.tensor_tensor(dst[:, m, a], src[:, m, a].unsqueeze(2).to_broadcast([P, B, GH, L]), kmask[:],
                                  ALU.mult).then_inc(kh_ready, 1)
                if (m, a) == (1, 0):
                    vec.wait_ge(klT_ready, 1)
            query_low(0, 0)
            normalise(0, 1)
            vec.wait_ge(consts, 1)

            def value_block(i):
                b, m = divmod(i, KD)
                vec.wait_ge(vrep_ps, i + 1)
                vec.tensor_tensor(vblk[:, b, m].rearrange("p c (h d) -> p (c h) d", h=HH),
                                  wide(psT).rearrange("p (c d) -> p c d", d=HD1),
                                  vmask[:].rearrange("p c h -> p (c h)").unsqueeze(2)
                                  .to_broadcast([VR, VC * HH, HD1]), ALU.mult).then_inc(vblk_ready, 1)

            value_block(0)
            vec.wait_ge(x_rest, 32)

            def body(i):
                start = link.n
                if not isinstance(i, int):
                    link.reg = (i - 1) * per_pair
                for g in range(2 * U):
                    c, u = divmod(g, U)
                    n = 2 * i + c if isinstance(i, int) else 2
                    s4 = psS[u % KD][:, :, 0:GH * L].rearrange("p a (g l) -> p a g l", g=GH)
                    upto(vec, s_ps, i, 2 * U, g + 1)
                    link(vec.tensor_reduce(mx[:, u].rearrange("p (a g) -> p a g", a=2), s4, AX.X, ALU.max))
                    upto(vec, pT_ps, i, 2 * U, g + 1 - U)
                    vec.tensor_tensor(pr[:, u, 0:HL].rearrange("p (a g l) -> p a g l", a=2, g=GH), s4,
                                      mx[:, u].rearrange("p (a g) -> p a g", a=2).unsqueeze(3)
                                      .to_broadcast([P, 2, GH, L]), ALU.subtract).then_inc(sub_done, 1)
                    if u == 1 and n + 1 < NT:
                        query_low(i, c + 1)
                    if not (isinstance(i, int) and 2 * U * i + g == 0):
                        sums(i, g - 1)
                    if n == 0 and isinstance(i, int) and u < 3:
                        value_block(u + 1)
                    if u == 0 and n + 2 < NT:
                        variance(i, c + 2)
                    if u == 2 and n >= 2:
                        add_output(i, c - 2)
                    if u == 2 and n + 2 < NT:
                        normalise(i, c + 2)
                return link.n - start

            per_pair = 2 * (2 * U) + 2 * 2
            body(0)
            with vec.Fori(1, NT // 2 - 1) as i:
                assert body(i) == per_pair
            link.reg, link.n = 0, link.n + (NT // 2 - 3) * per_pair
            body(NT // 2 - 1)
            end = NT // 2
            sums(end, -1)

            def finished(first, last):
                tiles = [b * NT + n for b in range(B) for n in range(first, last + 1)]
                for j, tile in enumerate(tiles):
                    ins = vec.bn_stats(final[:, j, :], x_all[:, tile, 0:D])
                link(ins)
                for j, tile in enumerate(tiles):
                    ins = vec.bn_aggr(t["mv"][:, tile, :], final[:, j, :])
                link(ins)

            vec.wait_ge(x_read, reads(NT))
            finished(0, NT - 3)
            add_output(end, -2)
            vec.wait_ge(x_read, reads(NT) + 1)
            finished(NT - 2, NT - 2)
            add_output(end, -1)
            vec.wait_ge(x_read, reads(NT) + 2)
            finished(NT - 1, NT - 1)
            vec.tensor_scalar(t["rstd"][:], t["mv"][:, :, 1], EPS, None, ALU.add)

        @block.tensor
        def _(pe):
            def transpose_x(i, n):
                upto(pe, xn_ready, i, 2, n + 1)
                for k in range(KD):
                    for b in range(B):
                        ins = pe.transpose(psX[:, k, b * P:(b + 1) * P], xn[:, b, k * P:(k + 1) * P], ident[:])
                ins.then_inc(xT_ps, 1)

            def query(i, n):
                for m in range(KD):
                    for k in range(KD):
                        ins = pe.matmul(psQ[:, m], wq[:, k, m * P:(m + 1) * P], xnT[:, k],
                                        start=(k == 0), stop=(k == KD - 1))
                ins.then_inc(q_ps, 1)

            def transpose_p(i, g):
                if isinstance(i, int) and i == g == 0:
                    pe.wait_ge(vblk_ready, U)
                upto(pe, pn_ready, i, 2 * U, g + 1)
                upto(pe, pT_sb, i, 2 * U, g)
                for c in range(VC):
                    ins = pe.transpose(wide(psT)[:, c * P:(c + 1) * P], pr[:, g % U, c * VR:(c + 1) * VR], ident[:])
                ins.then_inc(pT_ps, 1)

            def values(i, n, m):
                upto(pe, pT_sb, i, 2 * U, (n + 1) * U - (KD - 1 - m))
                for b in range(B):
                    for c in range(VC):
                        ins = pe.matmul(psQ[:, m, b * P:(b + 1) * P], vblk[:, b, m, c, :],
                                        pT[:, n % 2, m, c, b * P:(b + 1) * P], start=(c == 0), stop=(c == VC - 1))
                if m == KD - 1:
                    ins.then_inc(h_ps, 1)

            def output(i, n):
                for b in range(B):
                    for m in range(KD):
                        ins = pe.matmul(psX[:, b], hT[:, m, b * P:(b + 1) * P], wo[:, m, :],
                                        start=(m == 0), stop=(m == KD - 1))
                ins.then_inc(o_ps, 1)

            pe.wait_ge(c_in, 64)
            for m in range(KD):
                for a in range(2):
                    for k in range(KD):
                        ins = pe.matmul(psS[m][:, a, 0:B * L].rearrange("p (b l) -> p b l", b=B), wk[:, k, m, a, :],
                                        ctxT[:, :, k, :], start=(k == 0), stop=(k == KD - 1))
            ins.then_inc(k_ps, 1)
            pe.wait_ge(v_in, 32)
            for b in range(B):
                for k in range(KD):
                    ins = pe.matmul(psT[0:L, 0, b * D:(b + 1) * D], ctxT[:, b, k, :], wv[:, k, :],
                                    start=(k == 0), stop=(k == KD - 1))
            ins.then_inc(v_ps, 1)
            pe.wait_ge(ident_ready, 1)
            transpose_x(0, 0)
            pe.wait_ge(x_read, 1)
            pe.wait_ge(w_in, 64)
            query(0, 0)
            pe.wait_ge(consts, 1)
            pe.wait_ge(v_ready, 1)

            def repeat_values(i):
                b, m = divmod(i, KD)
                if i:
                    pe.wait_ge(vblk_ready, i)
                for c in range(VC):
                    ins = pe.matmul(wide(psT)[:, c * P:(c + 1) * P],
                                    sel[:, c * VR:(c + 1) * VR], v_sb[:, b, m * P:(m + 1) * P], start=True, stop=True)
                ins.then_inc(vrep_ps, 1)

            repeat_values(0)
            transpose_x(0, 1)

            def body(i):
                for g in range(2 * U):
                    c, u = divmod(g, U)
                    b, m = divmod(u, KD)
                    n = 2 * i + c if isinstance(i, int) else 2
                    if n == 0 and isinstance(i, int) and u < 2:
                        pe.wait_ge(kh_ready, (2, U + 1)[u])
                        pe.wait_ge(kl_ready, (2, U - 1)[u])
                    if u == 0:
                        upto(pe, q_lo, i, 2, c + 1)
                    upto(pe, sub_done, i, 2 * U, g - 1)
                    for a in range(2):
                        pe.matmul(psS[m][:, a, 0:GH * L], fill[:], drop[:, b], start=True, stop=False)
                        for part in (kh, kl):
                            ins = pe.matmul(psS[m][:, a, 0:GH * L], qs[c][:, a, m, b * P:(b + 1) * P],
                                            part[:, m, a, b], start=False, stop=(part is kl))
                    ins.then_inc(s_ps, 1)
                    if not (isinstance(i, int) and 2 * U * i + g < LAG):
                        transpose_p(i, g - LAG)
                    if n == 0 and isinstance(i, int) and u < 3:
                        repeat_values(u + 1)
                    if u == 0 and n + 1 < NT:
                        pe.wait_ge(x_read, reads(i * 2 + c))
                        upto(pe, h_sb, i, 2, c - 1)
                        query(i, c + 1)
                    if u == 1 and n >= 2:
                        pe.wait_ge(x_read, reads(i * 2 + c))
                        upto(pe, h_sb, i, 2, c - 1)
                        output(i, c - 2)
                    if u == 2 and n >= 1:
                        upto(pe, q_lo, i, 2, c + 2 if n + 1 < NT else c + 1)
                        upto(pe, h_sb, i, 2, c - 1)
                        values(i, c - 1, 0)
                    if u == 3 and n + 2 < NT:
                        pe.wait_ge(x_read, reads(i * 2 + c) + (1 if n >= 2 else 0))
                        transpose_x(i, c + 2)
                    if u == 3 and n >= 1:
                        values(i, c - 1, 1)

            iterations(pe, body)
            end = NT // 2
            transpose_p(end, -3)
            pe.wait_ge(x_read, reads(NT))
            pe.wait_ge(h_sb, NT - 1)
            output(end, -2)
            transpose_p(end, -2)
            values(end, -1, 0)
            transpose_p(end, -1)
            values(end, -1, 1)
            pe.wait_ge(h_sb, NT)
            pe.wait_ge(x_read, reads(NT) + 1)
            output(end, -1)


def gate_and_project(nc, top, t, io):
    with ExitStack() as ctx:
        def sb(name, shape, dt=F32):
            return ctx.enter_context(nc.sbuf_tensor(name, shape, dt))

        def sem(name):
            return top.enter_context(nc.semaphore(name))

        x_all, ident, xnT, v_all = t["x_all"], t["ident"], t["xnT"], t["v_all"]
        whead, bqk, bv = t["whead"], t["bqk"], t["bv"]
        NI = B * NA
        head_col = sb("g_head_col", [1, NI], I32)
        bo = sb("g_bo", [P, D])
        bqk_all, bv_all = sb("g_bqk_all", [P, H2]), sb("g_bv_all", [P, H2])
        one, onehot = sb("g_one", [1, P]), sb("g_onehot", [1, NI, H2])
        bsel = sb("g_bsel", [P, 2, NI, H2])
        mv, rstd, mhalf = t["mv"], t["rstd"], sb("g_mhalf", [P, CH])
        xn = sb("g_xn", [P, 2, CH, D])
        part = sb("g_part", [P, KD, NC])
        mean = sb("g_mean", [P, KD, B])
        wr, br = sb("g_wr", [P, KD, H2]), sb("g_br", [1, H2])
        dist, e, cand, rank, act_h, slot_of, weighted = (sb(f"g_{n}", [1, B, H2]) for n in
                                                         ("dist", "e", "cand", "rank", "acth", "slot", "wtd"))
        top1, tot = sb("g_top1", [1, B]), sb("g_tot", [1, B])
        above, same = sb("g_above", [1, B, H2, H2]), sb("g_same", [1, B, H2, H2])
        lower = sb("g_lower", [1, H2, H2])
        numi, num = sb("g_numi", [1, H2], I32), sb("g_num", [1, H2])
        pick = sb("g_pick", [1, B, NA, H2])
        col = sb("g_col", [1, NI])
        psX = [ctx.enter_context(nc.psum_tensor(f"g_psX{m}", [P, KD, CW], F32)) for m in range(2)]
        psV = [ctx.enter_context(nc.psum_tensor(f"g_psV{m}", [P, 512], F32)) for m in range(2)]
        psG = ctx.enter_context(nc.psum_tensor("g_psG", [1, 512], F32))
        psB = ctx.enter_context(nc.psum_tensor("g_psB", [P, 512], F32))
        w_in, dve, pool_sem = sem("g_w_in"), sem("g_dve"), sem("g_pool")
        consts, half_ready, rstd_ready, xn_ready = (sem(f"g_{n}") for n in ("consts", "half_s", "rstd_s", "xn_s"))
        xT_ps, xT_sb, mean_ready, logit_ps = (sem(f"g_{n}") for n in ("xT_ps", "xT_sb", "mean_s", "logit"))
        shifted, exp_done, col_ready, v_ps, v_sb = (sem(f"g_{n}") for n in ("shift", "exp", "col_s", "v_ps", "v_sb"))
        vpad, bias_in, bo_in, onehot_ready, onehot_ps, bo_added = (sem(f"g_{n}") for n in (
            "vpad", "bias_in", "bo_in", "onehot_s", "onehot_ps", "bo_added"))
        w_head = t["w_head"] = [sem(f"g_w_head{b}") for b in range(B)]
        block = ctx.enter_context(nc.Block())

        def fetch_heads(eng, par):
            eng.wait_ge(col_ready, 1)
            for i in range(par, NI, 2):
                r = eng.value_load(head_col[0:1, i:i + 1], min_val=0, max_val=H2 - 1)
                eng.dma_start(whead[:, i], io["f_w"][:, :, bass.ds(r, 1), :]
                              .rearrange("p k a c -> p k (a c)")).then_inc(w_head[i // NA], 16)

        @block.sync
        def _(sp):
            sp.dma_start(wr[:], io["f_wr"]).then_inc(w_in, 16)
            sp.dma_start(br[:], io["f_br"]).then_inc(w_in, 16)
            sp.dma_start(bqk_all[:], io["f_bqk"]).then_inc(bias_in, 16)
            sp.dma_start(bv_all[0:HD2], io["f_bv"]).then_inc(bias_in, 16)
            sp.dma_start(bo[:], io["f_bo"]).then_inc(bo_in, 16)
            fetch_heads(sp, 0)

        @block.gpsimd
        def _(pool):
            link = Link(pool, pool_sem)
            pool.memset(mhalf[:], -0.5).then_inc(half_ready, 1)
            pool.wait_ge(half_ready, 1)
            for n in range(NC):
                pool.tensor_tensor(rstd[:, n * CH:(n + 1) * CH], rstd[:, n * CH:(n + 1) * CH], mhalf[:],
                                   ALU.pow).then_inc(rstd_ready, 1)
            pool.memset(v_all[:, NI], 0.0)
            pool.memset(whead[:, NI:], 0.0)
            pool.memset(bqk[:, NI:], 0.0)
            pool.memset(bv[:, NI:], 0.0)
            pool.memset(one[:], 1.0).then_inc(vpad, 1)
            pool.iota(numi[:], pattern=[[1, H2]], base=0, channel_multiplier=0)
            link(pool.memset(lower[:], 1.0))
            pool.affine_select(out=lower[:], in_=lower[:], compare_op=ALU.is_gt, fill=0.0, base=0,
                               pattern=[[1, H2], [-1, H2]], channel_multiplier=0).then_inc(consts, 1)
            pool.wait_ge(bo_in, 16)
            for n in range(NC):
                pool.wait_ge(xn_ready, n + 1)
                xc = x_all[:, n * CH:(n + 1) * CH, 0:D]
                pool.tensor_tensor(xc, xc, bo[:].unsqueeze(1).to_broadcast([P, CH, D]), ALU.add).then_inc(bo_added, 1)

        @block.scalar
        def _(act):
            with act.Fori(0, NC // 2) as h:
                for par in range(2):
                    n = h * 2 + par
                    act.wait_ge(xT_ps, n + 1)
                    for k in range(KD):
                        act.activation(xnT[:, k, bass.ds(n * CW, CW)], psX[par][:, k], ACT.Identity,
                                       accum_out=part[:, k, bass.ds(n, 1)]).then_inc(xT_sb, 1)
            act.wait_ge(shifted, 1)
            act.activation(e[:], e[:], ACT.Exp).then_inc(exp_done, 1)
            fetch_heads(act, 1)
            for i in range(T // B):
                act.wait_ge(v_ps, i + 1)
                act.copy(v_all[:, 0:NA, i, :],
                         psV[i % 2][:, 0:NA * HD2].rearrange("p (h d) -> p h d", h=NA)).then_inc(v_sb, 1)

        @block.vector
        def _(vec):
            link = Link(vec, dve)
            vec.memset(bv_all[HD2:P], 0.0)
            for n in range(NC):
                vec.wait_ge(rstd_ready, n + 1)
                if n >= 2:
                    vec.wait_ge(xT_ps, n - 1)
                for j in range(n * CH, (n + 1) * CH):
                    ins = vec.tensor_scalar(xn[:, n % 2, j % CH], x_all[:, j, 0:D], mv[:, j, 0:1], rstd[:, j:j + 1],
                                            ALU.subtract, ALU.mult)
                ins.then_inc(xn_ready, 1)
            vec.wait_ge(xT_sb, NC * KD)
            link(vec.tensor_reduce(mean[:], part[:].rearrange("p k (b c) -> p k b c", b=B), AX.X, ALU.add))
            vec.tensor_scalar(mean[:], mean[:], 1.0 / S, None, ALU.mult).then_inc(mean_ready, 1)
            vec.wait_ge(w_in, 32)
            vec.wait_ge(logit_ps, 1)
            link(vec.tensor_tensor(dist[:], psG[0:1, 0:B * H2].rearrange("p (b h) -> p b h", b=B),
                                   br[:].unsqueeze(1).to_broadcast([1, B, H2]), ALU.add))
            link(vec.tensor_reduce(top1[:], dist[:], AX.X, ALU.max))
            vec.tensor_tensor(e[:], dist[:], top1[:].unsqueeze(2).to_broadcast([1, B, H2]),
                              ALU.subtract).then_inc(shifted, 1)
            vec.wait_ge(exp_done, 1)
            link(vec.tensor_reduce(tot[:], e[:], AX.X, ALU.add))
            link(vec.reciprocal(tot[:], tot[:]))
            link(vec.tensor_tensor(dist[:], e[:], tot[:].unsqueeze(2).to_broadcast([1, B, H2]), ALU.mult))
            full = [1, B, H2, H2]
            other, own = dist[:].unsqueeze(2).to_broadcast(full), dist[:].unsqueeze(3).to_broadcast(full)
            vec.tensor_tensor(above[:], other, own, ALU.is_gt)
            link(vec.tensor_tensor(same[:], other, own, ALU.is_equal))
            vec.wait_ge(consts, 1)
            low = lower[:].unsqueeze(1).to_broadcast(full)
            link(vec.tensor_tensor(same[:], same[:], low, ALU.mult))
            link(vec.tensor_tensor(above[:], above[:], same[:], ALU.add))
            link(vec.tensor_reduce(rank[:], above[:], AX.X, ALU.add))
            link(vec.tensor_scalar(act_h[:], rank[:], NA - 0.5, None, ALU.is_lt))
            link(vec.tensor_tensor(same[:], act_h[:].unsqueeze(2).to_broadcast(full), low, ALU.mult))
            link(vec.tensor_reduce(slot_of[:], same[:], AX.X, ALU.add))
            link(vec.tensor_copy(num[:], numi[:]))
            link(vec.tensor_tensor(weighted[:], act_h[:], num[:].unsqueeze(1).to_broadcast([1, B, H2]), ALU.mult))
            part_s = [1, B, NA, H2]
            link(vec.tensor_tensor(pick[:], slot_of[:].unsqueeze(2).to_broadcast(part_s),
                                   num[:, 0:NA].unsqueeze(1).unsqueeze(3).to_broadcast(part_s), ALU.is_equal))
            link(vec.tensor_tensor(pick[:], pick[:], weighted[:].unsqueeze(2).to_broadcast(part_s), ALU.mult))
            link(vec.tensor_reduce(col[:].rearrange("p (b s) -> p b s", b=B), pick[:], AX.X, ALU.add))
            vec.tensor_copy(head_col[:], col[:]).then_inc(col_ready, 1)
            vec.tensor_tensor(onehot[:], num[:].unsqueeze(1).to_broadcast([1, NI, H2]),
                              col[:].unsqueeze(2).to_broadcast([1, NI, H2]), ALU.is_equal).then_inc(onehot_ready, 1)
            vec.wait_ge(bias_in, 32)
            vec.wait_ge(vpad, 1)
            vec.wait_ge(onehot_ps, 1)
            for x, every in enumerate((bqk_all, bv_all)):
                ins = vec.tensor_tensor(bsel[:, x], psB[:, 0:NI * H2].rearrange("p (i h) -> p i h", i=NI),
                                        every[:].unsqueeze(1).to_broadcast([P, NI, H2]), ALU.mult)
            link(ins)
            for x, chosen in enumerate((bv, bqk)):
                ins = vec.tensor_reduce(chosen[:, 0:NI], bsel[:, 1 - x], AX.X, ALU.add)
            link(ins)
            vec.tensor_scalar(bqk[0:HD2], bqk[0:HD2], HD2 ** -0.5, None, ALU.mult)

        @block.tensor
        def _(pe):
            with pe.Fori(0, NC // 2) as h:
                for par in range(2):
                    n = h * 2 + par
                    pe.wait_ge(xn_ready, n + 1)
                    pe.wait_ge(xT_sb, h * 2 * KD)
                    for k in range(KD):
                        for j in range(CH):
                            ins = pe.transpose(psX[par][:, k, j * P:(j + 1) * P], xn[:, par, j, k * P:(k + 1) * P],
                                               ident[:])
                    ins.then_inc(xT_ps, 1)
            pe.wait_ge(mean_ready, 1)
            pe.wait_ge(w_in, 32)
            for b in range(B):
                for k in range(KD):
                    ins = pe.matmul(psG[0:1, b * H2:(b + 1) * H2], mean[:, k, b:b + 1], wr[:, k, :],
                                    start=(k == 0), stop=(k == KD - 1))
            ins.then_inc(logit_ps, 1)
            pe.wait_ge(vpad, 1)
            pe.wait_ge(onehot_ready, 1)
            pe.matmul(psB[:, 0:NI * H2], one[:], onehot[:].rearrange("p i h -> p (i h)"), start=True,
                      stop=True).then_inc(onehot_ps, 1)
            pe.wait_ge(w_head[0], 16 * NA)
            for i in range(T // B):
                if i >= 2:
                    pe.wait_ge(v_sb, i - 1)
                for k in range(KD):
                    ins = pe.matmul(psV[i % 2][:, 0:NA * HD2].rearrange("p (s d) -> p s d", s=NA), xnT[:, k, i * P:(i + 1) * P],
                                    whead[:, 0:NA, k, 2 * HD2:3 * HD2],
                                    start=(k == 0), stop=(k == KD - 1))
                ins.then_inc(v_ps, 1)


def gated_attention(nc, top, t, io):
    with ExitStack() as ctx:
        def sb(name, shape, dt=F32):
            return ctx.enter_context(nc.sbuf_tensor(name, shape, dt))

        def sem(name):
            return top.enter_context(nc.semaphore(name))

        x_all, ident, xnT, v_all = t["x_all"], t["ident"], t["xnT"], t["v_all"]
        whead, bqk, bv = t["whead"], t["bqk"], t["bv"]
        NI = B * NA
        NQ = S // P
        KT = S // P
        HK = KT // 2
        QP = 2
        SW = 2 * NQ
        GW = SW // QP
        LAG = 3
        wqk = [sb(f"h_wqk{i}", [P, KD, P]) for i in range(2)]
        qs = [sb(f"h_qs{i}", [P, S], F32R) for i in range(2)]
        kh = [sb(f"h_kh{i}", [P, S], F32R) for i in range(2)]
        kl = [sb(f"h_kl{i}", [P, S], F32R) for i in range(2)]
        vs = [sb(f"h_vs{i}", [P, KT, 2, HD2], F32R) for i in range(2)]
        pr = sb("h_p", [P, 4, S])
        nmx, sm, rs = sb("h_nmx", [P, SW]), sb("h_sm", [P, SW]), sb("h_rs", [P, SW])
        pTh = [sb(f"h_pTh{i}", [P, KT, QP * P], F32R) for i in range(2)]
        pTl = [sb(f"h_pTl{i}", [P, KT, QP * P], F32R) for i in range(2)]
        oT = sb("h_oT", [P, NI // 2 * S])
        olo = sb("h_olo", [HD2, 2, QP * P])
        stats, mhalf = sb("h_stats", [P, CH, 6]), sb("h_mhalf", [P, CH])
        wo = sb("h_wo", [P, NA // 2, D])
        psS = [ctx.enter_context(nc.psum_tensor(f"h_psS{m}", [P, S], F32)) for m in range(2)]
        psT = [ctx.enter_context(nc.psum_tensor(f"h_psT{m}", [P, HK, P], F32)) for m in range(2)]
        psP = ctx.enter_context(nc.psum_tensor("h_psP", [P, 512], F32))
        psO = ctx.enter_context(nc.psum_tensor("h_psO", [P, 512], F32))

        names = ("w_in", "scaled", "qk_ps", "qk_hi", "qk_lo", "qk_ready", "vh_ready",
                 "v_ready", "s_ps", "max_ready", "exp_done", "rs_ready", "pn_ready", "pT_ps", "pT_hi", "pT_lo",
                 "o_ps", "o_sb", "y_ps", "y_sb", "dve", "var", "half_s",
                 "v_ps", "v_sb", "olo_s")
        (w_in, scaled, qk_ps, qk_hi, qk_lo, qk_ready, vh_ready, v_ready, s_ps, max_ready,
         exp_done, rs_ready, pn_ready, pT_ps, pT_hi, pT_lo, o_ps, o_sb, y_ps, y_sb, dve,
         var_ready, half_ready, v_ps, v_sb, olo_ready) = (sem("h_" + n) for n in names)

        def upto(eng, s, n, per, c, held=None):
            count = n * per + c
            if not isinstance(n, int):
                count = eng.to_reg(count)
            if held is not None and not isinstance(n, int):
                eng.wait_ge(held, 1)
            if not isinstance(n, int) or count > 0:
                eng.wait_ge(s, count)

        def iterations(eng, body):
            body(0)
            with eng.Fori(1, NI // 2) as n:
                body(n)

        block = ctx.enter_context(nc.Block())


        @block.sync
        def _(sp):
            sp.dma_start(wo[:], io["f_wo"]).then_inc(w_in, 16)
            sp.dma_start(t["ctxT"][:], io["ctxT"]).then_inc(t["c_in"], 16)
            sp.dma_start(t["ctxs"][:], io["ctx"]).then_inc(t["c_in"], 16)
            sp.dma_start(t["wr"][:], io["m_wr"]).then_inc(t["c_in"], 16)

        @block.gpsimd
        def _(pool):
            def split_v(n, c, par):
                upto(pool, vh_ready, n, 2, c + 1, held=scaled)
                v = v_all[:, 2 * n + c] if isinstance(n, int) else \
                    v_all[:, bass.ds(n * 2 + c, 1)].rearrange("p a k d -> p (a k) d")
                pool.tensor_tensor(vs[par][:, :, 1, :], v, vs[par][:, :, 0, :], ALU.subtract).then_inc(v_ready, 1)

            def duplicate(n, c, par, ch):
                cols = slice(ch * CW, (ch + 1) * CW)
                if c > 0:
                    upto(pool, pn_ready, n, SW, NQ * (c - 1) + 3 * ch + 3, held=scaled)
                upto(pool, v_ready, n, 2, c)
                upto(pool, qk_lo, n, 4, 2 * c + ch + 1, held=scaled)
                pool.tensor_scalar(kh[par][0:HD2, cols], kh[par][HD2:P, cols], 1.0, 0.0, ALU.mult, ALU.add)
                pool.tensor_scalar(kl[par][0:HD2, cols], kl[par][HD2:P, cols], 1.0, 0.0, ALU.mult,
                                   ALU.add).then_inc(qk_ready, 1)
                upto(pool, qk_ready, n, 4, 2 * c + ch + 1, held=scaled)

            duplicate(0, 0, 0, 0)
            duplicate(0, 0, 0, 1)
            split_v(0, 0, 0)

            def body(n):
                for c in range(SW):
                    i, q = divmod(c, NQ)
                    upto(pool, rs_ready, n, SW, c + 1, held=scaled)
                    pool.tensor_scalar(pr[:, c % 4], pr[:, c % 4], rs[:, c:c + 1], 0.0, ALU.mult,
                                       ALU.add).then_inc(pn_ready, 1)
                    if q in (2, 5):
                        duplicate(n, i + 1, (i + 1) % 2, q // 3)
                    if q == 6:
                        split_v(n, i + 1, (i + 1) % 2)

            iterations(pool, body)
            pool.memset(mhalf[:], -0.5).then_inc(half_ready, 1)
            pool.wait_ge(half_ready, 1)
            for n in range(NC):
                pool.wait_ge(var_ready, n + 1)
                pool.tensor_tensor(t["rstd"][:, n * CH:(n + 1) * CH], t["rstd"][:, n * CH:(n + 1) * CH], mhalf[:],
                                   ALU.pow)

        @block.scalar
        def _(act):
            def scale_q(n, c, par):
                upto(act, qk_ps, n, 4, 2 * c - 2, held=scaled)
                w = whead[:, 2 * n + c] if isinstance(n, int) else \
                    whead[:, bass.ds(n * 2 + c, 1)].rearrange("p a k c -> p (a k) c")
                act.mul(wqk[par][:, :, 0:HD2], w[:, :, 0:HD2], HD2 ** -0.5)
                act.copy(wqk[par][:, :, HD2:P], w[:, :, HD2:P]).then_inc(scaled, 1)

            def project(n, c, par, ch, ps=psP):
                upto(act, qk_ps, n, 4, 2 * c + ch + 1, held=qk_ps)
                upto(act, s_ps, n, SW, NQ * (c - 1))
                cols = slice(ch * CW, (ch + 1) * CW)
                bias = [bqk[h, bass.ds(n * 2 + c, 1)] for h in (slice(0, HD2), slice(HD2, P))]
                act.activation(qs[par][0:HD2, cols], ps[0:HD2], ACT.Identity, bias=bias[0], scale=1.0)
                act.activation(kh[par][HD2:P, cols], ps[HD2:P], ACT.Identity, bias=bias[1],
                               scale=1.0).then_inc(qk_hi, 1)

            def split_v(n, c, par):
                upto(act, o_ps, n, GW, (c - 1) * NQ // QP, held=qk_ps)
                v = v_all[:, 2 * n + c] if isinstance(n, int) else \
                    v_all[:, bass.ds(n * 2 + c, 1)].rearrange("p a k d -> p (a k) d")
                act.copy(vs[par][:, :, 0, :], v).then_inc(vh_ready, 1)

            def high(n, c):
                for hf in range(2):
                    upto(act, pT_ps, n, 2 * SW, 2 * c + hf + 1)
                    upto(act, o_ps, n, GW, c // QP - 1)
                    act.copy(pTh[c // QP % 2][:, hf * HK:(hf + 1) * HK, c % QP * P:(c % QP + 1) * P],
                             psT[hf][:]).then_inc(pT_hi, 1)

            def output(n, g):
                upto(act, o_ps, n, GW, g + 1)
                act.copy(olo[:, g % 2], psO[HD2:P, 0:QP * P]).then_inc(olo_ready, 1)

            scale_q(0, 0, 0)
            scale_q(0, 1, 1)
            project(0, 0, 0, 0)
            project(0, 0, 0, 1, psO)
            for i in range(KT):
                act.wait_ge(v_ps, i + 1)
                act.copy(v_all[:, NA:2 * NA, i, :],
                         psT[i % 2][:, 0:2].rearrange("p a (s d) -> p (a s) d", d=HD2)).then_inc(v_sb, 1)
                if i == 0:
                    split_v(0, 0, 0)

            def body(n):
                for c in range(SW):
                    i, q = divmod(c, NQ)
                    if not (isinstance(n, int) and c < LAG):
                        high(n, c - LAG)
                    upto(act, max_ready, n, SW, c + 1)
                    upto(act, pT_ps, n, 2 * SW, 2 * (c - 3))
                    act.activation(pr[:, c % 4], psS[c % 2][:], ACT.Exp, bias=nmx[:, c:c + 1], scale=1.0,
                                   accum_out=sm[:, c:c + 1]).then_inc(exp_done, 1)
                    if c % 2 == 0 and not (isinstance(n, int) and c < 6):
                        output(n, (c - 6) // 2)
                    if q in (0, 4):
                        project(n, i + 1, (i + 1) % 2, q // 3)
                    if q == 6:
                        scale_q(n, i + 2, i % 2)
                    if q == 5:
                        split_v(n, i + 1, (i + 1) % 2)

            iterations(act, body)
            last = NI // 2
            high(last, -3)
            output(last, -3)
            high(last, -2)
            high(last, -1)
            output(last, -2)
            output(last, -1)

        @block.vector
        def _(vec):
            link = Link(vec, dve)

            def project(n, c, par, ch, ps=psP):
                upto(vec, qk_hi, n, 4, 2 * c + ch + 1)
                cols = slice(ch * CW, (ch + 1) * CW)
                bias = [bqk[h, bass.ds(n * 2 + c, 1)] for h in (slice(0, HD2), slice(HD2, P))]
                vec.scalar_tensor_tensor(qs[par][HD2:P, cols], ps[0:HD2], bias[0], qs[par][0:HD2, cols],
                                         ALU.add, ALU.subtract)
                vec.scalar_tensor_tensor(kl[par][HD2:P, cols], ps[HD2:P], bias[1], kh[par][HD2:P, cols],
                                         ALU.add, ALU.subtract).then_inc(qk_lo, 1)

            def low(n, c):
                for hf in range(2):
                    upto(vec, pT_hi, n, 2 * SW, 2 * c + hf + 1)
                    part = (slice(None), slice(hf * HK, (hf + 1) * HK), slice(c % QP * P, (c % QP + 1) * P))
                    vec.tensor_tensor(pTl[c // QP % 2][part], psT[hf][:], pTh[c // QP % 2][part],
                                      ALU.subtract).then_inc(pT_lo, 1)

            def output(n, g):
                upto(vec, olo_ready, n, GW, g + 1)
                per = NQ // QP
                half = slice(g // per % 2 * HD2, (g // per % 2 + 1) * HD2)
                vec.scalar_tensor_tensor(oT[half, bass.ds(n * S + (g // GW * S + g % per * QP * P), QP * P)],
                                         psO[0:HD2, 0:QP * P], bv[0:HD2, bass.ds(n * 2 + g // per, 1)],
                                         olo[:, g % 2], ALU.add, ALU.add).then_inc(o_sb, 1)

            def invert(n, c):
                upto(vec, exp_done, n, SW, c + 1)
                vec.reciprocal(rs[:, c % SW:c % SW + 1], sm[:, c % SW:c % SW + 1]).then_inc(rs_ready, 1)

            project(0, 0, 0, 0)
            project(0, 0, 0, 1, psO)

            def body(n):
                for c in range(SW):
                    i, q = divmod(c, NQ)
                    upto(vec, s_ps, n, SW, c + 1)
                    vec.tensor_reduce(nmx[:, c:c + 1], psS[c % 2][:], AX.X, ALU.max, negate=True).then_inc(max_ready, 1)
                    if not (isinstance(n, int) and c == 0):
                        invert(n, c - 1)
                    if not (isinstance(n, int) and c < LAG):
                        low(n, c - LAG)
                    if q in (1, 5):
                        project(n, i + 1, (i + 1) % 2, q // 3)
                    if c % 2 == 0 and not (isinstance(n, int) and c < 6):
                        output(n, (c - 6) // 2)

            iterations(vec, body)
            last = NI // 2
            invert(last, -1)
            low(last, -3)
            output(last, -3)
            low(last, -2)
            low(last, -1)
            output(last, -2)
            output(last, -1)
            for r in range(T // 2):
                vec.wait_ge(y_ps, r + 1)
                xc = x_all[:, 2 * r:2 * r + 2, 0:D]
                vec.tensor_tensor(xc, (psP, psO)[r % 2][:].rearrange("p (a d) -> p a d", a=2), xc,
                                  ALU.add).then_inc(y_sb, 1)
                if r % 2 == 1:
                    n = r // 2
                    vec.wait_ge(y_sb, r + 1)
                    link(layernorm_stats(vec, link, [x_all[:, n * CH + j, 0:D] for j in range(CH)], stats,
                                         t["mv"][:, n * CH:(n + 1) * CH]))
                    vec.tensor_scalar(t["rstd"][:, n * CH:(n + 1) * CH], t["mv"][:, n * CH:(n + 1) * CH, 1], EPS,
                                      None, ALU.add).then_inc(var_ready, 1)

        @block.tensor
        def _(pe):
            def project(n, c, par, ch, ps=psP):
                upto(pe, scaled, n, 2, c + 1)
                if ps is psP:
                    upto(pe, qk_hi, n, 4, 2 * c + ch)
                    upto(pe, qk_lo, n, 4, 2 * c + ch)
                batch = (2 * n + c) // NA if isinstance(n, int) else ((n * 2 + c) // NA) % B
                for k in range(KD):
                    ins = pe.matmul(ps[:], wqk[par][:, k, :], xnT[:, k, bass.ds(batch * S + ch * CW, CW)],
                                    start=(k == 0), stop=(k == KD - 1))
                ins.then_inc(qk_ps, 1)

            def transposes(n, c):
                for hf in range(2):
                    upto(pe, pn_ready, n, SW, c + 1)
                    upto(pe, pT_lo, n, 2 * SW, 2 * c + hf - 1)
                    for k in range(HK):
                        ins = pe.transpose(psT[hf][:, k], pr[:, c % 4, (hf * HK + k) * P:(hf * HK + k + 1) * P], ident[:])
                    ins.then_inc(pT_ps, 1)

            def values(n, g, hf):
                par = g * QP // NQ % 2
                if hf == 0:
                    upto(pe, pT_lo, n, 2 * SW, 2 * QP * (g + 1))
                    upto(pe, v_ready, n, 2, g * QP // NQ + 1)
                    upto(pe, o_sb, n, GW, g)
                for k in range(hf * HK, (hf + 1) * HK):
                    for part in (pTh, pTl):
                        ins = pe.matmul(psO[:, 0:QP * P], vs[par][:, k], part[g % 2][:, k],
                                        start=(k == 0 and part is pTh), stop=(k == KT - 1 and part is pTl))
                if hf == 1:
                    ins.then_inc(o_ps, 1)

            project(0, 0, 0, 0)
            project(0, 0, 0, 1, psO)
            pe.wait_ge(t["w_head"][1], 16 * NA)
            for i in range(KT):
                if i >= 2:
                    pe.wait_ge(v_sb, i - 1)
                for k in range(KD):
                    ins = pe.matmul(psT[i % 2][:, 0:2].rearrange("p a (s d) -> p (a s) d", d=HD2),
                                    xnT[:, k, S + i * P:S + (i + 1) * P], whead[:, NA:2 * NA, k, 2 * HD2:3 * HD2],
                                    start=(k == 0), stop=(k == KD - 1))
                ins.then_inc(v_ps, 1)
            pe.wait_ge(v_sb, KT)

            def body(n):
                for c in range(SW):
                    i, q = divmod(c, NQ)
                    if q == 0:
                        upto(pe, qk_ready, n, 4, 2 * i + 2)
                    upto(pe, exp_done, n, SW, c - 1)
                    for hf in range(2):
                        for part in (kh, kl):
                            ins = pe.matmul(psS[c % 2][:, hf * CW:(hf + 1) * CW], qs[i][:, q * P:(q + 1) * P],
                                            part[i][:, hf * CW:(hf + 1) * CW], start=(part is kh), stop=(part is kl))
                    ins.then_inc(s_ps, 1)
                    if not (isinstance(n, int) and c < LAG):
                        transposes(n, c - LAG)
                    if not (isinstance(n, int) and c < 5):
                        values(n, (c - 5) // 2, (c - 5) % 2)
                    if q in (0, 4):
                        project(n, i + 1, (i + 1) % 2, q // 3)

            iterations(pe, body)
            last = NI // 2
            transposes(last, -3)
            values(last, -3, 1)
            transposes(last, -2)
            values(last, -2, 0)
            transposes(last, -1)
            values(last, -2, 1)
            values(last, -1, 0)
            values(last, -1, 1)
            pe.wait_ge(w_in, 16)
            pe.wait_ge(o_sb, NI * NQ // QP)
            pe.wait_ge(qk_hi, 2 * (NI + 1))
            pe.wait_ge(qk_lo, 2 * (NI + 1))
            for r in range(T // 2):
                if r >= 2:
                    pe.wait_ge(y_sb, r - 1)
                for j in range(2):
                    b, q = divmod(2 * r + j, NQ)
                    for s in range(NA // 2):
                        ins = pe.matmul((psP, psO)[r % 2][:, j * D:(j + 1) * D],
                                        oT[:, (b * NA // 2 + s) * S + q * P:(b * NA // 2 + s) * S + (q + 1) * P],
                                        wo[:, s, :], start=(s == 0), stop=(s == NA // 2 - 1))
                ins.then_inc(y_ps, 1)


def context_mlp(nc, top, t, io):
    with ExitStack() as ctx:
        def sb(name, shape, dt=F32):
            return ctx.enter_context(nc.sbuf_tensor(name, shape, dt))

        def sem(name):
            return top.enter_context(nc.semaphore(name))

        x_all, ident, table, slot = t["x_all"], t["ident"], t["table"], t["slot"]
        ctxT, ctxs, wr = t["ctxT"], t["ctxs"], t["wr"]
        stats = sb("c_stats", [P, 2, CH, 6])
        mv, rstd = t["mv"], t["rstd"]
        mhalf, mv4, rstd4 = sb("c_mhalf", [P, CH]), sb("c_mv4", [P, T, 2]), sb("c_rstd4", [P, T])
        flat = t["xg"][:].rearrange("p g r -> p (g r)")
        xn = flat[:, 0:2 * CH * D].rearrange("p (s j d) -> p s j d", s=2, j=CH)
        xnT = flat[:, 2 * CH * D:2 * (CH * D + KD * CW)].rearrange("p (s k q) -> p s k q", s=2, k=KD)
        sq, inner, th, g = (sb(f"c_{n}", [L, 2, CW]) for n in ("sq", "inner", "th", "g"))
        lg, e, first, oh, rank, base = (sb(f"c_{n}", [P, T, NE]) for n in ("lg", "e", "first", "oh", "rank", "base"))
        scan = sb("c_scan", [P, 2, T, NE])
        best, tot = sb("c_best", [P, T]), sb("c_tot", [P, T])
        low = sb("c_low", [P, T])
        before, ones = sb("c_before", [P, P]), sb("c_ones", [P, P])
        numi, num = sb("c_numi", [P, 32], I32), sb("c_num", [P, 32])
        steps = sb("c_steps", [P, T])
        tok = sb("c_tok", [P, T], I32)
        fits = sb("c_fits", [P, NE, T])
        tiles, ends = sb("c_tiles", [P, NE]), sb("c_ends", [P, 2, NE])
        slotf = sb("c_slotf", [P, T])
        tabf, done_e = sb("c_tabf", [1, TABLE]), sb("c_done_e", [1, TG, NE])
        blank, cleared = sb("c_blank", [P, ROW]), sem("c_cleared")
        w_high, scattered = sem("c_w_high"), sem("c_scattered")
        t["back"] = [sem(f"c_back{i}") for i in range(2)]
        psX = ctx.enter_context(nc.psum_tensor("c_psX", [P, KD, CW], F32))
        psH = [ctx.enter_context(nc.psum_tensor(f"c_psH{i}", [L, CW], F32)) for i in range(2)]
        psO = ctx.enter_context(nc.psum_tensor("c_psO", [P, CH, D], F32))
        psR = ctx.enter_context(nc.psum_tensor("c_psR", [P, T, NE], F32))
        psC = ctx.enter_context(nc.psum_tensor("c_psC", [P, 2, T, NE], F32))
        names = ("dve", "pool", "consts", "var", "rstd_s", "xn_s", "xT_ps", "xT_sb", "h_ps", "sq_s",
                 "inner_s", "th_s", "g_s", "o_ps", "x_done", "r_ps", "shift", "exp", "oh_s", "count_ps", "slot_s")
        (dve, pool_sem, consts, var_ready, rstd_ready, xn_ready, xT_ps, xT_sb, h_ps, sq_ready, inner_ready,
         th_ready, g_ready, o_ps, x_done, r_ps, shifted, exp_done, oh_ready, count_ps, slot_ready) = (
             sem("c_" + n) for n in names)
        def quarter(q):
            return slice(q * WE // NC, (q + 1) * WE // NC)

        block = ctx.enter_context(nc.Block())

        @block.sync
        def _(sp):
            fetch_expert(sp, t, io, 0)
            sp.wait_ge(t["w_in"], 48)
            fetch_expert(sp, t, io, 1)
            sp.wait_ge(cleared, 1)
            sp.dma_start(t["rows"].rearrange("(g p) r -> p g r", p=P),
                         blank[:].unsqueeze(1).to_broadcast([P, TG, ROW])).then_inc(t["rows_cleared"], 16)
            for x in range(2, 4):
                next_expert(sp, t, io, x)
            sp.wait_ge(scattered, 16 * T)
            rows = t["rows"].rearrange("(g p) r -> p g r", p=P)
            sp.dma_start(t["xg"][:, 0:2], rows[:, 0:2]).then_inc(t["back"][0], 16)
            sp.dma_start(t["xg"][:, 2:TG], rows[:, 2:TG]).then_inc(t["back"][1], 16)

        @block.gpsimd
        def _(pool):
            link = Link(pool, pool_sem)
            link(pool.memset(blank[:], 0.0))
            pool.memset(blank[:, D + 3:], float(2 * B * S)).then_inc(cleared, 1)
            pool.memset(mhalf[:], -0.5)
            pool.iota(numi[:], pattern=[[1, 32]], base=0, channel_multiplier=0)
            pool.iota(tok[:], pattern=[[P, T]], base=0, channel_multiplier=1)
            pool.memset(ones[:], 1.0)
            link(pool.memset(before[:], 1.0))
            pool.affine_select(out=before[:], in_=before[:], compare_op=ALU.is_gt, fill=0.0, base=0,
                               pattern=[[1, P]], channel_multiplier=-1).then_inc(consts, 1)
            pool.wait_ge(consts, 1)
            def power(n):
                pool.wait_ge(var_ready, n + 1)
                pool.tensor_tensor(rstd4[:, n * CH:(n + 1) * CH], rstd4[:, n * CH:(n + 1) * CH], mhalf[:],
                                   ALU.pow).then_inc(rstd_ready, 1)

            def low(i):
                x, q = divmod(i, NC)
                pool.wait_ge(w_high, i + 1)
                pool.tensor_tensor(t["wl"][:, x, quarter(q)], t["wst"][:, x, quarter(q)], t["wh"][:, x, quarter(q)],
                                   ALU.subtract).then_inc(t[("w_split", "w1_ready", "w_split", "w_ready")[q]],
                                                          2 if q == 1 else 1)

            power(0)
            low(0)
            power(1)
            low(1)
            power(2)
            power(3)
            for i in range(2, 2 * NC):
                low(i)
            pool.wait_ge(t["rows_cleared"], 16)
            pool.wait_ge(slot_ready, 1)
            for i in range(T):
                pool.indirect_dma_start(out=t["rows"], out_offset=bass.IndirectOffsetOnAxis(
                    ap=slot[:, i:i + 1].bitcast(U32), axis=0), in_=x_all[:, i, :], in_offset=None,
                    bounds_check=TG * P - 1, oob_is_err=False).then_inc(scattered, 16)

        @block.scalar
        def _(act):
            def copy_x(i):
                act.wait_ge(xT_ps, i + 1)
                if i >= 2:
                    act.wait_ge(*((h_ps, i - 1) if i - 2 < NC else (r_ps, i - 1 - NC)))
                act.copy(xnT[:, i % 2], psX[:]).then_inc(xT_sb, 1)

            def square(n):
                act.wait_ge(h_ps, n + 1)
                act.activation(sq[:, n % 2], psH[n % 2][:], ACT.Square).then_inc(sq_ready, 1)

            def tanh(n):
                act.wait_ge(inner_ready, n + 1)
                act.activation(th[:, n % 2], inner[:, n % 2], ACT.Tanh, bias=0.0,
                               scale=0.7978845608028654).then_inc(th_ready, 1)

            def high(i):
                x, q = divmod(i, NC)
                act.wait_ge(t["w_in"], 48 * (x + 1))
                act.copy(t["wh"][:, x, quarter(q)], t["wst"][:, x, quarter(q)]).then_inc(w_high, 1)

            copy_x(0)
            square(0)
            copy_x(1)
            tanh(0)
            for n in range(1, NC):
                square(n)
                copy_x(n + 1)
                tanh(n)
                if n >= 2:
                    high(n - 2)
            copy_x(NC + 1)
            high(2)
            copy_x(NC + 2)
            high(3)
            copy_x(NC + 3)
            high(4)
            high(5)
            act.wait_ge(shifted, 1)
            act.activation(e[:], e[:], ACT.Exp).then_inc(exp_done, 1)
            high(6)
            high(7)

        @block.vector
        def _(vec):
            link = Link(vec, dve)

            def normalise(i):
                n = i % NC
                m_, r_ = (mv, rstd) if i < NC else (mv4, rstd4)
                if i >= NC:
                    vec.wait_ge(rstd_ready, n + 1)
                if i >= 2:
                    vec.wait_ge(xT_ps, i - 1)
                for j in range(CH):
                    t_ = n * CH + j
                    ins = vec.tensor_scalar(xn[:, i % 2, j], x_all[:, t_, 0:D], m_[:, t_, 0:1], r_[:, t_:t_ + 1],
                                            ALU.subtract, ALU.mult)
                ins.then_inc(xn_ready, 1)

            def gelu(n):
                p = n % 2
                vec.wait_ge(sq_ready, n + 1)
                link(vec.tensor_scalar(inner[:, p], sq[:, p], 0.044715, 1.0, ALU.mult, ALU.add))
                vec.tensor_tensor(inner[:, p], psH[p][:], inner[:, p], ALU.mult).then_inc(inner_ready, 1)
                vec.wait_ge(th_ready, n + 1)
                vec.scalar_tensor_tensor(g[:, p], th[:, p], 1.0, psH[p][:], ALU.add, ALU.mult).then_inc(g_ready, 1)

            def update(n):
                vec.wait_ge(o_ps, n + 1)
                xc = x_all[:, n * CH:(n + 1) * CH, 0:D]
                vec.scalar_tensor_tensor(xc, psO[:], 0.5, xc, ALU.mult, ALU.add).then_inc(x_done, 1)
                vec.wait_ge(x_done, n + 1)
                link(layernorm_stats(vec, link, [x_all[:, n * CH + j, 0:D] for j in range(CH)], stats[:, n % 2],
                                     mv4[:, n * CH:(n + 1) * CH]))
                vec.tensor_scalar(rstd4[:, n * CH:(n + 1) * CH], mv4[:, n * CH:(n + 1) * CH, 1], EPS, None,
                                  ALU.add).then_inc(var_ready, 1)

            normalise(0)
            normalise(1)
            gelu(0)
            normalise(2)
            gelu(1)
            normalise(3)
            for n in range(NC):
                update(n)
                if n + 2 < NC:
                    gelu(n + 2)
                normalise(NC + n)
            vec.wait_ge(consts, 1)
            vec.tensor_copy(x_all[:, :, D], mv4[:, :, 0])
            vec.tensor_copy(x_all[:, :, D + 1], rstd4[:])
            vec.tensor_copy(x_all[:, :, D + 3], tok[:])
            link(vec.tensor_copy(num[:], numi[:]))
            vec.wait_ge(r_ps, NC)
            link(vec.tensor_copy(lg[:], psR[:]))
            full = [P, T, NE]
            link(vec.tensor_reduce(best[:], lg[:], AX.X, ALU.max))
            vec.tensor_tensor(e[:], lg[:], best[:].unsqueeze(2).to_broadcast(full), ALU.subtract).then_inc(shifted, 1)
            vec.wait_ge(exp_done, 1)
            link(vec.tensor_reduce(tot[:], e[:], AX.X, ALU.add))
            link(vec.reciprocal(tot[:], tot[:]))
            link(vec.tensor_tensor(e[:], e[:], tot[:].unsqueeze(2).to_broadcast(full), ALU.mult))
            link(vec.tensor_reduce(x_all[:, :, D + 2], e[:], AX.X, ALU.max))
            link(vec.tensor_tensor(first[:], e[:], x_all[:, :, D + 2:D + 3].to_broadcast(full), ALU.is_equal))
            link(vec.scalar_tensor_tensor(first[:], first[:], -float(NE), num[:, 0:NE].unsqueeze(1)
                                          .to_broadcast(full), ALU.mult, ALU.add))
            link(vec.tensor_reduce(low[:], first[:], AX.X, ALU.min))
            vec.tensor_tensor(oh[:], first[:], low[:].unsqueeze(2).to_broadcast(full), ALU.is_equal).then_inc(oh_ready, 1)
            vec.wait_ge(count_ps, 1)
            vec.tensor_copy(rank[:], psC[:, 0])
            link(vec.tensor_copy(scan[:, 0], psC[:, 1]))
            a = 0
            for d in (1, 2, 4, 8):
                vec.tensor_copy(scan[:, 1 - a, 0:d], scan[:, a, 0:d])
                link(vec.tensor_tensor(scan[:, 1 - a, d:T], scan[:, a, d:T], scan[:, a, 0:T - d], ALU.add))
                a = 1 - a
            vec.tensor_tensor(base[:], psC[:, 1], scan[:, a], ALU.subtract)
            link(vec.tensor_scalar(steps[:], num[:, 0:T], float(P), None, ALU.mult))
            link(vec.tensor_tensor(fits[:], scan[:, a, T - 1].unsqueeze(2).to_broadcast([P, NE, T]),
                                   steps[:].unsqueeze(1).to_broadcast([P, NE, T]), ALU.is_gt))
            link(vec.tensor_reduce(tiles[:], fits[:], AX.X, ALU.add))
            link(vec.tensor_scalar(tiles[:], tiles[:], 1.0, None, ALU.max))
            link(vec.tensor_copy(ends[:, 0], tiles[:]))
            a = 0
            for d in (1, 2, 4):
                vec.tensor_copy(ends[:, 1 - a, 0:d], ends[:, a, 0:d])
                link(vec.tensor_tensor(ends[:, 1 - a, d:NE], ends[:, a, d:NE], ends[:, a, 0:NE - d], ALU.add))
                a = 1 - a
            end = ends[:, a]
            link(vec.tensor_tensor(tiles[:], end, tiles[:], ALU.subtract))
            link(vec.tensor_scalar(tiles[:], tiles[:], float(P), None, ALU.mult))
            link(vec.tensor_tensor(rank[:], rank[:], base[:], ALU.subtract))
            link(vec.tensor_tensor(rank[:], rank[:], tiles[:].unsqueeze(1).to_broadcast(full), ALU.add))
            link(vec.tensor_tensor(rank[:], rank[:], oh[:], ALU.mult))
            link(vec.tensor_reduce(slotf[:], rank[:], AX.X, ALU.add))
            vec.tensor_copy(slot[:], slotf[:]).then_inc(slot_ready, 1)
            link(vec.tensor_tensor(done_e[:], end[0:1].unsqueeze(1).to_broadcast([1, TG, NE]),
                                   num[0:1, 0:TG].unsqueeze(2).to_broadcast([1, TG, NE]), ALU.is_le))
            link(vec.tensor_reduce(tabf[:, 0:TG], done_e[:], AX.X, ALU.add))
            link(vec.tensor_scalar(tabf[:, 0:TG], tabf[:, 0:TG], float(NE - 1), None, ALU.min))
            vec.tensor_scalar(tabf[:, TG:2 * TG], num[0:1, 0:TG], 1.0, end[0:1, NE - 1:NE], ALU.add, ALU.min)
            vec.tensor_copy(tabf[:, 2 * TG:LAST], end[0:1])
            link(vec.tensor_scalar(tabf[:, LAST:], end[0:1, NE - 1:NE], -1.0, None, ALU.add))
            vec.tensor_copy(table[:], tabf[:])

        @block.tensor
        def _(pe):
            pe.wait_ge(t["c_in"], 48)

            def transpose(i):
                pe.wait_ge(xn_ready, i + 1)
                if i >= 1:
                    pe.wait_ge(xT_sb, i)
                for k in range(KD):
                    for j in range(CH):
                        ins = pe.transpose(psX[:, k, j * P:(j + 1) * P], xn[:, i % 2, j, k * P:(k + 1) * P], ident[:])
                ins.then_inc(xT_ps, 1)

            def hidden(n):
                pe.wait_ge(xT_sb, n + 1)
                if n >= 2:
                    pe.wait_ge(g_ready, n - 1)
                for k in range(KD):
                    ins = pe.matmul(psH[n % 2][:], ctxT[:, n // (NC // B), k, :], xnT[:, n % 2, k],
                                    start=(k == 0), stop=(k == KD - 1))
                ins.then_inc(h_ps, 1)

            def output(n):
                pe.wait_ge(g_ready, n + 1)
                if n >= 1:
                    pe.wait_ge(x_done, n)
                for j in range(CH):
                    ins = pe.matmul(psO[:, j], g[:, n % 2, j * P:(j + 1) * P], ctxs[:, n // (NC // B)],
                                    start=True, stop=True)
                ins.then_inc(o_ps, 1)

            def route(n):
                pe.wait_ge(xT_sb, NC + n + 1)
                for j in range(CH):
                    for k in range(KD):
                        ins = pe.matmul(psR[:, n * CH + j], xnT[:, (NC + n) % 2, k, j * P:(j + 1) * P], wr[:, k],
                                        start=(k == 0), stop=(k == KD - 1))
                ins.then_inc(r_ps, 1)

            for n in range(2):
                transpose(n)
                hidden(n)
            for n in range(NC):
                if n + 1 == NC:
                    route(0)
                output(n)
                transpose(n + 2)
                if n + 2 < NC:
                    hidden(n + 2)
            for n in range(1, NC):
                if n + 1 < NC:
                    transpose(NC + n + 1)
                route(n)
            pe.wait_ge(consts, 1)
            pe.wait_ge(oh_ready, 1)
            pe.matmul(psC[:, 0], before[:], oh[:], start=True, stop=True)
            pe.matmul(psC[:, 1], ones[:], oh[:], start=True, stop=True).then_inc(count_ps, 1)


def experts(nc, top, t, io):
    with ExitStack() as ctx:
        def sb(name, shape, dt=F32):
            return ctx.enter_context(nc.sbuf_tensor(name, shape, dt))

        def sem(name):
            return top.enter_context(nc.semaphore(name))

        ident, table, xg, wst, wh, wl = (t[n] for n in ("ident", "table", "xg", "wst", "wh", "wl"))
        bias = t["bias"]
        xn = sb("e_xn", [P, D])
        xh, xl = sb("e_xh", [P, KD, P], F32R), sb("e_xl", [P, KD, P], F32R)
        h = sb("e_h", [P, 2, 512])
        hh, hl = sb("e_hh", [P, FB, P], F32R), sb("e_hl", [P, FB, P], F32R)
        y = sb("e_y", [P, D])
        tokid = sb("e_tokid", [P, MT], I32)
        psX = ctx.enter_context(nc.psum_tensor("e_psX", [P, KD, P], F32))
        psH = [ctx.enter_context(nc.psum_tensor(f"e_psH{i}", [P, 512], F32)) for i in range(2)]
        psT = [ctx.enter_context(nc.psum_tensor(f"e_psT{i}", [P, FB // 2, P], F32)) for i in range(2)]
        psY = ctx.enter_context(nc.psum_tensor("e_psY", [P, 512], F32))
        names = ("dve", "xn_s", "xT_ps", "xh_s", "xl_s", "h_ps", "h_sb", "hT_ps", "hh_s", "hl_s",
                 "y_ps", "y_s", "y_done", "tok_s", "out_s", "hgone")
        (dve, xn_ready, xT_ps, xh_ready, xl_ready, h_ps, h_sb, hT_ps, hh_ready, hl_ready, y_ps, y_sb,
         y_done, tok_ready, out_done, hgone) = (sem("e_" + n) for n in names)
        w_high = [sem(f"e_w_high{i}") for i in range(3)]
        w_in, w1_ready, w_ready, back = t["w_in"], t["w1_ready"], t["w_ready"], t["back"]
        block = ctx.enter_context(nc.Block())

        def upto(eng, s, n, per, c):
            if not isinstance(n, int):
                eng.wait_ge(s, n * per + c)
            elif per * n + c > 0:
                eng.wait_ge(s, per * n + c)

        def load(eng, at, top_value, least=0):
            return eng.value_load(table[0:1, bass.ds(at, 1)], min_val=least, max_val=top_value)

        def tiles(eng, body):
            body(0)
            with eng.Fori(1, load(eng, TILES, MT, NE)) as g:
                body(g)

        @block.sync
        def _(sp):
            for e in range(4, NE):
                next_expert(sp, t, io, e)
            written = sp.to_reg(load(sp, TILES, MT, NE) * 16)
            sp.wait_ge(t["rows_cleared"], 16)
            sp.wait_ge(out_done, written)

        @block.gpsimd
        def _(pool):
            most = pool.to_reg(B * S - 1)

            def split(g, e, par):
                landed = pool.to_reg(e * 48 + 96)
                pool.wait_ge(h_ps, 2 * g)
                pool.wait_ge(w_in, landed)
                for part in range(3):
                    raw, high, low = (
                        w[:, par, 0:KD * FF].rearrange("p (k h f) -> p k h f", k=KD, h=2)[:, :, part] if part < 2 else
                        w[:, par, KD * FF:WE].rearrange("p (k f) -> p k f", k=KD) for w in (wst, wh, wl))
                    if part == 2:
                        pool.wait_ge(y_sb, g)
                    pool.tensor_scalar(high, raw, 1.0, 0.0, ALU.mult, ALU.add).then_inc(w_high[part], 1)
                    pool.wait_ge(tok_ready, 1)
                    pool.wait_ge(w_high[part], e)
                    pool.tensor_tensor(low, raw, high, ALU.subtract).then_inc((w1_ready, w1_ready, w_ready)[part], 1)

            for g in range(1, MT + 1):
                if g < MT:
                    e = load(pool, g, NE - 1)
                    with pool.If(e < NE - 1):
                        before = load(pool, g - 1, NE - 1)
                        with pool.If(before < e):
                            e = load(pool, g, NE - 2, 1)
                            for par in range(2):
                                with pool.If(e % 2 == 1 - par):
                                    split(g, e, par)
                with pool.If(load(pool, TG + g - 1, MT) > g - 1):
                    pool.wait_ge(tok_ready, 1)
                    pool.wait_ge(y_done, g)
                    pool.indirect_dma_start(out=io["out"], out_offset=bass.IndirectOffsetOnAxis(
                        ap=tokid[:, g - 1:g].bitcast(U32), axis=0), in_=xg[:, g - 1, 0:D], in_offset=None,
                        bounds_check=most, oob_is_err=False).then_inc(out_done, 16)

        @block.scalar
        def _(act):
            def x_high(g):
                upto(act, xT_ps, g, 1, 1)
                upto(act, h_ps, g, 2, 0)
                act.copy(xh[:], psX[:]).then_inc(xh_ready, 1)

            x_high(0)

            def body(g):
                x_high(g + 1)
                for hf in range(2):
                    upto(act, hT_ps, g, 2, hf + 1)
                    upto(act, y_ps, g, 1, 0)
                    act.activation(hh[:, hf * FB // 2:(hf + 1) * FB // 2], psT[hf][:], ACT.Relu).then_inc(hh_ready, 1)

            tiles(act, body)

        @block.vector
        def _(vec):
            link = Link(vec, dve)

            def normalise(g):
                upto(vec, xT_ps, g, 1, 0)
                row = xg[:, bass.ds(g, 1), :].rearrange("p a r -> p (a r)")
                vec.tensor_scalar(xn[:], row[:, 0:D], row[:, D:D + 1], row[:, D + 1:D + 2], ALU.subtract,
                                  ALU.mult).then_inc(xn_ready, 1)

            def x_low(g):
                upto(vec, xh_ready, g, 1, 1)
                vec.tensor_tensor(xl[:], psX[:], xh[:], ALU.subtract).then_inc(xl_ready, 1)

            def finish(g):
                e = load(vec, g, NE - 1)
                upto(vec, y_ps, g, 1, 1)
                row = xg[:, bass.ds(g, 1), :].rearrange("p a r -> p (a r)")
                vec.tensor_tensor(y[:], psY[:, 0:D], bias[:, bass.ds((e % NB) * (FF + D) + FF, D)],
                                  ALU.add).then_inc(y_sb, 1)
                upto(vec, y_sb, g, 1, 1)
                vec.scalar_tensor_tensor(row[:, 0:D], y[:], row[:, D + 2:D + 3], row[:, 0:D], ALU.mult,
                                         ALU.add).then_inc(y_done, 1)

            vec.wait_ge(back[0], 16)
            normalise(0)
            x_low(0)
            normalise(1)

            def body(g):
                e = load(vec, g, NE - 1)
                for hf in range(2):
                    upto(vec, h_ps, g, 2, hf + 1)
                    upto(vec, hT_ps, g, 2, 0)
                    vec.tensor_tensor(h[:, hf], psH[hf][:], bias[:, bass.ds((e % NB) * (FF + D) + hf * 512, 512)],
                                      ALU.add).then_inc(h_sb, 1)
                x_low(g + 1)
                if isinstance(g, int):
                    vec.wait_ge(back[1], 16)
                    vec.tensor_copy(tokid[:], xg[:, 0:MT, D + 3]).then_inc(tok_ready, 1)
                else:
                    finish(g - 1)
                for hf in range(2):
                    upto(vec, hh_ready, g, 2, hf + 1)
                    part = slice(hf * FB // 2, (hf + 1) * FB // 2)
                    vec.scalar_tensor_tensor(hl[:, part], psT[hf][:], 0.0, hh[:, part], ALU.max,
                                             ALU.subtract).then_inc(hl_ready, 1)
                normalise(g + 2)

            tiles(vec, body)
            finish(load(vec, LAST, MT - 1, NE - 1))

        @block.tensor
        def _(pe):
            def transpose_x(g):
                upto(pe, xn_ready, g, 1, 1)
                upto(pe, xl_ready, g, 1, 0)
                for k in range(KD):
                    ins = pe.transpose(psX[:, k], xn[:, k * P:(k + 1) * P], ident[:])
                ins.then_inc(xT_ps, 1)

            def hidden(g, e):
                upto(pe, xl_ready, g, 1, 1)
                for hf in range(2):
                    pe.wait_ge(w1_ready, e * 2 + (hf + 1))
                    upto(pe, h_sb, g, 2, hf - 1)
                    for k in range(KD):
                        off = (e % 2) * WE + (k * FF + hf * 512)
                        for n, (x_, w_) in enumerate(((xh, wh), (xl, wh), (xh, wl))):
                            ins = pe.matmul(psH[hf][:], x_[:, k], w_[:].rearrange("p a w -> p (a w)")[:, bass.ds(off, 512)],
                                            start=(k == 0 and n == 0), stop=(k == KD - 1 and n == 2))
                    ins.then_inc(h_ps, 1)

            def transpose_h(g):
                for hf in range(2):
                    upto(pe, h_sb, g, 2, hf + 1)
                    upto(pe, hl_ready, g, 2, hf - 1)
                    for k in range(FB // 2):
                        ins = pe.transpose(psT[hf][:, k], h[:, hf, k * P:(k + 1) * P], ident[:])
                    ins.then_inc(hT_ps, 1)

            def output(g, e):
                pe.wait_ge(w_ready, e + 1)
                upto(pe, hl_ready, g, 2, 2)
                upto(pe, y_sb, g, 1, 0)
                for k in range(FB):
                    off = (e % 2) * WE + (KD * FF + k * D)
                    for n, (h_, w_) in enumerate(((hh, wh), (hl, wh), (hh, wl))):
                        ins = pe.matmul(psY[:, 0:D], h_[:, k], w_[:].rearrange("p a w -> p (a w)")[:, bass.ds(off, D)],
                                        start=(k == 0 and n == 0), stop=(k == FB - 1 and n == 2))
                ins.then_inc(y_ps, 1)

            transpose_x(0)

            def body(g):
                e = 0 if isinstance(g, int) else load(pe, g, NE - 1)
                before = 0 if isinstance(g, int) else load(pe, g - 1, NE - 1)
                hidden(g, e)
                transpose_x(g + 1)
                if not isinstance(g, int):
                    output(g - 1, before)
                transpose_h(g)

            tiles(pe, body)
            output(load(pe, LAST, MT - 1, NE - 1), NE - 1)


def next_expert(sp, t, io, e):
    sp.wait_ge(t["w_in"], 48 * e)
    sp.wait_ge(t["w_ready"], e - 1)
    fetch_expert(sp, t, io, e)


def fetch_expert(sp, t, io, e):
    sp.dma_start(t["wst"][:, e % 2, 0:KD * FF], io["m_w1"][e]).then_inc(t["w_in"], 16)
    sp.dma_start(t["wst"][:, e % 2, KD * FF:WE], io["m_w2"][e]).then_inc(t["w_in"], 16)
    sp.dma_start(t["bias"][:, e % NB * (FF + D):(e % NB + 1) * (FF + D)], io["m_b"][e]).then_inc(t["w_in"], 16)


def program(nc, io):
    with ExitStack() as top:
        def sb(name, shape, dt=F32):
            return top.enter_context(nc.sbuf_tensor(name, shape, dt))

        t = {"x_all": sb("x_all", [P, T, ROW]), "ident": sb("ident", [P, P])}
        t["ctxT"], t["ctxs"], t["wr"] = sb("ctxT", [P, B, KD, L]), sb("ctx", [L, B, D]), sb("wr", [P, KD, NE])
        t["mv"], t["rstd"] = sb("mv", [P, T, 2]), sb("rstd", [P, T])
        t["table"], t["slot"] = sb("table", [1, TABLE], I32), sb("slot", [P, T], I32)
        for name in ("c_in", "w_in", "w1_ready", "w_ready", "w_split", "rows_cleared"):
            t[name] = top.enter_context(nc.semaphore(name))
        t["rows"] = nc.dram_tensor("rows", (TG * P, ROW), F32, kind="Internal").ap()
        cross_attention(nc, top, t, io)
        with ExitStack() as attention:
            for name, shape, dt in (("xnT", [P, KD, B * S], F32), ("v_all", [P, B * NA + 1, S // P, HD2], F32),
                                    ("whead", [P, B * NA + 2, KD, 3 * HD2], F32),
                                    ("bqk", [P, B * NA + 1], F32),
                                    ("bv", [P, B * NA + 1], F32)):
                t[name] = attention.enter_context(nc.sbuf_tensor(name, shape, dt))
            gate_and_project(nc, top, t, io)
            gated_attention(nc, top, t, io)
        for name, shape, dt in (("wst", [P, 2, WE], F32), ("wh", [P, 2, WE], F32R), ("wl", [P, 2, WE], F32R),
                                ("xg", [P, TG, ROW], F32), ("bias", [P, NB * (FF + D)], F32)):
            t[name] = sb(name, shape, dt)
        context_mlp(nc, top, t, io)
        experts(nc, top, t, io)


def kernel(**inputs):
    import numpy as np
    import concourse.bacc as bacc
    from concourse.bass_utils import run_bass_kernel_spmd

    def blocks(w):
        return w.reshape(-1, P, w.shape[-1]).transpose(1, 0, 2)

    def twice(v):
        return np.concatenate([v, v], -1)

    def rows(v, n=P):
        return np.broadcast_to(v, (n,) + v.shape)

    a = {k: np.asarray(v) for k, v in inputs.items()}
    ctx_ = a["ctx_1024"]
    arrays = {
        "x": a["x"].reshape(T, P, D).transpose(1, 0, 2),
        "ctxT": ctx_.reshape(B, L, KD, P).transpose(3, 0, 2, 1),
        "mask": rows(a["mask_Bx1x1xS2_ik0"].reshape(B, L)),
        "xa_wq": blocks(a["L0_xattn_Wq"].T),
        "xa_wk": twice(blocks(a["L0_xattn_Wk"].T).reshape(P, KD, KD, 2, P // 2)),
        "xa_wv": blocks(a["L0_xattn_Wv"].T), "xa_wo": blocks(a["L0_xattn_Wo"].T),
        "xa_bq": a["L0_xattn_bq"].reshape(KD, P).T, "xa_bk": twice(a["L0_xattn_bk"].reshape(KD, 2, P // 2)).transpose(2, 0, 1),
        "xa_bv": rows(a["L0_xattn_bv"]), "xa_bo": rows(a["L0_xattn_bo"]),
        "ctx": ctx_.transpose(1, 0, 2),
        "m_wr": blocks(a["L1_ffn_w_router"]),
        "m_w1": a["L1_ffn_w1"].reshape(NE, KD, P, FF).transpose(0, 2, 1, 3).reshape(NE, P, KD * FF),
        "m_w2": a["L1_ffn_w2"].reshape(NE, FB, P, D).transpose(0, 2, 1, 3).reshape(NE, P, FB * D),
        "m_b": np.broadcast_to(np.concatenate([a["L1_ffn_b1"], a["L1_ffn_b2"]], -1)[:, None], (NE, P, FF + D)),
        "f_w": np.concatenate([blocks(a[f"L0_ffn_W{n}"]).reshape(P, KD, H2, HD2) for n in "qkv"], -1),
        "f_wr": blocks(a["L0_ffn_Wr"]), "f_br": a["L0_ffn_br"][None],
        "f_bqk": np.concatenate([a[f"L0_ffn_b{n}"].reshape(H2, HD2).T for n in "qk"], 0),
        "f_bv": a["L0_ffn_bv"].reshape(H2, HD2).T,
        "f_wo": blocks(a["L0_ffn_Wo"]), "f_bo": rows(a["L0_ffn_bo"]),
    }
    nc = bacc.Bacc("TRN2", target_bir_lowering=False, num_devices=1)
    io = {}
    for name, v in arrays.items():
        arrays[name] = v = np.ascontiguousarray(v)
        io[name] = nc.dram_tensor(f"in_{name}", v.shape, mybir.dt.from_np(v.dtype), kind="ExternalInput").ap()
    io["out"] = nc.dram_tensor("out", (B * S, D), F32, kind="ExternalOutput").ap()
    program(nc, io)
    r = run_bass_kernel_spmd(nc, [{f"in_{k}": v for k, v in arrays.items()}], core_ids=[0])
    return r.results[0]["out"].reshape(B, S, D)
```
